# Optimizing a Trainium2 kernel written in Bass

```python
import numpy as np
import jax
import jax.numpy as jnp

def _softmax(x, axis=-1):
    return jax.nn.softmax(x, axis=axis)

def _gelu(x):
    return jax.nn.gelu(x, approximate=True)

def _silu(x):
    return jax.nn.silu(x)

def _sigmoid(x):
    return jax.nn.sigmoid(x)

def _layernorm(x, axis=-1, eps=1e-05):
    m = jnp.mean(x, axis=axis, keepdims=True)
    v = jnp.var(x, axis=axis, keepdims=True)
    return (x - m) / jnp.sqrt(v + eps)

def _scatter_add(tgt, idx, src, axis=0):
    return tgt.at[idx].add(src)

def _segment_sum(src, seg, n):
    return jax.ops.segment_sum(src, seg, n)
kernel_name = 'mk_flamingo_gated_d2_seqx_r8_fa1d31'

def setup_inputs(seed: int=0):
    np.random.seed(seed)
    _w = jnp.asarray

    def _rec_inputs():
        import jax
        import jax.numpy as jnp
        _rk = jax.random.key(seed)
        x = 7.22e-05 + 1 * jax.random.normal(jax.random.fold_in(_rk, 1), (4, 512, 128), jnp.float32)
        _lenS = 512 - jax.random.randint(jax.random.fold_in(_rk, 7), (4,), 0, max(1, 512 // 4) + 1, jnp.int32)
        _lenS2 = 77 - jax.random.randint(jax.random.fold_in(_rk, 8), (4,), 0, max(1, 77 // 4) + 1, jnp.int32)
        _ctx_1024P = jax.random.normal(jax.random.fold_in(_rk, 11), (4, 16, 128), jnp.float32)
        _ctx_1024c = jax.random.dirichlet(jax.random.fold_in(_rk, 511), 0.3 * jnp.ones((16,), jnp.float32), (4, 77))
        _ctx_1024t = jnp.einsum('bsk,bkd->bsd', _ctx_1024c, _ctx_1024P)
        _ctx_1024t = _ctx_1024t * jax.lax.rsqrt(jnp.mean(jnp.square(_ctx_1024t)) + 1e-12) * 0.953939
        ctx_1024 = 4.13588e-05 + 0.999923 * (_ctx_1024t + 0.3 * jax.random.normal(jax.random.fold_in(_rk, 611), (4, 77, 128), jnp.float32))
        _validS = jnp.arange(512)[None, :] < _lenS[:, None]
        _validS2 = jnp.arange(77)[None, :] < _lenS2[:, None]
        _causal = jnp.tril(jnp.ones((512, 512), dtype=bool))
        mask_B_ik0 = jnp.where(jnp.ones((4,), dtype=bool), 69, 1564).astype(jnp.int32)
        _g = jax.random.normal(jax.random.fold_in(_rk, 9001), (2, 2), jnp.float32)
        _g = jnp.sign(_g) * jnp.maximum(jnp.abs(_g), 1.0) + (_g == 0) * 1.0
        g_xattn = _g[0]
        g_ffn = _g[1]
        return (x, ctx_1024, mask_B_ik0, g_xattn, g_ffn)
    x, ctx_1024, mask_B_ik0, g_xattn, g_ffn = _rec_inputs()

    def _L0_xattn_setup():
        import jax, jax.numpy as jnp
        import numpy as np
        DIM = 128
        CTX_DIM = 128
        HEADS = 8
        DIM_HEAD = 64
        INNER = HEADS * DIM_HEAD
        EPS = 1e-05

        def _layer_norm(x, gamma, beta):
            mu = jnp.mean(x, axis=-1, keepdims=True)
            var = jnp.mean(jnp.square(x - mu), axis=-1, keepdims=True)
            return (x - mu) * jax.lax.rsqrt(var + EPS) * gamma + beta
        key = jax.random.key(seed)
        ks = jax.random.split(key, 8)
        b, n, m = (4, 256, 256)
        x = jax.random.normal(ks[0], (b, n, DIM), dtype=jnp.float32)
        context = jax.random.normal(ks[1], (b, m, CTX_DIM), dtype=jnp.float32)
        Wq = jax.random.normal(ks[2], (DIM, INNER), dtype=jnp.float32) / np.sqrt(DIM)
        Wkv = jax.random.normal(ks[3], (CTX_DIM, 2 * INNER), dtype=jnp.float32) / np.sqrt(CTX_DIM)
        Wout = jax.random.normal(ks[4], (INNER, DIM), dtype=jnp.float32) / np.sqrt(INNER)
        bout = jnp.zeros((DIM,), dtype=jnp.float32)
        g1 = jnp.ones((DIM,), dtype=jnp.float32)
        b1 = jnp.zeros((DIM,), dtype=jnp.float32)
        g2 = jnp.ones((CTX_DIM,), dtype=jnp.float32)
        b2 = jnp.zeros((CTX_DIM,), dtype=jnp.float32)
        return {'x': x, 'context': context, 'g1': g1, 'b1': b1, 'g2': g2, 'b2': b2, 'Wq': Wq, 'Wkv': Wkv, 'Wout': Wout, 'bout': bout}
    _L0_xattn_all = _L0_xattn_setup()
    _L0_xattn_in = {k: v for k, v in _L0_xattn_all.items() if k in ('g1', 'b1', 'g2', 'b2', 'Wq', 'Wkv', 'Wout', 'bout')}
    del _L0_xattn_all

    def _L0_ffn_setup():
        import jax, jax.numpy as jnp
        import numpy as np
        B, S, DIM, FFN, E = (4, 256, 128, 512, 8)
        key = jax.random.key(seed)
        k0, k1, k2, k3 = jax.random.split(key, 4)
        scale = 0.02
        return {'hidden_states': jax.random.normal(k0, (B, S, DIM), jnp.float32), 'router_w': jax.random.normal(k1, (DIM, E), jnp.float32) * scale, 'router_b': jnp.zeros((E,), jnp.float32), 'w1': jax.random.normal(k2, (E, DIM, 2 * FFN), jnp.float32) * scale, 'w2': jax.random.normal(k3, (E, FFN, DIM), jnp.float32) * scale}
    _L0_ffn_all = _L0_ffn_setup()
    _L0_ffn_in = {k: v for k, v in _L0_ffn_all.items() if k in ('router_w', 'router_b', 'w1', 'w2')}
    del _L0_ffn_all

    def _L1_xattn_setup():
        import jax, jax.numpy as jnp
        import numpy as np
        import math
        B, S, D, H = (2, 256, 128, 16)
        HD = D // H
        key = jax.random.key(seed)
        ks = jax.random.split(key, 8)
        scale = 0.02
        return {'queries': jax.random.normal(ks[0], (B, S, D), dtype=jnp.float32), 'keys': jax.random.normal(ks[1], (B, S, D), dtype=jnp.float32), 'values': jax.random.normal(ks[2], (B, S, D), dtype=jnp.float32), 'valid_lens': jax.random.randint(ks[3], (B,), 1, S + 1, dtype=jnp.int32), 'Wq': jax.random.normal(ks[4], (H, D, HD), dtype=jnp.float32) * scale, 'Wk': jax.random.normal(ks[5], (H, D, HD), dtype=jnp.float32) * scale, 'Wv': jax.random.normal(ks[6], (H, D, HD), dtype=jnp.float32) * scale, 'Wo': jax.random.normal(ks[7], (H * HD, D), dtype=jnp.float32) * scale}
    _L1_xattn_all = _L1_xattn_setup()
    _L1_xattn_in = {k: v for k, v in _L1_xattn_all.items() if k in ('Wq', 'Wk', 'Wv', 'Wo')}
    del _L1_xattn_all

    def _L1_ffn_setup():
        import jax, jax.numpy as jnp
        import numpy as np
        from jax import lax
        D = 128
        H = 512
        E = 8
        TOPK = 2
        key = jax.random.key(seed)
        ks = jax.random.split(key, 7)
        s = 0.02
        return {'x': jax.random.normal(ks[0], (2, 256, D), dtype=jnp.float32), 'W1': jax.random.normal(ks[1], (E, D, H), dtype=jnp.float32) * s, 'b1': jnp.zeros((E, H), dtype=jnp.float32), 'W2': jax.random.normal(ks[2], (E, H, D), dtype=jnp.float32) * s, 'b2': jnp.zeros((E, D), dtype=jnp.float32), 'Wr': jax.random.normal(ks[3], (D, E), dtype=jnp.float32) * s, 'br': jnp.zeros((E,), dtype=jnp.float32)}
    _L1_ffn_all = _L1_ffn_setup()
    _L1_ffn_in = {k: v for k, v in _L1_ffn_all.items() if k in ('W1', 'b1', 'W2', 'b2', 'Wr', 'br')}
    del _L1_ffn_all
    return {'x': x, 'ctx_1024': ctx_1024, 'mask_B_ik0': mask_B_ik0, 'g_xattn': g_xattn, 'g_ffn': g_ffn, 'L0_xattn_g1': _L0_xattn_in['g1'], 'L0_xattn_b1': _L0_xattn_in['b1'], 'L0_xattn_g2': _L0_xattn_in['g2'], 'L0_xattn_b2': _L0_xattn_in['b2'], 'L0_xattn_Wq': _L0_xattn_in['Wq'], 'L0_xattn_Wkv': _L0_xattn_in['Wkv'], 'L0_xattn_Wout': _L0_xattn_in['Wout'], 'L0_xattn_bout': _L0_xattn_in['bout'], 'L0_ffn_router_w': _L0_ffn_in['router_w'], 'L0_ffn_router_b': _L0_ffn_in['router_b'], 'L0_ffn_w1': _L0_ffn_in['w1'], 'L0_ffn_w2': _L0_ffn_in['w2'], 'L1_xattn_Wq': _L1_xattn_in['Wq'], 'L1_xattn_Wk': _L1_xattn_in['Wk'], 'L1_xattn_Wv': _L1_xattn_in['Wv'], 'L1_xattn_Wo': _L1_xattn_in['Wo'], 'L1_ffn_W1': _L1_ffn_in['W1'], 'L1_ffn_b1': _L1_ffn_in['b1'], 'L1_ffn_W2': _L1_ffn_in['W2'], 'L1_ffn_b2': _L1_ffn_in['b2'], 'L1_ffn_Wr': _L1_ffn_in['Wr'], 'L1_ffn_br': _L1_ffn_in['br']}

def reference(x, ctx_1024, mask_B_ik0, g_xattn, g_ffn, L0_xattn_g1, L0_xattn_b1, L0_xattn_g2, L0_xattn_b2, L0_xattn_Wq, L0_xattn_Wkv, L0_xattn_Wout, L0_xattn_bout, L0_ffn_router_w, L0_ffn_router_b, L0_ffn_w1, L0_ffn_w2, L1_xattn_Wq, L1_xattn_Wk, L1_xattn_Wv, L1_xattn_Wo, L1_ffn_W1, L1_ffn_b1, L1_ffn_W2, L1_ffn_b2, L1_ffn_Wr, L1_ffn_br):
    import jax
    import jax.numpy as jnp

    def _L0_xattn_ref(x, context, g1, b1, g2, b2, Wq, Wkv, Wout, bout):
        import jax, jax.numpy as jnp
        import numpy as np
        DIM = 128
        CTX_DIM = 128
        HEADS = 8
        DIM_HEAD = 64
        INNER = HEADS * DIM_HEAD
        EPS = 1e-05

        def _layer_norm(x, gamma, beta):
            mu = jnp.mean(x, axis=-1, keepdims=True)
            var = jnp.mean(jnp.square(x - mu), axis=-1, keepdims=True)
            return (x - mu) * jax.lax.rsqrt(var + EPS) * gamma + beta
        b, n, _ = x.shape
        m = context.shape[1]
        scale = DIM_HEAD ** (-0.5)
        xn = _layer_norm(x, g1, b1)
        cn = _layer_norm(context, g2, b2)
        q = xn @ Wq
        kv = cn @ Wkv
        k, v = jnp.split(kv, 2, axis=-1)
        q = q.reshape(b, n, HEADS, DIM_HEAD).transpose(0, 2, 1, 3)
        k = k.reshape(b, m, HEADS, DIM_HEAD).transpose(0, 2, 1, 3)
        v = v.reshape(b, m, HEADS, DIM_HEAD).transpose(0, 2, 1, 3)
        sim = jnp.einsum('bhid,bhjd->bhij', q, k) * scale
        attn = jax.nn.softmax(sim, axis=-1)
        out = jnp.einsum('bhij,bhjd->bhid', attn, v)
        out = out.transpose(0, 2, 1, 3).reshape(b, n, INNER)
        return out @ Wout + bout

    def _L0_ffn_ref(hidden_states, router_w, router_b, w1, w2):
        import jax, jax.numpy as jnp
        import numpy as np
        B, S, DIM, FFN, E = (4, 256, 128, 512, 8)
        b, s, d = hidden_states.shape
        x = hidden_states.reshape(-1, d)
        logits = x @ router_w + router_b
        route = jax.nn.softmax(logits, axis=1)
        max_prob = jnp.max(route, axis=1, keepdims=True)
        max_ind = jnp.argmax(route, axis=1)
        out = jnp.zeros_like(x)
        num_experts = w1.shape[0]
        for e in range(num_experts):
            h = x @ w1[e]
            a, g = jnp.split(h, 2, axis=1)
            y = jax.nn.silu(a) * g @ w2[e]
            out = jnp.where((max_ind == e)[:, None], y, out)
        out = out * max_prob
        return out.reshape(b, s, d)

    def _L1_xattn_ref(queries, keys, values, valid_lens, Wq, Wk, Wv, Wo):
        import jax, jax.numpy as jnp
        import numpy as np
        import math
        B, S, D, H = (2, 256, 128, 16)
        HD = D // H
        q = jnp.einsum('bsd,hde->bhse', queries, Wq)
        k = jnp.einsum('bsd,hde->bhse', keys, Wk)
        v = jnp.einsum('bsd,hde->bhse', values, Wv)
        scores = jnp.einsum('bhqe,bhke->bhqk', q, k) / math.sqrt(HD)
        kv_len = keys.shape[1]
        pos = jnp.arange(1, kv_len + 1, dtype=jnp.int32)
        mask = pos[None, :] > valid_lens[:, None]
        scores = jnp.where(mask[:, None, None, :], jnp.float32(-1000000.0), scores)
        attn = jax.nn.softmax(scores, axis=-1)
        out = jnp.einsum('bhqk,bhke->bhqe', attn, v)
        out = out.transpose(0, 2, 1, 3).reshape(queries.shape[0], queries.shape[1], H * HD)
        return out @ Wo

    def _L1_ffn_ref(x, W1, b1, W2, b2, Wr, br):
        import jax, jax.numpy as jnp
        import numpy as np
        from jax import lax
        D = 128
        H = 512
        E = 8
        TOPK = 2
        B, S, _ = x.shape
        xf = x.reshape(-1, D)
        logits = xf @ Wr + br
        topv, _ = lax.top_k(logits, TOPK)
        thresh = topv[:, TOPK - 1:TOPK]
        masked = jnp.where(logits >= thresh, logits, -jnp.inf)
        weights = jax.nn.softmax(masked, axis=-1)
        h = jax.nn.gelu(jnp.einsum('td,edh->eth', xf, W1) + b1[:, None, :], approximate=False)
        expert_out = jnp.einsum('eth,ehd->etd', h, W2) + b2[:, None, :]
        out = jnp.einsum('etd,te->td', expert_out, weights)
        return out.reshape(B, S, D)
    x = x + jnp.tanh(g_xattn[0]) * _L0_xattn_ref(_layernorm(x, axis=-1), ctx_1024, L0_xattn_g1, L0_xattn_b1, L0_xattn_g2, L0_xattn_b2, L0_xattn_Wq, L0_xattn_Wkv, L0_xattn_Wout, L0_xattn_bout)
    x = x + jnp.tanh(g_ffn[0]) * _L0_ffn_ref(_layernorm(x, axis=-1), L0_ffn_router_w, L0_ffn_router_b, L0_ffn_w1, L0_ffn_w2)
    x = x + jnp.tanh(g_xattn[1]) * _L1_xattn_ref(_layernorm(x, axis=-1), ctx_1024, ctx_1024, mask_B_ik0, L1_xattn_Wq, L1_xattn_Wk, L1_xattn_Wv, L1_xattn_Wo)
    x = x + jnp.tanh(g_ffn[1]) * _L1_ffn_ref(_layernorm(x, axis=-1), L1_ffn_W1, L1_ffn_b1, L1_ffn_W2, L1_ffn_b2, L1_ffn_Wr, L1_ffn_br)
    return x

_drawn_inputs = setup_inputs


def setup_inputs(seed=0):
    import zlib

    import numpy as np

    out = dict(_drawn_inputs(seed))
    spreads = {'g_ffn': (-1.0, 0.6),
     'L0_xattn_g1': (1.0, 0.2),
     'L0_xattn_b1': (0.0, 0.512),
     'L0_xattn_g2': (1.0, 0.2),
     'L0_xattn_b2': (0.0, 0.1),
     'L0_xattn_bout': (0.0, 0.1),
     'L0_ffn_router_b': (0.0, 0.8),
     'L1_ffn_b1': (0.0, 0.608),
     'L1_ffn_b2': (0.0, 0.445),
     'L1_ffn_br': (0.0, 0.372)}
    factors = {'L0_ffn_router_w': 8.0,
     'L0_ffn_w1': 8.0,
     'L0_ffn_w2': 8.0,
     'L1_xattn_Wq': 53.018,
     'L1_xattn_Wk': 52.183,
     'L1_xattn_Wv': 5.257,
     'L1_xattn_Wo': 5.201,
     'L1_ffn_W1': 5.093}
    for name, (base, spread) in spreads.items():
        noise = np.random.default_rng([zlib.crc32(name.encode()), seed]).standard_normal(out[name].shape)
        drawn = base * np.exp(spread * noise) if base else spread * noise
        out[name] = jnp.asarray(drawn.astype(out[name].dtype))
    for name, factor in factors.items():
        out[name] = (out[name] * factor).astype(out[name].dtype)
    return out
```

```python
from collections import namedtuple
from contextlib import ExitStack

import concourse.bass as bass
from concourse import mybir

P = 128
B, S, D = 4, 512, 128
NKEY = 77
CTX = B * NKEY
NT = B * S // P
TPB = NT // B
E = 8
H0, HD0 = 8, 64
H1, HD1 = 16, 8
FFN = 512
EPS = 1e-5
NEG = -1.0e6
BIG = 1.0e30

ALU = mybir.AluOpType
ACT = mybir.ActivationFunctionType
AX = mybir.AxisListType
F32 = mybir.dt.float32
BF16 = mybir.dt.bfloat16
I32 = mybir.dt.int32
U32 = mybir.dt.uint32
ds = bass.ds

MAXSLOTS = 2 * NT + E - 1
CONST_COLS = {}
_at = 0
for _name, _n in (("ident", P), ("ones", P), ("before", P), ("earlier_tile", P), ("same_expert", E),
                  ("lower_expert", P), ("upto_expert", E), ("row_number", P), ("slot_number", MAXSLOTS),
                  ("partition", 1), ("tile_number", 2 * NT), ("expert_rank", E), ("head_rows", H1),
                  ("slot_edges", NT), ("key_number", NKEY), ("pad_rows", MAXSLOTS), ("eps", 1), ("eps2", 1)):
    CONST_COLS[_name] = (_at, _n)
    _at += _n
NCONST = _at


def live(step, lag, n):
    return not isinstance(step, int) or 0 <= step - lag < n


def past(i, n):
    return not isinstance(i, int) or i >= n


def pipeline(eng, n, depth, body):
    head = min((depth + 3) // 2 * 2, n // 2 * 2)
    end = n // 2 * 2
    for step in range(head):
        body(step, step % 2)
    if end > head:
        with eng.Fori(head // 2, end // 2) as pair:
            body(pair * 2, 0)
            body(pair * 2 + 1, 1)
    for step in range(end, n + depth):
        body(step, step % 2)


def key_chunks(heads):
    cols = heads * NKEY
    chunks = [(a, min(P, cols - a)) for a in range(0, cols, P)]
    return chunks, [list(range(a, min(a + 4, len(chunks)))) for a in range(0, len(chunks), 4)]


def full_and_rest(group, chunks):
    full = [c for c in group if chunks[c][1] == P]
    rest = [c for c in group if chunks[c][1] < P]
    return [r for r in (full, rest) if r]


Layer = namedtuple("Layer", "n heads scale parts choices cols chunks groups slots")


def layer_plan(n, heads, scale, parts, choices):
    return Layer(n, heads, scale, parts, choices, heads * NKEY, *key_chunks(heads), choices * NT + E - 1)


def gated_stack(nc, x, ctx_rows, ctx_cols, valid_len, g_xattn, g_ffn, ln_gb, out_bias, wq0, wkv0, wout0,
                rw0, rb0, w1_0, w2_0, wqkvo1, w1_1, b1_1, w2_1, b2_1, rw1, rb1, const, out):
    with ExitStack() as stack:
        def sb(name, shape, dt=F32):
            return stack.enter_context(nc.sbuf_tensor(name, shape, dt))

        def sem(name):
            return stack.enter_context(nc.semaphore(name))

        def sems(tag, names):
            return namedtuple("Sems", names)(*[sem(f"{n}_{tag}") for n in names.split()])

        ps = stack.enter_context(nc.psum_tensor("ps", [P, 8, 512], F32))
        k_sb = sb("k_sb", [P, NCONST])
        kb_sb = sb("kb_sb", [P, NCONST], BF16)
        res = sb("res", [P, NT, D])
        base = sb("base", [P, NT, D])
        gate_in = sb("gate_in", [P, 4])
        gate_t = sb("gate_t", [P, 4])
        gb = sb("gb", [P, 4])
        bout_b = sb("bout_b", [P, D])
        bout_g = sb("bout_g", [P, D])
        vlen_i = sb("vlen_i", [P, B], I32)
        vlen = sb("vlen", [P, B])
        keep = sb("keep", [P, B, NKEY])
        drop = sb("drop", [P, B, NKEY], BF16)
        ctx_sb = sb("ctx_sb", [P, 3, D])
        ctx_n = sb("ctx_n", [P, 3, D])
        ctx_st = sb("ctx_st", [P, 3, 6])
        ctx_mv = sb("ctx_mv", [P, 3, 2])
        ctx_rs = sb("ctx_rs", [P, 3, 2])
        cn_t = sb("cn_t", [P, CTX])
        c_t = sb("c_t", [P, CTX])
        wq0_sb = sb("wq0_sb", [P, 4, D])
        wkv0_sb = sb("wkv0_sb", [P, 2 * H0 * HD0])
        wout0_sb = sb("wout0_sb", [P, 4, D])
        wqkvo1_sb = sb("wqkvo1_sb", [P, 4, D])
        kv1_t = sb("kv1_t", [P, 2, CTX])
        score_mat = [sb("score_mat0", [P, B, H0 * NKEY]), sb("score_mat1", [P, B, H1 * NKEY])]
        value_mat = [sb("value_mat0", [P, B * 5, D]), sb("value_mat1", [P, B * 10, D])]
        shared = sb("shared", [P, E * 2 * FFN])
        vw_t = shared[:, 0:B * H1 * NKEY]
        kv_t = shared[:, 4928:4928 + 8 * CTX].rearrange("p (c n) -> p c n", c=8)
        head_kv = shared[:, 7392:7392 + 2 * CTX].rearrange("p (c n) -> p c n", c=2)
        w_up = [shared[:, :].rearrange("p (e f) -> p e f", e=E),
                shared[:, 0:E * FFN].rearrange("p (e f) -> p e f", e=E)]
        b_up = shared[:, E * FFN:2 * E * FFN].rearrange("p (e f) -> p e f", e=E)
        y_second = shared[:, 0:NT * D].rearrange("p (t d) -> p t d", t=NT)
        w_down = sb("w_down", [P, E, 4, D])
        b_down = sb("b_down", [P, E, D])
        rw = sb("rw", [P, 2, E])
        rb = sb("rb", [P, 2, E])
        xn = sb("xn", [P, 2, D])
        xn_t = sb("xn_t", [P, 2, P])
        work = sb("work", [P, 3 * H1 * NKEY])
        sub = work[:, 0:H1 * NKEY]
        expd = [work[:, (1 + k) * H1 * NKEY:(2 + k) * H1 * NKEY] for k in range(2)]
        act_a = work[:, 0:2 * FFN].rearrange("p (k f) -> p k f", k=2)
        hid = work[:, 2 * FFN:4 * FFN].rearrange("p (k f) -> p k f", k=2)
        hid_t = work[:, 4 * FFN:6 * FFN].rearrange("p (k c n) -> p k c n", k=2, c=4)
        probs_t = sb("probs_t", [P, 10, P])
        mx = sb("mx", [P, H1])
        rec = sb("rec", [P, 2, 2, H1])
        stats = sb("stats", [P, 4, 6])
        mv = sb("mv", [P, 8, 2])
        rs = sb("rs", [P, 8, 2])
        xo = sb("xo", [P, 2, D])
        xo_t = sb("xo_t", [P, 2, P])
        logits = sb("logits", [P, NT, E])
        pick = sb("pick", [P, 2, NT, E])
        rt = sb("rt", [P, 3, NT, E])
        rcol = sb("rcol", [P, 8, NT])
        pick_b = sb("pick_b", [P, NT, E], BF16)
        totals = sb("totals", [P, P], BF16)
        nblk = sb("nblk", [P, NT + 1])
        nblk_b = sb("nblk_b", [P, P], BF16)
        pos_f = sb("pos_f", [P, 3, 2 * NT])
        pos_i = sb("pos_i", [P, 3, 2 * NT], I32)
        slot_rhs = sb("slot_rhs", [P, 2 * NT, 3, MAXSLOTS], BF16)
        at_row = sb("at_row", [P, 4, P], BF16)
        ids_f = sb("ids_f", [P, 5, MAXSLOTS])
        ids_put = sb("ids_put", [P, MAXSLOTS], I32)
        ids_get = sb("ids_get", [P, MAXSLOTS], I32)
        cums = sb("cums", [1, E])
        exp_cmp = sb("exp_cmp", [1, MAXSLOTS, E])
        exp_f = sb("exp_f", [1, MAXSLOTS])
        exp_i = sb("exp_i", [1, MAXSLOTS], I32)
        coef = sb("coef", [P, 2, NT])
        xg = sb("xg", [P, 2, D])
        xg_t = sb("xg_t", [P, 2, P])
        y_out = sb("y_out", [P, 2, D])

        xn_dram = nc.dram_tensor("xn_scratch", [B * S, D], F32, kind="Internal").ap()
        y_dram = nc.dram_tensor("y_scratch", [2 * B * S + P * MAXSLOTS, D], F32, kind="Internal").ap()

        def kc(name, rows=P):
            a, n = CONST_COLS[name]
            return k_sb[0:rows, a:a + n]

        def kcb(name, rows=P):
            a, n = CONST_COLS[name]
            return kb_sb[0:rows, a:a + n]

        ident = kc("ident")
        x_tiles = x.rearrange("(t p) d -> p t d", p=P)
        out_tiles = out.rearrange("(t p) d -> p t d", p=P)
        xn_tiles = xn_dram.rearrange("(t p) d -> p t d", p=P)
        y_tiles = y_dram.rearrange("(t p) d -> p t d", p=P)

        def spread(ap, shape, axis):
            return ap.unsqueeze(axis).to_broadcast(shape)

        ld = sems("landed", "const x small ctx w0 w1 up0 up1 down0 down1")
        N_SMALL = 10
        init = sems("ready", "gates base_bias base constb vlen keep drop neg")
        prep = [sems(f"prep{n}", names + " prod prod_out turned turned_out")
                for n, names in enumerate(("stats mv ln rs cn cn_turned cn_t", "kept rows"))]
        att = [sems(f"att{n}", names + "st_a mv_a ln_a rs_a xn xn_turned xn_t scores max sub exp sum "
                    "rec probs turned probs_t pv res st_b mv_b ln_b rs_b xo xo_turned xo_t stored0 stored1 "
                    "logit logit_out") for n, names in enumerate(("", "y0 y1 y2 y3 base "))]
        rout = [sems(f"route{n}", "dve picked totals counts blocks positions gap expd at_row ids tables")
                for n in range(2)]
        ffn = [sems(f"ffn{n}", names + "gathered0 gathered1 turned xg_t up hid hid_turned hid_t down y "
                    "scattered0 scattered1") for n, names in enumerate(("act ", "biased "))]
        fin = sems("final", "y0 y1 y2 y3 half done0 stored")

        LAYERS = (layer_plan(0, H0, HD0 ** -0.5, ((0, 2, 4),), 1),
                  layer_plan(1, H1, HD1 ** -0.5, ((0, 2, 6), (2, 1, 4)), 2))

        def score_views(layer, flat):
            h = 0
            for bank, nb, hn in layer.parts:
                cols = slice(h * NKEY, (h + nb * hn) * NKEY)
                yield (ps[:, bank:bank + nb, 0:hn * NKEY].rearrange("p b (h k) -> p b h k", k=NKEY),
                       flat[:, cols].rearrange("p (b h k) -> p b h k", b=nb, k=NKEY),
                       mx[:, h:h + nb * hn].rearrange("p (b h) -> p b h", b=nb))
                h += nb * hn

        def score_banks(layer):
            h = 0
            for bank, nb, hn in layer.parts:
                for k in range(nb):
                    yield bank + k, h, hn
                    h += hn

        def prep_products(layer):
            n_proj = 8 if layer.n == 0 else 2
            return n_proj, layer.heads

        def act_prep(act, layer):
            p = prep[layer.n]
            n_proj, heads = prep_products(layer)
            for j in range(n_proj + 2 * heads):
                src = ps[:, j % 4, 0:CTX]
                act.wait_ge(p.prod, j + 1)
                if j < n_proj:
                    if layer.n == 0:
                        nc.scalar.copy(kv_t[:, j, :], src).then_inc(p.prod_out, 1)
                    else:
                        nc.scalar.copy(kv1_t[:, j, :], src).then_inc(p.prod_out, 1)
                elif j < n_proj + heads:
                    h = j - n_proj
                    nc.scalar.copy(score_mat[layer.n][:, :, h * NKEY:(h + 1) * NKEY],
                                   src.rearrange("p (b k) -> p b k", b=B)).then_inc(p.prod_out, 1)
                else:
                    h = j - n_proj - heads
                    vw = vw_t[:, 0:B * layer.cols].rearrange("p (b c) -> p b c", b=B)
                    nc.scalar.activation(vw[:, :, h * NKEY:(h + 1) * NKEY],
                                         src.rearrange("p (b k) -> p b k", b=B), ACT.Copy,
                                         scale=gate_t[:, layer.n:layer.n + 1]).then_inc(p.prod_out, 1)

        def pe_prep(pe, layer):
            p = prep[layer.n]
            n_proj, heads = prep_products(layer)
            if layer.n == 1:
                pe.wait_ge(prep[0].turned_out, B * 2)
                pe.wait_ge(prep[0].prod_out, sum(prep_products(LAYERS[0])) + H0)
            else:
                pe.wait_ge(p.cn_t, 1)
            for j in range(n_proj + 2 * heads):
                if j >= 4:
                    pe.wait_ge(p.prod_out, j - 3)
                dst = ps[:, j % 4, 0:CTX]
                if j < n_proj:
                    if layer.n == 0:
                        last = nc.tensor.matmul(dst, wkv0_sb[:, j * P:(j + 1) * P], cn_t[:, :], start=True, stop=True)
                    else:
                        last = nc.tensor.matmul(dst, wqkvo1_sb[:, 1 + j, :], c_t[:, :], start=True, stop=True)
                else:
                    value = j >= n_proj + heads
                    h = (j - n_proj) % heads
                    if layer.n == 0:
                        pe.wait_ge(p.prod_out, 4 * value + h // 2 + 1)
                        w = wout0_sb if value else wq0_sb
                        r = slice(64 * (h % 2), 64 * (h % 2) + 64)
                        last = nc.tensor.matmul(dst, w[r, h // 2, :], kv_t[r, 4 * value + h // 2, :],
                                                start=True, stop=True)
                    else:
                        pe.wait_ge(p.rows, j - n_proj + 1)
                        w = wqkvo1_sb[:, 3 if value else 0, :]
                        last = nc.tensor.matmul(dst, w, head_kv[:, j % 2, :], start=True, stop=True)
                last.then_inc(p.prod, 1)
            pe.wait_ge(p.prod_out, n_proj + 2 * heads)
            vw = vw_t[:, 0:B * layer.cols].rearrange("p (b c) -> p b c", b=B)
            n = 0
            for b in range(B):
                for group in layer.groups:
                    if n >= 2:
                        pe.wait_ge(p.turned_out, n - 1)
                    for k, c in enumerate(group):
                        a, size = layer.chunks[c]
                        last = nc.tensor.transpose(ps[0:size, 4 + n % 2, k * P:(k + 1) * P],
                                                   vw[:, b, a:a + size], ident)
                    last.then_inc(p.turned, 1)
                    n += 1

        def dve_prep_turned(dve, layer):
            p = prep[layer.n]
            n, per = 0, len(layer.chunks)
            for b in range(B):
                for group in layer.groups:
                    dve.wait_ge(p.turned, n + 1)
                    for run in full_and_rest(group, layer.chunks):
                        size = layer.chunks[run[0]][1]
                        k = run[0] - group[0]
                        last = nc.vector.tensor_copy(
                            value_mat[layer.n][0:size, b * per + run[0]:b * per + run[-1] + 1, :],
                            ps[0:size, 4 + n % 2, k * P:(k + len(run)) * P].rearrange("p (c d) -> p c d", d=D))
                    last.then_inc(p.turned_out, 1)
                    n += 1

        (ROWS, RSTD_A, NORM_A, SCORES, SOFTMAX, SUMS, VALUES, RESIDUAL, RSTD_B, NORM_B, ROUTER, LOGITS) = range(12)
        STEPS = range(NT + LOGITS)

        def tiles(t, *stages):
            return [t - stage if 0 <= t - stage < NT else None for stage in stages]

        def dve_attention(dve, layer):
            s, L = att[layer.n], layer
            src = res if L.n == 0 else base
            for t in STEPS:
                i_res, i_rows = tiles(t, RESIDUAL, ROWS)
                if i_res is not None:
                    dve.wait_ge(s.pv, i_res + 1)
                    nc.vector.tensor_tensor(res[:, i_res, :], ps[:, 5, 0:D], base[:, i_res, :],
                                            ALU.add).then_inc(s.res, 1)
                i, = tiles(t, SOFTMAX)
                if i is not None:
                    dve.wait_ge(s.scores, i + 1)
                    for scores, _, maxima in score_views(L, sub):
                        last = nc.vector.tensor_reduce(maxima, scores, AX.X, ALU.max)
                    last.then_inc(s.max, 1)
                    dve.wait_ge(s.max, i + 1)
                    if i >= 1:
                        dve.wait_ge(s.exp, i)
                    for scores, flat, maxima in score_views(L, sub):
                        last = nc.vector.tensor_tensor(flat, scores, spread(maxima, list(scores.shape), 3),
                                                       ALU.subtract)
                    last.then_inc(s.sub, 1)
                i, = tiles(t, SUMS)
                if i is not None:
                    dve.wait_ge(s.exp, i + 1)
                    nc.vector.tensor_reduce(rec[:, i % 2, 0, 0:L.heads],
                                            expd[i % 2][:, 0:L.cols].rearrange("p (h k) -> p h k", k=NKEY),
                                            AX.X, ALU.add).then_inc(s.sum, 1)
                    dve.wait_ge(s.sum, i + 1)
                    if i >= 2:
                        dve.wait_ge(s.probs, i - 1)
                    nc.vector.reciprocal(rec[:, i % 2, 1, 0:L.heads], rec[:, i % 2, 0, 0:L.heads]).then_inc(s.rec, 1)
                i, = tiles(t, NORM_A)
                if i is not None:
                    dve.wait_ge(s.rs_a, i + 1)
                    if i >= 2:
                        dve.wait_ge(s.xn_turned, i - 1)
                    nc.vector.tensor_scalar(xn[:, i % 2, :], src[:, i, :], mv[:, i % 4, 0:1], rs[:, i % 4, 1:2],
                                            ALU.subtract, ALU.mult).then_inc(s.xn, 1)
                i, = tiles(t, ROWS)
                if i is not None:
                    if L.n == 1:
                        dve.wait_ge((s.y0, s.y1, s.y2, s.y3)[i // TPB], 16)
                        nc.vector.scalar_tensor_tensor(base[:, i, :], base[:, i, :], coef[:, 0, i:i + 1],
                                                       res[:, i, :], ALU.mult, ALU.add).then_inc(s.base, 1)
                        dve.wait_ge(s.base, i + 1)
                    nc.vector.bn_stats(stats[:, i % 2, :], src[:, i, :]).then_inc(s.st_a, 1)
                if i_rows is not None:
                    dve.wait_ge(s.st_a, i_rows + 1)
                    nc.vector.bn_aggr(mv[:, i_rows % 4, :], stats[:, i_rows % 2, :]).then_inc(s.mv_a, 1)
                if i_res is not None:
                    dve.wait_ge(s.res, i_res + 1)
                    nc.vector.bn_stats(stats[:, 2 + i_res % 2, :], res[:, i_res, :]).then_inc(s.st_b, 1)
                i, = tiles(t, NORM_B)
                if i is not None:
                    dve.wait_ge(s.rs_b, i + 1)
                    if i >= 2:
                        dve.wait_ge(s.xo_turned, i - 1)
                        dve.wait_ge((s.stored0, s.stored1)[i % 2], i // 2 * 16)
                    nc.vector.tensor_scalar(xo[:, i % 2, :], res[:, i, :], mv[:, 4 + i % 4, 0:1],
                                            rs[:, 4 + i % 4, 1:2], ALU.subtract, ALU.mult).then_inc(s.xo, 1)
                if i_res is not None:
                    dve.wait_ge(s.st_b, i_res + 1)
                    nc.vector.bn_aggr(mv[:, 4 + i_res % 4, :], stats[:, 2 + i_res % 2, :]).then_inc(s.mv_b, 1)
                i, = tiles(t, LOGITS)
                if i is not None:
                    dve.wait_ge(s.logit, i + 1)
                    nc.vector.tensor_tensor(logits[:, i, :], ps[:, 7, 0:E], rb[:, L.n, :],
                                            ALU.add).then_inc(s.logit_out, 1)

        def act_attention(act, layer):
            s, L = att[layer.n], layer
            v_scale, eps_a = (1.0 + EPS, kc("eps2")) if L.n == 0 else (1.0, kc("eps"))
            nc.scalar.preload_act_table_set("natural_log_exp_and_others")
            for t in STEPS:
                i_a, i_b = tiles(t, RSTD_A, RSTD_B)
                if i_a is not None:
                    act.wait_ge(s.mv_a, i_a + 1)
                    nc.scalar.activation(rs[:, i_a % 4, 0:1], mv[:, i_a % 4, 1:2], ACT.Ln, bias=eps_a,
                                         scale=v_scale).then_inc(s.ln_a, 1)
                if i_b is not None:
                    act.wait_ge(s.mv_b, i_b + 1)
                    nc.scalar.activation(rs[:, 4 + i_b % 4, 0:1], mv[:, 4 + i_b % 4, 1:2], ACT.Ln,
                                         bias=kc("eps")).then_inc(s.ln_b, 1)
                if i_a is not None:
                    act.wait_ge(s.ln_a, i_a + 1)
                    nc.scalar.activation(rs[:, i_a % 4, 1:2], rs[:, i_a % 4, 0:1], ACT.Exp,
                                         scale=-0.5).then_inc(s.rs_a, 1)
                if i_b is not None:
                    act.wait_ge(s.ln_b, i_b + 1)
                    nc.scalar.activation(rs[:, 4 + i_b % 4, 1:2], rs[:, 4 + i_b % 4, 0:1], ACT.Exp,
                                         scale=-0.5).then_inc(s.rs_b, 1)
                i, = tiles(t, SCORES)
                if i is not None:
                    act.wait_ge(s.xn_turned, i + 1)
                    if i >= 2:
                        act.wait_ge(s.scores, i - 1)
                    if L.n == 0:
                        nc.scalar.activation(xn_t[:, i % 2, :], ps[:, 6, 0:P], ACT.Identity, bias=gb[:, 1:2],
                                             scale=gb[:, 0:1]).then_inc(s.xn_t, 1)
                    else:
                        nc.scalar.copy(xn_t[:, i % 2, :], ps[:, 6, 0:P]).then_inc(s.xn_t, 1)
                i, = tiles(t, VALUES)
                if i is not None:
                    if i >= 1:
                        act.wait_ge(s.pv, i)
                    for g, group in enumerate(L.groups):
                        act.wait_ge(s.turned, i * len(L.groups) + g + 1)
                        for run in full_and_rest(group, L.chunks):
                            size, k = L.chunks[run[0]][1], run[0] - group[0]
                            last = nc.scalar.copy(
                                probs_t[0:size, run[0]:run[-1] + 1, :],
                                ps[0:size, 3 + g % 2, k * P:(k + len(run)) * P].rearrange("p (c n) -> p c n", n=P))
                        last.then_inc(s.probs_t, 1)
                i, = tiles(t, ROUTER)
                if i is not None:
                    act.wait_ge(s.xo_turned, i + 1)
                    if i >= 2:
                        act.wait_ge(s.logit, i - 1)
                    nc.scalar.copy(xo_t[:, i % 2, :], ps[:, 6, 0:P]).then_inc(s.xo_t, 1)
                i, = tiles(t, SOFTMAX)
                if i is not None:
                    act.wait_ge(s.sub, i + 1)
                    if i >= 2:
                        act.wait_ge(s.turned, (i - 1) * len(L.groups))
                    nc.scalar.activation(expd[i % 2][:, 0:L.cols], sub[:, 0:L.cols], ACT.Exp,
                                         scale=L.scale).then_inc(s.exp, 1)

        def pool_attention(pool, layer):
            s, L = att[layer.n], layer
            for i in range(NT):
                pool.wait_ge(s.rec, i + 1)
                e = expd[i % 2][:, 0:L.cols].rearrange("p (h k) -> p h k", k=NKEY)
                nc.gpsimd.tensor_tensor(e, e, spread(rec[:, i % 2, 1, 0:L.heads], [P, L.heads, NKEY], 2),
                                        ALU.mult).then_inc(s.probs, 1)

        def pe_attention(pe, layer):
            s, L = att[layer.n], layer
            G, per = len(L.groups), len(L.chunks)
            turned_in = {}
            for t in STEPS:
                i, = tiles(t, SCORES)
                if i is not None:
                    pe.wait_ge(s.xn, i + 1)
                    if i >= 1:
                        pe.wait_ge(s.xn_t, i)
                    router, = tiles(t - 1, ROUTER)
                    if router is not None:
                        pe.wait_ge(s.xo_t, router + 1)
                    nc.tensor.transpose(ps[:, 6, 0:P], xn[:, i % 2, :], ident).then_inc(s.xn_turned, 1)
                i, = tiles(t, VALUES)
                if i is not None:
                    pe.wait_ge(s.probs, i + 1)
                    for g, group in enumerate(L.groups):
                        if g % 2 in turned_in:
                            pe.wait_ge(s.probs_t, turned_in[g % 2] + 1)
                        turned_in[g % 2] = i * G + g
                        for k, c in enumerate(group):
                            a, size = L.chunks[c]
                            last = nc.tensor.transpose(ps[0:size, 3 + g % 2, k * P:(k + 1) * P],
                                                       expd[i % 2][:, a:a + size], ident)
                        last.then_inc(s.turned, 1)
                i, = tiles(t, ROUTER)
                if i is not None:
                    pe.wait_ge(s.xo, i + 1)
                    if i >= 1:
                        pe.wait_ge(s.xo_t, i)
                    pe.wait_ge(s.xn_t, min(t - SCORES + 1, NT))
                    nc.tensor.transpose(ps[:, 6, 0:P], xo[:, i % 2, :], ident).then_inc(s.xo_turned, 1)
                i, = tiles(t, VALUES)
                if i is not None:
                    if i >= 1:
                        pe.wait_ge(s.res, i)
                    for g, group in enumerate(L.groups):
                        pe.wait_ge(s.probs_t, i * G + g + 1)
                        for c in group:
                            size = L.chunks[c][1]
                            last = nc.tensor.matmul(ps[:, 5, 0:D], probs_t[0:size, c, :],
                                                    value_mat[L.n][0:size, i // TPB * per + c, :],
                                                    start=(c == 0), stop=(c == per - 1))
                    last.then_inc(s.pv, 1)
                i, = tiles(t, SCORES)
                if i is not None:
                    pe.wait_ge(s.xn_t, i + 1)
                    if i >= 1:
                        pe.wait_ge(s.sub, i)
                    for bank, h, hn in score_banks(L):
                        dst = ps[:, bank, 0:hn * NKEY]
                        if L.n == 1:
                            nc.tensor.matmul(dst, kcb("ones", 1),
                                             spread(drop[0:1, i // TPB, :], [1, hn, NKEY], 1),
                                             start=True, stop=False)
                        last = nc.tensor.matmul(dst, xn_t[:, i % 2, :],
                                                score_mat[L.n][:, i // TPB, h * NKEY:(h + hn) * NKEY],
                                                start=(L.n == 0), stop=True)
                    last.then_inc(s.scores, 1)
                i, = tiles(t, ROUTER)
                if i is not None:
                    pe.wait_ge(s.xo_t, i + 1)
                    if i >= 1:
                        pe.wait_ge(s.logit_out, i)
                    nc.tensor.matmul(ps[:, 7, 0:E], xo_t[:, i % 2, :], rw[:, L.n, :], start=True,
                                     stop=True).then_inc(s.logit, 1)

        def sp_attention(sp, layer):
            s = att[layer.n]
            for i in range(NT):
                sp.wait_ge(s.xo, i + 1)
                sp.dma_start(xn_tiles[:, i, :], xo[:, i % 2, :]).then_inc((s.stored0, s.stored1)[i % 2], 16)

        def dve_route(dve, layer):
            r, L, K, NS = rout[layer.n], layer, layer.choices, layer.slots
            done = [0]

            def link(ins):
                done[0] += 1
                ins.then_inc(r.dve, 1)
                dve.wait_ge(r.dve, done[0])

            def col(c, shape=(P, NT, E)):
                return spread(rcol[:, c, :], list(shape), 2)

            dve.wait_ge(att[L.n].logit_out, NT)
            rank = spread(kc("expert_rank"), [P, NT, E], 1)
            cand = logits
            for k in range(K):
                link(nc.vector.tensor_reduce(rcol[:, 2 * k, :], cand[:, :, :], AX.X, ALU.max))
                link(nc.vector.tensor_tensor(rt[:, 0], cand[:, :, :], col(2 * k), ALU.is_equal))
                link(nc.vector.tensor_tensor(rt[:, 0], rt[:, 0], rank, ALU.mult))
                link(nc.vector.tensor_reduce(rcol[:, 1, :], rt[:, 0], AX.X, ALU.max))
                link(nc.vector.tensor_tensor(pick[:, k], rt[:, 0], col(1), ALU.is_equal))
                if k + 1 < K:
                    link(nc.vector.scalar_tensor_tensor(rt[:, 1], pick[:, k], -BIG, logits[:, :, :],
                                                        ALU.mult, ALU.add))
                    cand = rt[:, 1]
            if K == 1:
                nc.vector.tensor_copy(pick_b[:, :, :], pick[:, 0]).then_inc(r.picked, 1)
            else:
                nc.vector.tensor_tensor(pick_b[:, :, :], pick[:, 0], pick[:, 1], ALU.add).then_inc(r.picked, 1)
            if K == 1:
                nc.vector.tensor_tensor(rt[:, 2], logits[:, :, :], col(0), ALU.subtract).then_inc(r.gap, 1)
            else:
                nc.vector.tensor_tensor(rcol[:, 4, :], rcol[:, 2, :], rcol[:, 0, :], ALU.subtract).then_inc(r.gap, 1)
            dve.wait_ge(r.totals, 1)
            nc.vector.tensor_copy(totals[:, :], ps[:, 1, 0:P]).then_inc(r.totals, 1)
            dve.wait_ge(r.counts, 1)
            link(nc.vector.tensor_scalar(nblk[0:E, 0:NT], kc("slot_edges", E), ps[0:E, 2, 0:1], None, ALU.is_lt))
            link(nc.vector.tensor_reduce(nblk[0:E, NT:NT + 1], nblk[0:E, 0:NT], AX.X, ALU.add))
            nc.vector.tensor_scalar(nblk_b[0:E, :], kc("ones", E), nblk[0:E, NT:NT + 1], None,
                                    ALU.mult).then_inc(r.blocks, 1)
            dve.wait_ge(r.positions, 1)
            for k in range(K):
                link(nc.vector.tensor_tensor(rt[:, 0], ps[:, 0, 0:P].rearrange("p (t e) -> p t e", e=E),
                                             pick[:, k], ALU.mult))
                link(nc.vector.tensor_reduce(pos_f[:, 0, k * NT:(k + 1) * NT], rt[:, 0], AX.X, ALU.add))
            n = K * NT
            link(nc.vector.tensor_copy(pos_i[:, 0, 0:n], pos_f[:, 0, 0:n]))
            link(nc.vector.tensor_scalar(pos_i[:, 1, 0:n], pos_i[:, 0, 0:n], 7, None, ALU.logical_shift_right))
            link(nc.vector.tensor_scalar(pos_i[:, 2, 0:n], pos_i[:, 0, 0:n], P - 1, None, ALU.bitwise_and))
            link(nc.vector.tensor_copy(pos_f[:, 1:3, 0:n], pos_i[:, 1:3, 0:n]))
            hit = slot_rhs[:, 0:n, 2, 0:NS]
            link(nc.vector.tensor_tensor(hit, spread(kc("slot_number")[:, 0:NS], [P, n, NS], 1),
                                         spread(pos_f[:, 1, 0:n], [P, n, NS], 2), ALU.is_equal))
            link(nc.vector.tensor_scalar(slot_rhs[:, 0:n, 0, 0:NS], hit, kc("partition"), None, ALU.mult))
            link(nc.vector.tensor_tensor(slot_rhs[:, 0:n, 1, 0:NS], hit,
                                         spread(kc("tile_number")[:, 0:n], [P, n, NS], 2), ALU.mult))
            for m in range(n):
                if m >= 4:
                    dve.wait_ge(r.ids, m - 3)
                nc.vector.tensor_scalar(at_row[:, m % 4, :], kcb("row_number"), pos_f[:, 2, m:m + 1], None,
                                        ALU.is_equal).then_inc(r.at_row, 1)
            link(nc.vector.tensor_copy(cums[:, :], ps[0:1, 3, 0:E]))
            link(nc.vector.tensor_tensor(exp_cmp[:, 0:NS, :], spread(cums[:, :], [1, NS, E], 1),
                                         spread(kc("slot_number", 1)[:, 0:NS], [1, NS, E], 2), ALU.is_le))
            link(nc.vector.tensor_reduce(exp_f[:, 0:NS], exp_cmp[:, 0:NS, :], AX.X, ALU.add))
            link(nc.vector.tensor_scalar(exp_i[:, 0:NS], exp_f[:, 0:NS], E - 1.0, None, ALU.min))
            dve.wait_ge(r.ids, n)
            link(nc.vector.tensor_copy(ids_f[:, 0:3, 0:NS],
                                       ps[:, 4, 0:3 * NS].rearrange("p (c s) -> p c s", c=3)))
            link(nc.vector.scalar_tensor_tensor(ids_f[:, 3, 0:NS], ids_f[:, 1, 0:NS], float(P), ids_f[:, 0, 0:NS],
                                                ALU.mult, ALU.add))
            link(nc.vector.tensor_scalar(ids_f[:, 4, 0:NS], ids_f[:, 2, 0:NS], -1.0, 1.0, ALU.mult, ALU.add))
            link(nc.vector.tensor_tensor(ids_f[:, 4, 0:NS], ids_f[:, 4, 0:NS], kc("pad_rows")[:, 0:NS], ALU.mult))
            link(nc.vector.tensor_tensor(ids_put[:, 0:NS], ids_f[:, 3, 0:NS], ids_f[:, 4, 0:NS], ALU.add))
            nc.vector.tensor_scalar(ids_get[:, 0:NS], ids_put[:, 0:NS], B * S - 1, None,
                                    ALU.bitwise_and).then_inc(r.tables, 1)
            gate = gate_t[:, 2 + L.n:3 + L.n]
            dve.wait_ge(r.expd, 1)
            if K == 1:
                link(nc.vector.tensor_reduce(rcol[:, 5, :], rt[:, 2], AX.X, ALU.add))
                link(nc.vector.reciprocal(rcol[:, 6, :], rcol[:, 5, :]))
            else:
                link(nc.vector.tensor_scalar(rcol[:, 5, :], rcol[:, 7, :], 1.0, None, ALU.add))
                link(nc.vector.reciprocal(rcol[:, 6, :], rcol[:, 5, :]))
            link(nc.vector.tensor_scalar(coef[:, 0, :], rcol[:, 6, :], gate, None, ALU.mult))
            if K == 2:
                link(nc.vector.tensor_tensor(coef[:, 1, :], coef[:, 0, :], rcol[:, 7, :], ALU.mult))

        def act_route(act, layer):
            r = rout[layer.n]
            act.wait_ge(r.gap, 1)
            if layer.choices == 1:
                nc.scalar.activation(rt[:, 2], rt[:, 2], ACT.Exp).then_inc(r.expd, 1)
            else:
                nc.scalar.activation(rcol[:, 7, :], rcol[:, 4, :], ACT.Exp).then_inc(r.expd, 1)

        def pe_route(pe, layer):
            r, n, NS = rout[layer.n], layer.choices * NT, layer.slots
            flat = pick_b[:, :, :].rearrange("p t e -> p (t e)")
            pe.wait_ge(r.picked, 1)
            nc.tensor.matmul(ps[:, 0, 0:P], kcb("before"), flat, start=True, stop=False)
            nc.tensor.matmul(ps[:, 1, 0:P], flat, kcb("ones"), start=True, stop=True).then_inc(r.totals, 1)
            pe.wait_ge(r.totals, 2)
            nc.tensor.matmul(ps[0:E, 2, 0:P], kcb("same_expert"), totals[:, :], start=True,
                             stop=True).then_inc(r.counts, 1)
            nc.tensor.matmul(ps[:, 0, 0:P], totals[:, :], kcb("earlier_tile"), start=False, stop=False)
            pe.wait_ge(r.blocks, 1)
            nc.tensor.matmul(ps[:, 3, 0:E], nblk_b[0:E, :], kcb("upto_expert", E), start=True, stop=True)
            nc.tensor.matmul(ps[:, 0, 0:P], nblk_b[0:E, :], kcb("lower_expert", E), start=False,
                             stop=True).then_inc(r.positions, 1)
            for m in range(n):
                pe.wait_ge(r.at_row, m + 1)
                nc.tensor.matmul(ps[:, 4, 0:3 * NS], at_row[:, m % 4, :], slot_rhs[:, m, :, 0:NS],
                                 start=(m == 0), stop=(m == n - 1)).then_inc(r.ids, 1)

        def up_banks(layer, q):
            return (q, (2, 7)[q]) if layer.n == 0 else (q,)

        def pool_experts(pool, layer):
            f, NS = ffn[layer.n], layer.slots
            a = att[layer.n]
            pool.wait_ge(rout[layer.n].tables, 1)
            pool.wait_ge(a.stored0, 16 * NT // 2)
            pool.wait_ge(a.stored1, 16 * NT // 2)
            for t in range(NS + 4):
                if t < NS:
                    if t >= 2:
                        pool.wait_ge(f.turned, t - 1)
                    pool.indirect_dma_start(
                        xg[:, t % 2, :], None, xn_dram,
                        bass.IndirectOffsetOnAxis(ap=ids_get[:, t:t + 1].bitcast(U32), axis=0)
                    ).then_inc((f.gathered0, f.gathered1)[t % 2], 16)
                if t >= 4:
                    j = t - 4
                    pool.wait_ge(f.y, j + 1)
                    pool.indirect_dma_start(
                        y_dram, bass.IndirectOffsetOnAxis(ap=ids_put[:, j:j + 1].bitcast(U32), axis=0),
                        y_out[:, j % 2, :], None
                    ).then_inc((f.scattered0, f.scattered1)[j % 2], 16)

        def pe_experts(pe, layer):
            f, L, NS = ffn[layer.n], layer, layer.slots
            pe.wait_ge(rout[L.n].tables, 1)
            pe.wait_ge((ld.up0, ld.up1)[L.n], 16 * (L.n + 1))
            pe.wait_ge((ld.down0, ld.down1)[L.n], 16)

            def expert(j):
                return pe.value_load(exp_i[0:1, ds(j, 1)], min_val=0, max_val=E - 1)

            def step(t, par):
                if live(t, 0, NS):
                    i, q = t, par
                    pe.wait_ge((f.gathered0, f.gathered1)[q], (i - q) * 8 + 16)
                    if past(i, 1):
                        pe.wait_ge(f.xg_t, i)
                    nc.tensor.transpose(ps[:, 6, 0:P], xg[:, q, :], ident).then_inc(f.turned, 1)
                if live(t, 3, NS):
                    i, q = t - 3, (par - 3) % 2
                    pe.wait_ge(f.hid, i + 1)
                    if past(i, 2):
                        pe.wait_ge(f.hid_t, i - 1)
                    for c in range(4):
                        last = nc.tensor.transpose(ps[:, 3 + q, c * P:(c + 1) * P],
                                                   hid[:, q, c * P:(c + 1) * P], ident)
                    last.then_inc(f.hid_turned, 1)
                if live(t, 1, NS):
                    i, q = t - 1, (par - 1) % 2
                    e = expert(i)
                    pe.wait_ge(f.xg_t, i + 1)
                    if past(i, 2):
                        pe.wait_ge(f.hid if L.n == 0 else f.biased, i - 1)
                    for k, bank in enumerate(up_banks(L, q)):
                        last = nc.tensor.matmul(ps[:, bank, :], xg_t[:, q, :],
                                                w_up[L.n][:, ds(e, 1), k * FFN:(k + 1) * FFN], start=True, stop=True)
                    last.then_inc(f.up, 1)
                if live(t, 3, NS):
                    i, q = t - 3, (par - 3) % 2
                    e = expert(i)
                    pe.wait_ge(f.hid_t, i + 1)
                    if past(i, 1):
                        pe.wait_ge(f.y, i)
                    for c in range(4):
                        last = nc.tensor.matmul(ps[:, 5, 0:D], hid_t[:, q, c, :], w_down[:, ds(e, 1), c, :],
                                                start=(c == 0), stop=(c == 3))
                    last.then_inc(f.down, 1)

            pipeline(pe, NS, 3, step)

        def act_experts(act, layer):
            f, L, NS = ffn[layer.n], layer, layer.slots

            def step(t, par):
                if live(t, 0, NS):
                    i, q = t, par
                    act.wait_ge(f.turned, i + 1)
                    if past(i, 2):
                        act.wait_ge(f.up, i - 1)
                    nc.scalar.copy(xg_t[:, q, :], ps[:, 6, 0:P]).then_inc(f.xg_t, 1)
                if live(t, 3, NS):
                    i, q = t - 3, (par - 3) % 2
                    act.wait_ge(f.hid_turned, i + 1)
                    if past(i, 2):
                        act.wait_ge(f.down, i - 1)
                    nc.scalar.copy(hid_t[:, q], ps[:, 3 + q, :].rearrange("p (c n) -> p c n", c=4)).then_inc(f.hid_t, 1)
                if live(t, 1, NS):
                    i, q = t - 1, (par - 1) % 2
                    if L.n == 0:
                        act.wait_ge(f.up, i + 1)
                        if past(i, 2):
                            act.wait_ge(f.hid, i - 1)
                        nc.scalar.activation(act_a[:, q, :], ps[:, up_banks(L, q)[0], :], ACT.Silu).then_inc(f.act, 1)
                    else:
                        act.wait_ge(f.biased, i + 1)
                        if past(i, 2):
                            act.wait_ge(f.hid_turned, i - 1)
                        nc.scalar.activation(hid[:, q, :], act_a[:, q, :], ACT.Gelu).then_inc(f.hid, 1)

            pipeline(act, NS, 3, step)

        def dve_experts(dve, layer):
            f, L, NS = ffn[layer.n], layer, layer.slots
            dve.wait_ge(rout[L.n].tables, 1)
            if L.n == 1:
                dve.wait_ge(ld.up1, 32)
                dve.wait_ge(ld.small, 16 * N_SMALL)

            def step(t, par):
                if live(t, 0, NS):
                    i, q = t, par
                    dve.wait_ge(f.up, i + 1)
                    if L.n == 0:
                        dve.wait_ge(f.act, i + 1)
                        if past(i, 2):
                            dve.wait_ge(f.hid_turned, i - 1)
                        nc.vector.tensor_tensor(hid[:, q, :], ps[:, up_banks(L, q)[1], :], act_a[:, q, :],
                                                ALU.mult).then_inc(f.hid, 1)
                    else:
                        e = dve.value_load(exp_i[0:1, ds(i, 1)], min_val=0, max_val=E - 1)
                        if past(i, 2):
                            dve.wait_ge(f.hid, i - 1)
                        nc.vector.tensor_tensor(act_a[:, q, :], ps[:, q, :], b_up[:, ds(e, 1), :],
                                                ALU.add).then_inc(f.biased, 1)
                if live(t, 1, NS):
                    i, q = t - 1, (par - 1) % 2
                    if L.n == 1:
                        e = dve.value_load(exp_i[0:1, ds(i, 1)], min_val=0, max_val=E - 1)
                    dve.wait_ge(f.down, i + 1)
                    if past(i, 2):
                        dve.wait_ge((f.scattered0, f.scattered1)[q], (i - q) * 8)
                    if L.n == 0:
                        nc.vector.tensor_copy(y_out[:, q, :], ps[:, 5, 0:D]).then_inc(f.y, 1)
                    else:
                        nc.vector.tensor_tensor(y_out[:, q, :], ps[:, 5, 0:D], b_down[:, ds(e, 1), :],
                                                ALU.add).then_inc(f.y, 1)

            pipeline(dve, NS, 1, step)

        def wait_scattered(eng, layer):
            f, NS = ffn[layer.n], layer.slots
            eng.wait_ge(f.scattered0, 16 * ((NS + 1) // 2))
            eng.wait_ge(f.scattered1, 16 * (NS // 2))

        block = stack.enter_context(nc.Block())

        @block.sync
        def _(sp):
            sp.dma_start(ctx_sb[:, 0:2, :], ctx_rows[0:2 * P, :].rearrange("(t p) d -> p t d", p=P)).then_inc(ld.ctx, 16)
            sp.dma_start(ctx_sb[0:CTX - 2 * P, 2, :], ctx_rows[2 * P:CTX, :]).then_inc(ld.ctx, 16)
            sp.dma_start(k_sb[:, :], const).then_inc(ld.const, 16)
            small = ((gb[:, :], ln_gb), (gate_in[:, 0:2], g_xattn.to_broadcast([P, 2])),
                     (gate_in[:, 2:4], g_ffn.to_broadcast([P, 2])), (bout_b[:, :], out_bias.to_broadcast([P, D])),
                     (vlen_i[:, :], valid_len.to_broadcast([P, B])), (rw[:, 0, :], rw0), (rw[:, 1, :], rw1),
                     (rb[:, 0, :], rb0.to_broadcast([P, E])), (rb[:, 1, :], rb1.to_broadcast([P, E])),
                     (b_down[:, :, :], b2_1.to_broadcast([P, E, D])))
            assert len(small) == N_SMALL
            for dst, src in small:
                sp.dma_start(dst, src).then_inc(ld.small, 16)
            sp.dma_start(wkv0_sb[:, :], wkv0).then_inc(ld.w0, 16)
            sp.dma_start(wq0_sb[:, :, :], wq0.rearrange("(c p) d -> p c d", p=P)).then_inc(ld.w0, 16)
            sp.dma_start(wout0_sb[:, :, :], wout0.rearrange("(c p) d -> p c d", p=P)).then_inc(ld.w0, 16)
            sp.dma_start(res[:, :, :], x_tiles).then_inc(ld.x, 16)
            sp.dma_start(c_t[:, :], ctx_cols).then_inc(ld.w1, 16)
            sp.dma_start(wqkvo1_sb[:, :, :], wqkvo1).then_inc(ld.w1, 16)
            sp.dma_start(w_down[:, :, :, :], w2_0.rearrange("e (c p) d -> p e c d", p=P)).then_inc(ld.down0, 16)
            sp.wait_ge(prep[1].turned, B * len(LAYERS[1].groups))
            sp.dma_start(w_up[0], w1_0.rearrange("e d f -> d e f")).then_inc(ld.up0, 16)
            sp_attention(sp, LAYERS[0])
            for k in range(2):
                sp.wait_ge(ffn[0].up, LAYERS[0].slots)
                sp.dma_start((w_up[1], b_up)[k], (w1_1.rearrange("e d f -> d e f"), b1_1.to_broadcast([P, E, FFN]))[k]
                             ).then_inc(ld.up1, 16)
            sp.wait_ge(ffn[0].down, LAYERS[0].slots)
            sp.dma_start(w_down[:, :, :, :], w2_1.rearrange("e (c p) d -> p e c d", p=P)).then_inc(ld.down1, 16)
            wait_scattered(sp, LAYERS[0])
            for b, landed in enumerate((att[1].y0, att[1].y1, att[1].y2, att[1].y3)):
                t = slice(b * TPB, (b + 1) * TPB)
                sp.dma_start(base[:, t, :], y_tiles[:, t, :]).then_inc(landed, 16)
            sp_attention(sp, LAYERS[1])
            wait_scattered(sp, LAYERS[1])
            sp.wait_ge(ffn[1].up, LAYERS[1].slots)
            for b, landed in enumerate((fin.y0, fin.y1, fin.y2, fin.y3)):
                t = slice(b * TPB, (b + 1) * TPB)
                sp.dma_start(base[:, t, :], y_tiles[:, t, :]).then_inc(landed, 16)
                sp.dma_start(y_second[:, t, :], y_tiles[:, NT + b * TPB:NT + (b + 1) * TPB, :]).then_inc(landed, 16)
            for b in range(B):
                t = slice(b * TPB, (b + 1) * TPB)
                sp.wait_ge(fin.done0, (b + 1) * TPB)
                sp.dma_start(out_tiles[:, t, :], res[:, t, :]).then_inc(fin.stored, 16)
            sp.wait_ge(fin.stored, 16 * B)

        @block.gpsimd
        def _(pool):
            pool.wait_ge(ld.x, 16)
            pool.wait_ge(init.base_bias, 1)
            nc.gpsimd.tensor_tensor(base[:, :, :], res[:, :, :], spread(bout_g[:, :], [P, NT, D], 1),
                                    ALU.add).then_inc(init.base, 1)
            for layer in LAYERS:
                pool_attention(pool, layer)
                pool_experts(pool, layer)

        @block.scalar
        def _(act):
            act.wait_ge(ld.small, 16 * N_SMALL)
            nc.scalar.activation(gate_t[:, :], gate_in[:, :], ACT.Tanh).then_inc(init.gates, 1)
            p = prep[0]
            act.wait_ge(p.mv, 3)
            act.wait_ge(ld.const, 16)
            nc.scalar.activation(ctx_rs[:, :, 0:1], ctx_mv[:, :, 1:2], ACT.Ln, bias=kc("eps")).then_inc(p.ln, 1)
            act.wait_ge(p.ln, 1)
            nc.scalar.activation(ctx_rs[:, :, 1:2], ctx_rs[:, :, 0:1], ACT.Exp, scale=-0.5).then_inc(p.rs, 1)
            act.wait_ge(p.cn_turned, 1)
            nc.scalar.activation(cn_t[:, :], ps[:, 6, 0:CTX], ACT.Identity, bias=gb[:, 3:4],
                                 scale=gb[:, 2:3]).then_inc(p.cn_t, 1)
            act.wait_ge(init.gates, 1)
            for layer in LAYERS:
                act_prep(act, layer)
            for layer in LAYERS:
                act_attention(act, layer)
                act_route(act, layer)
                act_experts(act, layer)

        @block.tensor
        def _(pe):
            p = prep[0]
            pe.wait_ge(ld.const, 16)
            pe.wait_ge(p.cn, 3)
            for k in range(3):
                rows = min(P, CTX - k * P)
                last = nc.tensor.transpose(ps[:, 6, k * P:k * P + rows], ctx_n[0:rows, k, :], ident[0:rows, 0:rows])
            last.then_inc(p.cn_turned, 1)
            pe.wait_ge(ld.w0, 48)
            pe.wait_ge(ld.w1, 32)
            for layer in LAYERS:
                pe_prep(pe, layer)
            pe.wait_ge(prep[1].turned_out, B * len(LAYERS[1].groups))
            pe.wait_ge(ld.small, 16 * N_SMALL)
            pe.wait_ge(init.constb, 1)
            pe.wait_ge(init.drop, 1)
            for layer in LAYERS:
                pe_attention(pe, layer)
                pe_route(pe, layer)
                pe_experts(pe, layer)

        @block.vector
        def _(dve):
            p = prep[0]
            nc.vector.memset(ctx_mv[:, :, :], 1.0).then_inc(init.neg, 1)
            dve.wait_ge(init.neg, 1)
            dve.wait_ge(ld.ctx, 32)
            for k in range(3):
                rows = min(P, CTX - k * P)
                nc.vector.bn_stats(ctx_st[0:rows, k, :], ctx_sb[0:rows, k, :]).then_inc(p.stats, 1)
                dve.wait_ge(p.stats, k + 1)
                nc.vector.bn_aggr(ctx_mv[0:rows, k, :], ctx_st[0:rows, k, :]).then_inc(p.mv, 1)
            dve.wait_ge(p.rs, 1)
            for k in range(3):
                rows = min(P, CTX - k * P)
                nc.vector.tensor_scalar(ctx_n[0:rows, k, :], ctx_sb[0:rows, k, :], ctx_mv[0:rows, k, 0:1],
                                        ctx_rs[0:rows, k, 1:2], ALU.subtract, ALU.mult).then_inc(p.cn, 1)
            dve.wait_ge(ld.const, 16)
            nc.vector.tensor_copy(kb_sb[:, :], k_sb[:, :]).then_inc(init.constb, 1)
            dve.wait_ge(ld.small, 16 * N_SMALL)
            dve.wait_ge(init.gates, 1)
            nc.vector.tensor_scalar(bout_g[:, :], bout_b[:, :], gate_t[:, 0:1], None, ALU.mult
                                    ).then_inc(init.base_bias, 1)
            nc.vector.tensor_copy(vlen[:, :], vlen_i[:, :]).then_inc(init.vlen, 1)
            dve.wait_ge(init.vlen, 1)
            nc.vector.tensor_tensor(keep[:, :, :], spread(kc("key_number"), [P, B, NKEY], 1),
                                    spread(vlen[:, :], [P, B, NKEY], 2), ALU.is_le).then_inc(init.keep, 1)
            dve.wait_ge(init.keep, 1)
            nc.vector.tensor_scalar(drop[:, :, :], keep[:, :, :], -1.0, -NEG / LAYERS[1].scale,
                                    ALU.add, ALU.mult).then_inc(init.drop, 1)
            dve_prep_turned(dve, LAYERS[0])
            q = prep[1]
            dve.wait_ge(q.prod_out, 2)
            nc.vector.tensor_tensor(kv1_t[:, 0, :], kv1_t[:, 0, :], keep[:, :, :].rearrange("p b k -> p (b k)"),
                                    ALU.mult).then_inc(q.kept, 1)
            dve.wait_ge(q.kept, 1)
            for n in range(2 * H1):
                if n >= 2:
                    dve.wait_ge(q.prod, 2 + n - 1)
                nc.vector.tensor_scalar(head_kv[:, n % 2, :], kv1_t[:, n // H1, :],
                                        kc("head_rows")[:, n % H1:n % H1 + 1], None, ALU.mult).then_inc(q.rows, 1)
            dve_prep_turned(dve, LAYERS[1])
            dve.wait_ge(ld.x, 16)
            dve.wait_ge(init.base, 1)
            for layer in LAYERS:
                dve_attention(dve, layer)
                dve_route(dve, layer)
                dve_experts(dve, layer)
            for t in range(NT):
                dve.wait_ge((fin.y0, fin.y1, fin.y2, fin.y3)[t // TPB], 32)
                nc.vector.scalar_tensor_tensor(base[:, t, :], base[:, t, :], coef[:, 0, t:t + 1], res[:, t, :],
                                               ALU.mult, ALU.add).then_inc(fin.half, 1)
                dve.wait_ge(fin.half, t + 1)
                nc.vector.scalar_tensor_tensor(res[:, t, :], y_second[:, t, :], coef[:, 1, t:t + 1], base[:, t, :],
                                               ALU.mult, ALU.add).then_inc(fin.done0, 1)


def constants():
    import numpy as np

    k = np.zeros((P, NCONST), np.float32)

    def put(name, values):
        a, n = CONST_COLS[name]
        values = np.asarray(values, np.float32)
        k[:values.shape[0], a:a + n] = values

    p, t, e = np.arange(P), np.arange(P) // E, np.arange(P) % E
    put("ident", np.eye(P))
    put("ones", np.ones((P, P)))
    put("before", p[:, None] < p[None, :])
    put("earlier_tile", (e[:, None] == e[None, :]) & (t[:, None] < t[None, :]))
    put("same_expert", e[:, None] == np.arange(E)[None, :])
    put("lower_expert", P * (np.arange(E)[:, None] < e[None, :]))
    put("upto_expert", np.arange(E)[:, None] <= np.arange(E)[None, :])
    put("row_number", np.tile(p, (P, 1)))
    put("slot_number", np.tile(np.arange(MAXSLOTS), (P, 1)))
    put("partition", p[:, None])
    put("tile_number", np.tile(np.arange(2 * NT), (P, 1)))
    put("expert_rank", np.tile(E - np.arange(E), (P, 1)))
    put("head_rows", p[:, None] // HD1 == np.arange(H1)[None, :])
    put("slot_edges", np.tile(P * np.arange(NT), (P, 1)))
    put("key_number", np.tile(1 + np.arange(NKEY), (P, 1)))
    put("pad_rows", 2 * B * S + P * np.arange(MAXSLOTS)[None, :] + p[:, None])
    put("eps", np.full((P, 1), EPS))
    put("eps2", np.full((P, 1), EPS * EPS))
    return k


def kernel(**inputs):
    import numpy as np
    import concourse.bacc as bacc
    from concourse.bass_utils import run_bass_kernel_spmd

    a = {n: np.asarray(v) for n, v in inputs.items()}
    ctx = a["ctx_1024"].reshape(CTX, D)
    by_head = a["L1_xattn_Wq"].transpose(0, 2, 1).reshape(D, D)
    wqkvo1 = np.stack([by_head, a["L1_xattn_Wk"].transpose(1, 0, 2).reshape(D, D),
                       a["L1_xattn_Wv"].transpose(1, 0, 2).reshape(D, D), a["L1_xattn_Wo"]], axis=1)
    arrays = {
        "x": a["x"].reshape(B * S, D),
        "ctx_rows": ctx,
        "ctx_cols": ctx.T,
        "valid_len": a["mask_B_ik0"][None, :],
        "g_xattn": a["g_xattn"][None, :],
        "g_ffn": a["g_ffn"][None, :],
        "ln_gb": np.stack([a["L0_xattn_g1"], a["L0_xattn_b1"], a["L0_xattn_g2"], a["L0_xattn_b2"]], axis=1),
        "out_bias": a["L0_xattn_bout"][None, :],
        "wq0": a["L0_xattn_Wq"].T,
        "wkv0": a["L0_xattn_Wkv"],
        "wout0": a["L0_xattn_Wout"],
        "rw0": a["L0_ffn_router_w"],
        "rb0": a["L0_ffn_router_b"][None, :],
        "w1_0": a["L0_ffn_w1"],
        "w2_0": a["L0_ffn_w2"],
        "wqkvo1": wqkvo1,
        "w1_1": a["L1_ffn_W1"],
        "b1_1": a["L1_ffn_b1"][None, :, :],
        "w2_1": a["L1_ffn_W2"],
        "b2_1": a["L1_ffn_b2"][None, :, :],
        "rw1": a["L1_ffn_Wr"],
        "rb1": a["L1_ffn_br"][None, :],
        "const": constants(),
    }
    arrays = {n: np.ascontiguousarray(v) for n, v in arrays.items()}
    nc = bacc.Bacc("TRN2", target_bir_lowering=False, num_devices=1)
    aps = {n: nc.dram_tensor(f"in_{n}", v.shape, mybir.dt.from_np(v.dtype), kind="ExternalInput").ap()
           for n, v in arrays.items()}
    aps["out"] = nc.dram_tensor("out_dram", (B * S, D), F32, kind="ExternalOutput").ap()
    gated_stack(nc, **aps)
    r = run_bass_kernel_spmd(nc, [{f"in_{n}": v for n, v in arrays.items()}], core_ids=[0])
    return r.results[0]["out_dram"].reshape(B, S, D)
```

```python
from collections import namedtuple
from contextlib import ExitStack

import concourse.bass as bass
from concourse import mybir

P = 128
B, S, D = 4, 512, 128
NKEY = 77
CTX = B * NKEY
NT = B * S // P
TPB = NT // B
E = 8
H0, HD0 = 8, 64
H1, HD1 = 16, 8
FFN = 512
EPS = 1e-5
NEG = -1.0e6
BIG = 1.0e30
PAD = 3
RING = 4

ALU = mybir.AluOpType
ACT = mybir.ActivationFunctionType
AX = mybir.AxisListType
F32 = mybir.dt.float32
BF16 = mybir.dt.bfloat16
I32 = mybir.dt.int32
U32 = mybir.dt.uint32
ds = bass.ds

MAXSLOTS = 2 * NT + E - 1
CONST_COLS = {}
_at = 0
for _name, _n in (("ident", P), ("ones", P), ("before", P), ("earlier_tile", P), ("same_expert", E),
                  ("lower_expert", P), ("upto_expert", E), ("row_number", P), ("slot_number", MAXSLOTS),
                  ("partition", 1), ("tile_number", 2 * NT), ("expert_rank", E), ("head_rows", H1),
                  ("slot_edges", NT), ("key_number", NKEY), ("pad_rows", MAXSLOTS), ("eps", 1), ("eps2", 1)):
    CONST_COLS[_name] = (_at, _n)
    _at += _n
NCONST = _at


def live(step, lag, n):
    return not isinstance(step, int) or 0 <= step - lag < n


def past(i, n):
    return not isinstance(i, int) or i >= n


def pipeline(eng, n, depth, body, fetch=None):
    head = -(-(depth + RING) // RING) * RING
    end = n // RING * RING

    def turn(first):
        fetched = fetch(first) if fetch else None
        for k in range(RING):
            if not isinstance(first, int) or first + k < n + depth:
                body(first + k, k, fetched)

    for first in range(0, head, RING):
        turn(first)
    with eng.Fori(head // RING, end // RING) as number:
        turn(number * RING)
    for first in range(end, n + depth, RING):
        turn(first)


def key_chunks(heads):
    cols = heads * NKEY
    chunks = [(a, min(P, cols - a)) for a in range(0, cols, P)]
    return chunks, [list(range(a, min(a + 4, len(chunks)))) for a in range(0, len(chunks), 4)]


def full_and_rest(group, chunks):
    full = [c for c in group if chunks[c][1] == P]
    rest = [c for c in group if chunks[c][1] < P]
    return [r for r in (full, rest) if r]


Layer = namedtuple("Layer", "n heads scale pair choices cols chunks groups slots")


def layer_plan(n, heads, scale, pair, choices):
    return Layer(n, heads, scale, pair, choices, heads * NKEY, *key_chunks(heads), choices * NT + E - 1)


def gated_stack(nc, x, ctx_rows, ctx_cols, valid_len, g_xattn, g_ffn, ln_gb, out_bias, wq0, wkv0, wout0,
                rw0, rb0, w1_0, w2_0, wqkvo1, w1_1, b1_1, w2_1, b2_1, rw1, rb1, const, out):
    with ExitStack() as stack:
        def sb(name, shape, dt=F32):
            return stack.enter_context(nc.sbuf_tensor(name, shape, dt))

        def sem(name):
            return stack.enter_context(nc.semaphore(name))

        def sems(tag, names):
            return namedtuple("Sems", names)(*[sem(f"{n}_{tag}") for n in names.split()])

        ps = stack.enter_context(nc.psum_tensor("ps", [P, 8, 512], F32))
        k_sb = sb("k_sb", [P, NCONST])
        kb_sb = sb("kb_sb", [P, NCONST], BF16)
        res = sb("res", [P, NT, D])
        base = sb("base", [P, NT, D])
        gate_in = sb("gate_in", [P, 4])
        gate_t = sb("gate_t", [P, 4])
        gb = sb("gb", [P, 4])
        bout_b = sb("bout_b", [P, D])
        bout_g = sb("bout_g", [P, D])
        vlen_i = sb("vlen_i", [P, B], I32)
        vlen = sb("vlen", [P, B])
        keep = sb("keep", [P, B, NKEY])
        drop = sb("drop", [P, B, NKEY], BF16)
        ctx_sb = sb("ctx_sb", [P, 3, D])
        ctx_n = sb("ctx_n", [P, 3, D])
        ctx_st = sb("ctx_st", [P, 3, 6])
        ctx_mv = sb("ctx_mv", [P, 3, 2])
        ctx_rs = sb("ctx_rs", [P, 3, 2])
        cn_t = sb("cn_t", [P, CTX])
        c_t = sb("c_t", [P, CTX])
        wq0_sb = sb("wq0_sb", [P, 4, D])
        wkv0_sb = sb("wkv0_sb", [P, 2 * H0 * HD0])
        wout0_sb = sb("wout0_sb", [P, 4, D])
        wqkvo1_sb = sb("wqkvo1_sb", [P, 4, D])
        kv1_t = sb("kv1_t", [P, 2, CTX])
        score_mat = [sb("score_mat0", [P, B, H0 * NKEY]), sb("score_mat1", [P, B, H1 * NKEY])]
        value_mat = [sb("value_mat0", [P, B * 5, D]), sb("value_mat1", [P, B * 10, D])]
        temp = score_mat[1][:, :, :].rearrange("p b c -> p (b c)")
        kv_t = temp[:, 0:8 * CTX].rearrange("p (c n) -> p c n", c=8)
        vw_t = temp[:, 8 * CTX:8 * CTX + B * H0 * NKEY].rearrange("p (b c) -> p b c", b=B)
        shared = sb("shared", [P, E * 2 * FFN])
        w_up = [shared[:, :].rearrange("p (e f) -> p e f", e=E),
                shared[:, 0:E * FFN].rearrange("p (e f) -> p e f", e=E)]
        b_up = shared[:, E * FFN:2 * E * FFN].rearrange("p (e f) -> p e f", e=E)
        y_second = shared[:, 0:NT * D].rearrange("p (t d) -> p t d", t=NT)
        w_down = sb("w_down", [P, E, 4, D])
        b_down = sb("b_down", [P, E, D])
        rw = sb("rw", [P, 2, E])
        rb = sb("rb", [P, 2, E])
        xn = sb("xn", [P, 2, D])
        xn_t = sb("xn_t", [P, 2, P])
        work = sb("work", [P, 3 * H1 * NKEY])
        sub = work[:, 0:H1 * NKEY]
        expd = [work[:, (1 + k) * H1 * NKEY:(2 + k) * H1 * NKEY] for k in range(2)]
        act_a = work[:, 0:2 * FFN].rearrange("p (k f) -> p k f", k=2)
        hid = work[:, 2 * FFN:4 * FFN].rearrange("p (k f) -> p k f", k=2)
        hid_t = work[:, 4 * FFN:6 * FFN].rearrange("p (k c n) -> p k c n", k=2, c=4)
        probs_t = sb("probs_t", [P, 10, P])
        mx = sb("mx", [P, H1])
        rec = sb("rec", [P, 2, 2, H1])
        stats = sb("stats", [P, 4, 6])
        mv = sb("mv", [P, 8, 2])
        rs = sb("rs", [P, 8, 2])
        xo = sb("xo", [P, RING, D])
        xo_t = sb("xo_t", [P, 2, P])
        logits = sb("logits", [P, NT, E])
        pick = sb("pick", [P, 2, NT, E])
        rt = sb("rt", [P, 3, NT, E])
        rcol = sb("rcol", [P, 8, NT])
        pick_b = sb("pick_b", [P, NT, E], BF16)
        totals = sb("totals", [P, P], BF16)
        nblk = sb("nblk", [P, NT + 1])
        nblk_b = sb("nblk_b", [P, P], BF16)
        pos_f = sb("pos_f", [P, 3, 2 * NT])
        pos_i = sb("pos_i", [P, 3, 2 * NT], I32)
        slot_rhs = sb("slot_rhs", [P, 2 * NT, 3, MAXSLOTS], BF16)
        at_row = sb("at_row", [P, 4, P], BF16)
        ids_f = sb("ids_f", [P, 5, MAXSLOTS])
        ids_put = sb("ids_put", [P, MAXSLOTS], I32)
        ids_get = sb("ids_get", [P, MAXSLOTS], I32)
        cums = sb("cums", [1, E])
        exp_cmp = sb("exp_cmp", [1, MAXSLOTS, E])
        exp_f = sb("exp_f", [1, MAXSLOTS])
        exp_i = sb("exp_i", [1, PAD + MAXSLOTS + 2 * RING], I32)
        coef = sb("coef", [P, 2, NT])
        xg = sb("xg", [P, RING, D])
        xg_t = sb("xg_t", [P, 2, P])
        y_out = sb("y_out", [P, RING, D])

        xn_dram = nc.dram_tensor("xn_scratch", [B * S, D], F32, kind="Internal").ap()
        y_dram = nc.dram_tensor("y_scratch", [2 * B * S + P * MAXSLOTS, D], F32, kind="Internal").ap()

        def kc(name, rows=P):
            a, n = CONST_COLS[name]
            return k_sb[0:rows, a:a + n]

        def kcb(name, rows=P):
            a, n = CONST_COLS[name]
            return kb_sb[0:rows, a:a + n]

        ident = kc("ident")
        x_tiles = x.rearrange("(t p) d -> p t d", p=P)
        out_tiles = out.rearrange("(t p) d -> p t d", p=P)
        xn_tiles = xn_dram.rearrange("(t p) d -> p t d", p=P)
        y_tiles = y_dram.rearrange("(t p) d -> p t d", p=P)

        def spread(ap, shape, axis):
            return ap.unsqueeze(axis).to_broadcast(shape)

        ld = sems("landed", "const x gates small ctx w0 w1 up0 up1 down0 down1")
        N_SMALL = 7
        init = sems("ready", "gates base_bias base constb vlen keep drop neg experts")
        prep = sems("prep0", "stats mv ln rs cn cn_turned cn_t prod out_act out_dve turned turned_act turned_dve")
        blk = sems("prep1", "kept built made copied")
        att = sems("att", "y0 y1 y2 y3 base st_a mv_a ln_a rs_a xn xn_turned xn_t scores max sub_pair sub_rest exp sum "
                    "rec probs turned probs_t pv res st_b mv_b ln_b rs_b xo xo_turned xo_t stored0 stored1 stored2 stored3 "
                    "logit logit_out")
        rout = [sems(f"route{n}", "dve picked totals counts blocks positions gap expd at_row ids tables")
                for n in range(2)]
        ffn = [sems(f"ffn{n}", names + "gathered0 gathered1 gathered2 gathered3 turned xg_t up hid hid_turned hid_t "
                    "down y scattered0 scattered1 scattered2 scattered3") for n, names in enumerate(("act ", "biased "))]
        fin = sems("final", "half done stored")

        LAYERS = (layer_plan(0, H0, HD0 ** -0.5, 4, 1), layer_plan(1, H1, HD1 ** -0.5, 6, 2))

        xn_ps, xo_ps = ps[:, 6, 0:P], ps[:, 6, P:2 * P]
        pv_ps, logit_ps = ps[:, 7, 0:P], ps[:, 7, P:P + E]

        def score_views(layer, i, flat):
            hn, n_pair = layer.pair, 2 * layer.pair
            views = [(ps[:, 0:2, 0:hn * NKEY].rearrange("p b (h k) -> p b h k", k=NKEY),
                      flat[:, 0:n_pair * NKEY].rearrange("p (b h k) -> p b h k", b=2, k=NKEY),
                      mx[:, 0:n_pair].rearrange("p (b h) -> p b h", b=2))]
            if layer.heads > n_pair:
                views.append((ps[:, 2 + i % 2, 0:(layer.heads - n_pair) * NKEY].rearrange("p (h k) -> p h k", k=NKEY),
                              flat[:, n_pair * NKEY:layer.cols].rearrange("p (h k) -> p h k", k=NKEY),
                              mx[:, n_pair:layer.heads]))
            return views

        def score_banks(layer, i):
            hn = layer.pair
            rest = [(2 + i % 2, 2 * hn, layer.heads - 2 * hn)] if layer.heads > 2 * hn else []
            return rest + [(0, 0, hn), (1, hn, hn)]

        N_PROJ = 10
        N_PROD = N_PROJ + 2 * H0

        def wait_copied(eng, j):
            eng.wait_ge((prep.out_act, prep.out_dve)[j % 2], j // 2 + 1)

        def copy_products(eng, which):
            for j in range(which, N_PROD, 2):
                eng.wait_ge(prep.prod, j + 1)
                src = ps[:, j % 4, 0:CTX]
                by_batch = src.rearrange("p (b k) -> p b k", b=B)
                h = (j - N_PROJ) % H0
                cols = slice(h * NKEY, (h + 1) * NKEY)
                value = j >= N_PROJ + H0
                if j < N_PROJ:
                    dst = kv_t[:, j, :] if j < 8 else kv1_t[:, j - 8, :]
                else:
                    dst, src = (vw_t if value else score_mat[0])[:, :, cols], by_batch
                if which == 0:
                    ins = nc.scalar.activation(dst, src, ACT.Copy, scale=gate_t[:, 0:1] if value else 1.0)
                    ins.then_inc(prep.out_act, 1)
                else:
                    ins = (nc.vector.tensor_scalar(dst, src, gate_t[:, 0:1], None, ALU.mult) if value
                           else nc.vector.tensor_copy(dst, src))
                    ins.then_inc(prep.out_dve, 1)

        def pe_products(pe):
            for j in range(N_PROD):
                if j >= 4:
                    wait_copied(pe, j - 4)
                dst = ps[:, j % 4, 0:CTX]
                if j < 8:
                    nc.tensor.matmul(dst, wkv0_sb[:, j * P:(j + 1) * P], cn_t[:, :], start=True,
                                     stop=True).then_inc(prep.prod, 1)
                elif j < N_PROJ:
                    pe.wait_ge(ld.w1, 32)
                    nc.tensor.matmul(dst, wqkvo1_sb[:, 1 + j - 8, :], c_t[:, :], start=True,
                                     stop=True).then_inc(prep.prod, 1)
                else:
                    value = j >= N_PROJ + H0
                    h = (j - N_PROJ) % H0
                    wait_copied(pe, 4 * value + h // 2)
                    w = wout0_sb if value else wq0_sb
                    r = slice(64 * (h % 2), 64 * (h % 2) + 64)
                    nc.tensor.matmul(dst, w[r, h // 2, :], kv_t[r, 4 * value + h // 2, :],
                                     start=True, stop=True).then_inc(prep.prod, 1)
            for j in range(N_PROD - 2, N_PROD):
                wait_copied(pe, j)
            L = LAYERS[0]
            for b in range(B):
                for g, group in enumerate(L.groups):
                    if b >= 2:
                        pe.wait_ge((prep.turned_dve, prep.turned_act)[b % 2], (b - 2) // 2 * 2 + g + 1)
                    for k, c in enumerate(group):
                        a, size = L.chunks[c]
                        last = nc.tensor.transpose(ps[0:size, 4 + 2 * (b % 2) + g, k * P:(k + 1) * P],
                                                   vw_t[:, b, a:a + size], ident)
                    last.then_inc(prep.turned, 1)

        def copy_turned(eng, copy, first, done):
            L = LAYERS[0]
            for b in range(first, B, 2):
                for g, group in enumerate(L.groups):
                    eng.wait_ge(prep.turned, b * 2 + g + 1)
                    for run in full_and_rest(group, L.chunks):
                        size, k = L.chunks[run[0]][1], run[0] - group[0]
                        last = copy(value_mat[0][0:size, b * 5 + run[0]:b * 5 + run[-1] + 1, :],
                                    ps[0:size, 4 + 2 * (b % 2) + g, k * P:(k + len(run)) * P
                                       ].rearrange("p (c d) -> p c d", d=D))
                    last.then_inc(done, 1)

        def pool_blocks(pool):
            pool.wait_ge(ld.const, 16)
            wait_copied(pool, 9)
            for value in (1, 0):
                if not value:
                    pool.wait_ge(blk.kept, 1)
                    pool.wait_ge(prep.turned, B * 2)
                for b in range(B):
                    dst = (value_mat[1][:, b * 10:(b + 1) * 10, :].rearrange("p c d -> p (c d)")[:, 0:H1 * NKEY]
                           if value else score_mat[1][:, b, :])
                    rows = kv1_t[:, value, b * NKEY:(b + 1) * NKEY]
                    nc.gpsimd.tensor_tensor(dst.rearrange("p (h k) -> p h k", k=NKEY),
                                            spread(rows, [P, H1, NKEY], 1),
                                            spread(kc("head_rows"), [P, H1, NKEY], 2),
                                            ALU.mult).then_inc(blk.built, 1)

        N_PARTS = 6 * B

        def score_part(n):
            b, k = n // 6, n % 6
            return score_mat[1][:, b, slice(k * 6 * NKEY, min((k + 1) * 6, H1) * NKEY)]

        def value_part(n):
            group = LAYERS[1].groups[n % 6 - 3]
            return n // 6 * 10, group[0], group

        def pe_part(pe, n):
            pe.wait_ge(blk.built, n // 6 + 1 + (B if n % 6 < 3 else 0))
            if n >= 2:
                pe.wait_ge(blk.copied, n - 1)
            bank = 2 + n % 2
            if n % 6 < 3:
                src = score_part(n)
                nc.tensor.matmul(ps[:, bank, 0:src.shape[-1]], wqkvo1_sb[:, 0, :], src, start=True,
                                 stop=True).then_inc(blk.made, 1)
            else:
                at, first, group = value_part(n)
                for c in group:
                    size = LAYERS[1].chunks[c][1]
                    last = nc.tensor.matmul(ps[0:size, bank, (c - first) * P:(c - first + 1) * P],
                                            value_mat[1][:, at + c, 0:size], wqkvo1_sb[:, 3, :],
                                            start=True, stop=True)
                last.then_inc(blk.made, 1)

        def act_part(act, n):
            act.wait_ge(blk.made, n + 1)
            bank = 2 + n % 2
            if n % 6 < 3:
                dst = score_part(n)
                nc.scalar.copy(dst, ps[:, bank, 0:dst.shape[-1]]).then_inc(blk.copied, 1)
            else:
                at, first, group = value_part(n)
                for run in full_and_rest(group, LAYERS[1].chunks):
                    size, k = LAYERS[1].chunks[run[0]][1], run[0] - first
                    last = nc.scalar.activation(
                        value_mat[1][0:size, at + run[0]:at + run[-1] + 1, :],
                        ps[0:size, bank, k * P:(k + len(run)) * P].rearrange("p (c d) -> p c d", d=D),
                        ACT.Copy, scale=gate_t[0:size, 1:2])
                last.then_inc(blk.copied, 1)

        (ROWS, RSTD_A, NORM_A, SCORES, SOFTMAX, SUMS, VALUES, RESIDUAL, RSTD_B, NORM_B, ROUTER, LOGITS) = range(12)
        STEPS = range(NT + LOGITS)
        FIRST_PART, PARTS_EARLY, PARTS_PICK = 2, 18, 21

        def tiles(t, *stages):
            return [t - stage if 0 <= t - stage < NT else None for stage in stages]

        def dve_attention(dve, layer):
            s, L = att, layer
            seen = L.n * NT
            src = res if L.n == 0 else base
            for t in STEPS:
                i_res, i_rows = tiles(t, RESIDUAL, ROWS)
                i, = tiles(t, SOFTMAX)
                if i is not None:
                    dve.wait_ge(s.scores, seen + i + 1)
                    views = score_views(L, i, sub)
                    for scores, _, maxima in views:
                        last = nc.vector.tensor_reduce(maxima, scores, AX.X, ALU.max)
                    last.then_inc(s.max, 1)
                    dve.wait_ge(s.max, seen + i + 1)
                    if i >= 1:
                        dve.wait_ge(s.exp, seen + i)
                    pair, rest = views[0], views[1:]
                    nc.vector.tensor_tensor(pair[1], pair[0], spread(pair[2], list(pair[0].shape), 3),
                                            ALU.subtract).then_inc(s.sub_pair, 1)
                    for scores, flat, maxima in rest:
                        nc.vector.tensor_tensor(flat, scores, spread(maxima, list(scores.shape), 2),
                                                ALU.subtract).then_inc(s.sub_rest, 1)
                i_res, i_log = tiles(t, RESIDUAL, LOGITS)
                if i_res is not None:
                    if L.n == 0 and i_res == 0:
                        dve.wait_ge(init.base, 1)
                    dve.wait_ge(s.pv, seen + i_res + 1)
                    if i_log is not None:
                        dve.wait_ge(s.logit, seen + i_log + 1)
                    nc.vector.tensor_tensor(res[:, i_res, :], pv_ps, base[:, i_res, :], ALU.add).then_inc(s.res, 1)
                if i_log is not None:
                    dve.wait_ge(s.logit, seen + i_log + 1)
                    nc.vector.tensor_tensor(logits[:, i_log, :], logit_ps, rb[:, L.n, :],
                                            ALU.add).then_inc(s.logit_out, 1)
                i, = tiles(t, SUMS)
                if i is not None:
                    dve.wait_ge(s.exp, seen + i + 1)
                    nc.vector.tensor_reduce(rec[:, i % 2, 0, 0:L.heads],
                                            expd[i % 2][:, 0:L.cols].rearrange("p (h k) -> p h k", k=NKEY),
                                            AX.X, ALU.add).then_inc(s.sum, 1)
                    dve.wait_ge(s.sum, seen + i + 1)
                    if i >= 2:
                        dve.wait_ge(s.probs, seen + i - 1)
                    nc.vector.reciprocal(rec[:, i % 2, 1, 0:L.heads], rec[:, i % 2, 0, 0:L.heads]).then_inc(s.rec, 1)
                if i_rows is not None:
                    i = i_rows
                    if L.n == 1:
                        dve.wait_ge((s.y0, s.y1, s.y2, s.y3)[i // TPB], 16)
                        nc.vector.scalar_tensor_tensor(base[:, i, :], base[:, i, :], coef[:, 0, i:i + 1],
                                                       res[:, i, :], ALU.mult, ALU.add).then_inc(s.base, 1)
                        dve.wait_ge(s.base, i + 1)
                    nc.vector.bn_stats(stats[:, i % 2, :], src[:, i, :]).then_inc(s.st_a, 1)
                if i_res is not None:
                    dve.wait_ge(s.res, seen + i_res + 1)
                    nc.vector.bn_stats(stats[:, 2 + i_res % 2, :], res[:, i_res, :]).then_inc(s.st_b, 1)
                if i_rows is not None:
                    dve.wait_ge(s.st_a, seen + i_rows + 1)
                    if i_rows >= 4:
                        dve.wait_ge(s.xn, seen + i_rows - 3)
                    nc.vector.bn_aggr(mv[:, i_rows % 4, :], stats[:, i_rows % 2, :]).then_inc(s.mv_a, 1)
                if i_res is not None:
                    dve.wait_ge(s.st_b, seen + i_res + 1)
                    if i_res >= 4:
                        dve.wait_ge(s.xo, seen + i_res - 3)
                    nc.vector.bn_aggr(mv[:, 4 + i_res % 4, :], stats[:, 2 + i_res % 2, :]).then_inc(s.mv_b, 1)

        def act_attention(act, layer):
            s, L = att, layer
            seen = L.n * NT
            seen_groups = L.n * NT * len(LAYERS[0].groups)
            v_scale, eps_a = (1.0 + EPS, kc("eps2")) if L.n == 0 else (1.0, kc("eps"))
            if L.n == 1:
                nc.scalar.preload_act_table_set("natural_log_exp_and_others")
            for t in STEPS:
                i, i_router = tiles(t, SCORES, ROUTER)
                if i_router is not None:
                    act.wait_ge(s.xo_turned, seen + i_router + 1)
                if i is not None:
                    act.wait_ge(s.xn_turned, seen + i + 1)
                    if i >= 2:
                        act.wait_ge(s.scores, seen + i - 1)
                    if L.n == 0:
                        nc.scalar.activation(xn_t[:, i % 2, :], xn_ps, ACT.Identity, bias=gb[:, 1:2],
                                             scale=gb[:, 0:1]).then_inc(s.xn_t, 1)
                    else:
                        nc.scalar.copy(xn_t[:, i % 2, :], xn_ps).then_inc(s.xn_t, 1)
                i = i_router
                if i is not None:
                    if i >= 2:
                        act.wait_ge(s.logit, seen + i - 1)
                    nc.scalar.copy(xo_t[:, i % 2, :], xo_ps).then_inc(s.xo_t, 1)
                i, = tiles(t, VALUES)
                if i is not None:
                    if i >= 1:
                        act.wait_ge(s.pv, seen + i)
                    for g, group in enumerate(L.groups):
                        act.wait_ge(s.turned, seen_groups + i * len(L.groups) + g + 1)
                        for run in full_and_rest(group, L.chunks):
                            size, k = L.chunks[run[0]][1], run[0] - group[0]
                            last = nc.scalar.copy(
                                probs_t[0:size, run[0]:run[-1] + 1, :],
                                ps[0:size, 4 + g % 2, k * P:(k + len(run)) * P].rearrange("p (c n) -> p c n", n=P))
                        last.then_inc(s.probs_t, 1)
                i_a, i_b = tiles(t, RSTD_A, RSTD_B)
                if i_a is not None:
                    act.wait_ge(s.mv_a, seen + i_a + 1)
                    nc.scalar.activation(rs[:, i_a % 4, 0:1], mv[:, i_a % 4, 1:2], ACT.Ln, bias=eps_a,
                                         scale=v_scale).then_inc(s.ln_a, 1)
                if i_b is not None:
                    act.wait_ge(s.mv_b, seen + i_b + 1)
                    nc.scalar.activation(rs[:, 4 + i_b % 4, 0:1], mv[:, 4 + i_b % 4, 1:2], ACT.Ln,
                                         bias=kc("eps")).then_inc(s.ln_b, 1)
                if i_a is not None:
                    act.wait_ge(s.ln_a, seen + i_a + 1)
                    nc.scalar.activation(rs[:, i_a % 4, 1:2], rs[:, i_a % 4, 0:1], ACT.Exp,
                                         scale=-0.5).then_inc(s.rs_a, 1)
                if i_b is not None:
                    act.wait_ge(s.ln_b, seen + i_b + 1)
                    nc.scalar.activation(rs[:, 4 + i_b % 4, 1:2], rs[:, 4 + i_b % 4, 0:1], ACT.Exp,
                                         scale=-0.5).then_inc(s.rs_b, 1)
                part = t - 1 - FIRST_PART
                if L.n == 0 and 0 <= part < PARTS_EARLY:
                    act_part(act, part)
                i, = tiles(t, SOFTMAX)
                if i is not None:
                    act.wait_ge(s.sub_pair, seen + i + 1)
                    if L.n == 1:
                        act.wait_ge(s.sub_rest, i + 1)
                    if i >= 2:
                        act.wait_ge(s.turned, seen_groups + (i - 1) * len(L.groups))
                    nc.scalar.activation(expd[i % 2][:, 0:L.cols], sub[:, 0:L.cols], ACT.Exp,
                                         scale=L.scale).then_inc(s.exp, 1)

        def stored(s):
            return s.stored0, s.stored1, s.stored2, s.stored3

        def pool_attention(pool, layer):
            s, L = att, layer
            seen = L.n * NT
            src = res if L.n == 0 else base
            for t in STEPS:
                i, = tiles(t, NORM_A)
                if i is not None:
                    pool.wait_ge(s.rs_a, seen + i + 1)
                    if i >= 2:
                        pool.wait_ge(s.xn_turned, seen + i - 1)
                    nc.gpsimd.tensor_scalar(xn[:, i % 2, :], src[:, i, :], mv[:, i % 4, 0:1], rs[:, i % 4, 1:2],
                                            ALU.subtract, ALU.mult).then_inc(s.xn, 1)
                i, = tiles(t, NORM_B)
                if i is not None:
                    pool.wait_ge(s.rs_b, seen + i + 1)
                    if i >= RING:
                        pool.wait_ge(s.xo_turned, seen + i - RING + 1)
                        pool.wait_ge(stored(s)[i % RING], (seen + i) // RING * 16)
                    nc.gpsimd.tensor_scalar(xo[:, i % RING, :], res[:, i, :], mv[:, 4 + i % 4, 0:1],
                                            rs[:, 4 + i % 4, 1:2], ALU.subtract, ALU.mult).then_inc(s.xo, 1)
                i, = tiles(t, SUMS)
                if i is not None:
                    pool.wait_ge(s.rec, seen + i + 1)
                    e = expd[i % 2][:, 0:L.cols].rearrange("p (h k) -> p h k", k=NKEY)
                    nc.gpsimd.tensor_tensor(e, e, spread(rec[:, i % 2, 1, 0:L.heads], [P, L.heads, NKEY], 2),
                                            ALU.mult).then_inc(s.probs, 1)

        def pe_attention(pe, layer):
            s, L = att, layer
            seen = L.n * NT
            G, per = len(L.groups), len(L.chunks)
            seen_groups = L.n * NT * len(LAYERS[0].groups)
            turned_in = {}
            for t in STEPS:
                i, i_router = tiles(t, SCORES, ROUTER)
                before, router_before = tiles(t - 1, SCORES, ROUTER)
                if before is not None:
                    pe.wait_ge(s.xn_t, seen + before + 1)
                if router_before is not None:
                    pe.wait_ge(s.xo_t, seen + router_before + 1)
                if i is not None:
                    pe.wait_ge(s.xn, seen + i + 1)
                    nc.tensor.transpose(xn_ps, xn[:, i % 2, :], ident).then_inc(s.xn_turned, 1)
                if i_router is not None:
                    pe.wait_ge(s.xo, seen + i_router + 1)
                    nc.tensor.transpose(xo_ps, xo[:, i_router % RING, :], ident).then_inc(s.xo_turned, 1)
                i, = tiles(t, VALUES)
                if i is not None:
                    pe.wait_ge(s.probs, seen + i + 1)
                    for g, group in enumerate(L.groups):
                        if g % 2 in turned_in:
                            pe.wait_ge(s.probs_t, seen_groups + turned_in[g % 2] + 1)
                        turned_in[g % 2] = i * G + g
                        for k, c in enumerate(group):
                            a, size = L.chunks[c]
                            last = nc.tensor.transpose(ps[0:size, 4 + g % 2, k * P:(k + 1) * P],
                                                       expd[i % 2][:, a:a + size], ident)
                        last.then_inc(s.turned, 1)
                i, = tiles(t, SCORES)
                if i is not None:
                    pe.wait_ge(s.xn_t, seen + i + 1)
                    if L.n == 1 and i >= 2:
                        pe.wait_ge(s.sub_rest, i - 1)
                    for bank, h, hn in score_banks(L, i):
                        if bank == 0 and i >= 1:
                            pe.wait_ge(s.sub_pair, seen + i)
                        dst = ps[:, bank, 0:hn * NKEY]
                        if L.n == 1:
                            nc.tensor.matmul(dst, kcb("ones", 1),
                                             spread(drop[0:1, i // TPB, :], [1, hn, NKEY], 1),
                                             start=True, stop=False)
                        last = nc.tensor.matmul(dst, xn_t[:, i % 2, :],
                                                score_mat[L.n][:, i // TPB, h * NKEY:(h + hn) * NKEY],
                                                start=(L.n == 0), stop=True)
                    last.then_inc(s.scores, 1)
                i, i_router = tiles(t, VALUES, ROUTER)
                before, router_before = tiles(t - 1, VALUES, ROUTER)
                if before is not None:
                    pe.wait_ge(s.res, seen + before + 1)
                if router_before is not None:
                    pe.wait_ge(s.logit_out, seen + router_before + 1)
                if i_router is not None:
                    pe.wait_ge(s.xo_t, seen + i_router + 1)
                    nc.tensor.matmul(logit_ps, xo_t[:, i_router % 2, :], rw[:, L.n, :], start=True,
                                     stop=True).then_inc(s.logit, 1)
                if i is not None:
                    for g, group in enumerate(L.groups):
                        pe.wait_ge(s.probs_t, seen_groups + i * G + g + 1)
                        for c in group:
                            size = L.chunks[c][1]
                            last = nc.tensor.matmul(pv_ps, probs_t[0:size, c, :],
                                                    value_mat[L.n][0:size, i // TPB * per + c, :],
                                                    start=(c == 0), stop=(c == per - 1))
                    last.then_inc(s.pv, 1)
                part = t - FIRST_PART
                if L.n == 0 and 0 <= part < PARTS_EARLY:
                    pe_part(pe, part)

        def sp_attention(sp, layer):
            s, seen = att, layer.n * NT
            for i in range(NT):
                sp.wait_ge(s.xo, seen + i + 1)
                sp.dma_start(xn_tiles[:, i, :], xo[:, i % RING, :]).then_inc(stored(s)[i % RING], 16)

        def dve_route(dve, layer):
            r, L, K, NS = rout[layer.n], layer, layer.choices, layer.slots
            done = [0]

            def link(ins):
                done[0] += 1
                ins.then_inc(r.dve, 1)
                dve.wait_ge(r.dve, done[0])

            def col(c, shape=(P, NT, E)):
                return spread(rcol[:, c, :], list(shape), 2)

            dve.wait_ge(att.logit_out, (L.n + 1) * NT)
            rank = spread(kc("expert_rank"), [P, NT, E], 1)
            cand = logits
            for k in range(K):
                link(nc.vector.tensor_reduce(rcol[:, 2 * k, :], cand[:, :, :], AX.X, ALU.max))
                link(nc.vector.tensor_tensor(rt[:, 0], cand[:, :, :], col(2 * k), ALU.is_equal))
                link(nc.vector.tensor_tensor(rt[:, 0], rt[:, 0], rank, ALU.mult))
                link(nc.vector.tensor_reduce(rcol[:, 1, :], rt[:, 0], AX.X, ALU.max))
                link(nc.vector.tensor_tensor(pick[:, k], rt[:, 0], col(1), ALU.is_equal))
                if k + 1 < K:
                    link(nc.vector.scalar_tensor_tensor(rt[:, 1], pick[:, k], -BIG, logits[:, :, :],
                                                        ALU.mult, ALU.add))
                    cand = rt[:, 1]
            if K == 1:
                nc.vector.tensor_copy(pick_b[:, :, :], pick[:, 0]).then_inc(r.picked, 1)
            else:
                nc.vector.tensor_tensor(pick_b[:, :, :], pick[:, 0], pick[:, 1], ALU.add).then_inc(r.picked, 1)
            if K == 1:
                nc.vector.tensor_tensor(rt[:, 2], logits[:, :, :], col(0), ALU.subtract).then_inc(r.gap, 1)
            else:
                nc.vector.tensor_tensor(rcol[:, 4, :], rcol[:, 2, :], rcol[:, 0, :], ALU.subtract).then_inc(r.gap, 1)
            dve.wait_ge(r.totals, 1)
            nc.vector.tensor_copy(totals[:, :], ps[:, 6, 0:P]).then_inc(r.totals, 1)
            dve.wait_ge(r.counts, 1)
            link(nc.vector.tensor_scalar(nblk[0:E, 0:NT], kc("slot_edges", E), ps[0:E, 7, 0:1], None, ALU.is_lt))
            link(nc.vector.tensor_reduce(nblk[0:E, NT:NT + 1], nblk[0:E, 0:NT], AX.X, ALU.add))
            nc.vector.tensor_scalar(nblk_b[0:E, :], kc("ones", E), nblk[0:E, NT:NT + 1], None,
                                    ALU.mult).then_inc(r.blocks, 1)
            dve.wait_ge(r.positions, 1)
            for k in range(K):
                link(nc.vector.tensor_tensor(rt[:, 0], ps[:, 5, 0:P].rearrange("p (t e) -> p t e", e=E),
                                             pick[:, k], ALU.mult))
                link(nc.vector.tensor_reduce(pos_f[:, 0, k * NT:(k + 1) * NT], rt[:, 0], AX.X, ALU.add))
            n = K * NT
            link(nc.vector.tensor_copy(pos_i[:, 0, 0:n], pos_f[:, 0, 0:n]))
            link(nc.vector.tensor_scalar(pos_i[:, 1, 0:n], pos_i[:, 0, 0:n], 7, None, ALU.logical_shift_right))
            link(nc.vector.tensor_scalar(pos_i[:, 2, 0:n], pos_i[:, 0, 0:n], P - 1, None, ALU.bitwise_and))
            link(nc.vector.tensor_copy(pos_f[:, 1:3, 0:n], pos_i[:, 1:3, 0:n]))
            hit = slot_rhs[:, 0:n, 2, 0:NS]
            link(nc.vector.tensor_tensor(hit, spread(kc("slot_number")[:, 0:NS], [P, n, NS], 1),
                                         spread(pos_f[:, 1, 0:n], [P, n, NS], 2), ALU.is_equal))
            link(nc.vector.tensor_scalar(slot_rhs[:, 0:n, 0, 0:NS], hit, kc("partition"), None, ALU.mult))
            link(nc.vector.tensor_tensor(slot_rhs[:, 0:n, 1, 0:NS], hit,
                                         spread(kc("tile_number")[:, 0:n], [P, n, NS], 2), ALU.mult))
            for m in range(n):
                if m >= 4:
                    dve.wait_ge(r.ids, m - 3)
                nc.vector.tensor_scalar(at_row[:, m % 4, :], kcb("row_number"), pos_f[:, 2, m:m + 1], None,
                                        ALU.is_equal).then_inc(r.at_row, 1)
            link(nc.vector.tensor_copy(cums[:, :], ps[0:1, 1, 0:E]))
            link(nc.vector.tensor_tensor(exp_cmp[:, 0:NS, :], spread(cums[:, :], [1, NS, E], 1),
                                         spread(kc("slot_number", 1)[:, 0:NS], [1, NS, E], 2), ALU.is_le))
            link(nc.vector.tensor_reduce(exp_f[:, 0:NS], exp_cmp[:, 0:NS, :], AX.X, ALU.add))
            link(nc.vector.tensor_scalar(exp_i[:, PAD:PAD + NS], exp_f[:, 0:NS], E - 1.0, None, ALU.min))
            dve.wait_ge(r.ids, n)
            link(nc.vector.tensor_copy(ids_f[:, 0:3, 0:NS],
                                       ps[:, 4, 0:3 * NS].rearrange("p (c s) -> p c s", c=3)))
            link(nc.vector.scalar_tensor_tensor(ids_f[:, 3, 0:NS], ids_f[:, 1, 0:NS], float(P), ids_f[:, 0, 0:NS],
                                                ALU.mult, ALU.add))
            link(nc.vector.tensor_scalar(ids_f[:, 4, 0:NS], ids_f[:, 2, 0:NS], -1.0, 1.0, ALU.mult, ALU.add))
            link(nc.vector.tensor_tensor(ids_f[:, 4, 0:NS], ids_f[:, 4, 0:NS], kc("pad_rows")[:, 0:NS], ALU.mult))
            link(nc.vector.tensor_tensor(ids_put[:, 0:NS], ids_f[:, 3, 0:NS], ids_f[:, 4, 0:NS], ALU.add))
            nc.vector.tensor_scalar(ids_get[:, 0:NS], ids_put[:, 0:NS], B * S - 1, None,
                                    ALU.bitwise_and).then_inc(r.tables, 1)
            gate = gate_t[:, 2 + L.n:3 + L.n]
            dve.wait_ge(r.expd, 1)
            if K == 1:
                link(nc.vector.tensor_reduce(rcol[:, 5, :], rt[:, 2], AX.X, ALU.add))
                link(nc.vector.reciprocal(rcol[:, 6, :], rcol[:, 5, :]))
            else:
                link(nc.vector.tensor_scalar(rcol[:, 5, :], rcol[:, 7, :], 1.0, None, ALU.add))
                link(nc.vector.reciprocal(rcol[:, 6, :], rcol[:, 5, :]))
            link(nc.vector.tensor_scalar(coef[:, 0, :], rcol[:, 6, :], gate, None, ALU.mult))
            if K == 2:
                link(nc.vector.tensor_tensor(coef[:, 1, :], coef[:, 0, :], rcol[:, 7, :], ALU.mult))

        def act_route(act, layer):
            r = rout[layer.n]
            if layer.n == 0:
                for part in range(PARTS_EARLY, PARTS_PICK):
                    act_part(act, part)
            act.wait_ge(r.gap, 1)
            if layer.choices == 1:
                nc.scalar.activation(rt[:, 2], rt[:, 2], ACT.Exp).then_inc(r.expd, 1)
            else:
                nc.scalar.activation(rcol[:, 7, :], rcol[:, 4, :], ACT.Exp).then_inc(r.expd, 1)
            if layer.n == 0:
                for part in range(PARTS_PICK, N_PARTS):
                    act_part(act, part)

        def pe_route(pe, layer):
            r, n, NS = rout[layer.n], layer.choices * NT, layer.slots
            flat = pick_b[:, :, :].rearrange("p t e -> p (t e)")
            if layer.n == 0:
                for part in range(PARTS_EARLY, PARTS_PICK):
                    pe_part(pe, part)
            pe.wait_ge(r.picked, 1)
            nc.tensor.matmul(ps[:, 5, 0:P], kcb("before"), flat, start=True, stop=False)
            nc.tensor.matmul(ps[:, 6, 0:P], flat, kcb("ones"), start=True, stop=True).then_inc(r.totals, 1)
            pe.wait_ge(r.totals, 2)
            nc.tensor.matmul(ps[0:E, 7, 0:P], kcb("same_expert"), totals[:, :], start=True,
                             stop=True).then_inc(r.counts, 1)
            nc.tensor.matmul(ps[:, 5, 0:P], totals[:, :], kcb("earlier_tile"), start=False, stop=False)
            pe.wait_ge(r.blocks, 1)
            nc.tensor.matmul(ps[:, 1, 0:E], nblk_b[0:E, :], kcb("upto_expert", E), start=True, stop=True)
            nc.tensor.matmul(ps[:, 5, 0:P], nblk_b[0:E, :], kcb("lower_expert", E), start=False,
                             stop=True).then_inc(r.positions, 1)
            if layer.n == 0:
                for part in range(PARTS_PICK, N_PARTS):
                    pe_part(pe, part)
            for m in range(n):
                pe.wait_ge(r.at_row, m + 1)
                nc.tensor.matmul(ps[:, 4, 0:3 * NS], at_row[:, m % 4, :], slot_rhs[:, m, :, 0:NS],
                                 start=(m == 0), stop=(m == n - 1)).then_inc(r.ids, 1)

        def up_banks(layer, q):
            return (q, (2, 7)[q]) if layer.n == 0 else (q,)

        def gathered(f):
            return f.gathered0, f.gathered1, f.gathered2, f.gathered3

        def scattered(f):
            return f.scattered0, f.scattered1, f.scattered2, f.scattered3

        def pool_experts(pool, layer):
            f, NS = ffn[layer.n], layer.slots
            pool.wait_ge(rout[layer.n].tables, 1)
            for buffer_stored in stored(att):
                pool.wait_ge(buffer_stored, 16 * (NT // RING) * (layer.n + 1))
            for t in range(NS + 7):
                if t < NS:
                    if t >= RING:
                        pool.wait_ge(f.turned, t - RING + 1)
                    pool.indirect_dma_start(
                        xg[:, t % RING, :], None, xn_dram,
                        bass.IndirectOffsetOnAxis(ap=ids_get[:, t:t + 1].bitcast(U32), axis=0)
                    ).then_inc(gathered(f)[t % RING], 16)
                if t >= 7:
                    j = t - 7
                    pool.wait_ge(f.y, j + 1)
                    pool.indirect_dma_start(
                        y_dram, bass.IndirectOffsetOnAxis(ap=ids_put[:, j:j + 1].bitcast(U32), axis=0),
                        y_out[:, j % RING, :], None
                    ).then_inc(scattered(f)[j % RING], 16)

        def expert_numbers(eng, first, n):
            return nc.values_load_multi_w_load_instructions(
                exp_i[0:1, ds(first, n)], engines=[eng.engine], min_val=0, max_val=E - 1,
                skip_runtime_bounds_check_because="the table is clamped to 0..E-1 where it is made")[1]

        def pe_experts(pe, layer):
            f, L, NS = ffn[layer.n], layer, layer.slots
            pe.wait_ge(rout[L.n].tables, 1)
            pe.wait_ge((ld.up0, ld.up1)[L.n], 16 * (L.n + 1))
            pe.wait_ge((ld.down0, ld.down1)[L.n], 16)

            def fetch(t):
                return expert_numbers(pe, t, PAD + RING)

            def step(t, par, fetched):
                if live(t, 0, NS):
                    i, q = t, par
                    pe.wait_ge(gathered(f)[q], (i - q) * (16 // RING) + 16)
                    if past(i, 1):
                        pe.wait_ge(f.xg_t, i)
                    nc.tensor.transpose(ps[:, 6, 0:P], xg[:, q, :], ident).then_inc(f.turned, 1)
                if live(t, 3, NS):
                    i, q = t - 3, (par - 3) % 2
                    pe.wait_ge(f.hid, i + 1)
                    if past(i, 2):
                        pe.wait_ge(f.hid_t, i - 1)
                    for c in range(4):
                        last = nc.tensor.transpose(ps[:, 3 + q, c * P:(c + 1) * P],
                                                   hid[:, q, c * P:(c + 1) * P], ident)
                    last.then_inc(f.hid_turned, 1)
                if live(t, 1, NS):
                    i, q = t - 1, (par - 1) % 2
                    e = fetched[PAD - 1 + par]
                    pe.wait_ge(f.xg_t, i + 1)
                    if past(i, 2):
                        pe.wait_ge(f.hid if L.n == 0 else f.biased, i - 1)
                    for k, bank in enumerate(up_banks(L, q)):
                        last = nc.tensor.matmul(ps[:, bank, :], xg_t[:, q, :],
                                                w_up[L.n][:, ds(e, 1), k * FFN:(k + 1) * FFN], start=True, stop=True)
                    last.then_inc(f.up, 1)
                if live(t, 3, NS):
                    i, q = t - 3, (par - 3) % 2
                    e = fetched[par]
                    pe.wait_ge(f.hid_t, i + 1)
                    if past(i, 1):
                        pe.wait_ge(f.y, i)
                    for c in range(4):
                        last = nc.tensor.matmul(ps[:, 5, 0:D], hid_t[:, q, c, :], w_down[:, ds(e, 1), c, :],
                                                start=(c == 0), stop=(c == 3))
                    last.then_inc(f.down, 1)

            pipeline(pe, NS, 3, step, fetch)

        def act_experts(act, layer):
            f, L, NS = ffn[layer.n], layer, layer.slots
            lag = 1 if L.n == 0 else 2

            def step(t, par, fetched):
                if live(t, 0, NS):
                    i, q = t, par % 2
                    act.wait_ge(f.turned, i + 1)
                    if past(i, 2):
                        act.wait_ge(f.up, i - 1)
                    nc.scalar.copy(xg_t[:, q, :], ps[:, 6, 0:P]).then_inc(f.xg_t, 1)
                if live(t, 3, NS):
                    i, q = t - 3, (par - 3) % 2
                    act.wait_ge(f.hid_turned, i + 1)
                    if past(i, 2):
                        act.wait_ge(f.down, i - 1)
                    nc.scalar.copy(hid_t[:, q], ps[:, 3 + q, :].rearrange("p (c n) -> p c n", c=4)).then_inc(f.hid_t, 1)
                if live(t, lag, NS):
                    i, q = t - lag, (par - lag) % 2
                    if L.n == 0:
                        act.wait_ge(f.up, i + 1)
                        if past(i, 2):
                            act.wait_ge(f.hid, i - 1)
                        nc.scalar.activation(act_a[:, q, :], ps[:, up_banks(L, q)[0], :], ACT.Silu).then_inc(f.act, 1)
                    else:
                        act.wait_ge(f.biased, i + 1)
                        if past(i, 2):
                            act.wait_ge(f.hid_turned, i - 1)
                        nc.scalar.activation(hid[:, q, :], act_a[:, q, :], ACT.Gelu).then_inc(f.hid, 1)

            pipeline(act, NS, 3, step)

        def dve_experts(dve, layer):
            f, L, NS = ffn[layer.n], layer, layer.slots
            dve.wait_ge(rout[L.n].tables, 1)
            if L.n == 1:
                dve.wait_ge(ld.up1, 32)
                dve.wait_ge(ld.small, 16 * N_SMALL)

            def fetch(t):
                return expert_numbers(dve, t, PAD + RING)

            def step(t, par, fetched):
                if live(t, 1, NS):
                    i, q = t - 1, (par - 1) % 2
                    dve.wait_ge(f.up, i + 1)
                    if L.n == 0:
                        dve.wait_ge(f.act, i + 1)
                        if past(i, 2):
                            dve.wait_ge(f.hid_turned, i - 1)
                        nc.vector.tensor_tensor(hid[:, q, :], ps[:, up_banks(L, q)[1], :], act_a[:, q, :],
                                                ALU.mult).then_inc(f.hid, 1)
                    else:
                        e = fetched[PAD - 1 + par]
                        if past(i, 2):
                            dve.wait_ge(f.hid, i - 1)
                        nc.vector.tensor_tensor(act_a[:, q, :], ps[:, q, :], b_up[:, ds(e, 1), :],
                                                ALU.add).then_inc(f.biased, 1)
                if live(t, 3, NS):
                    i, q = t - 3, (par - 3) % RING
                    dve.wait_ge(f.down, i + 1)
                    if past(i, RING):
                        dve.wait_ge(scattered(f)[q], (i - q) * (16 // RING))
                    if L.n == 0:
                        nc.vector.tensor_copy(y_out[:, q, :], ps[:, 5, 0:D]).then_inc(f.y, 1)
                    else:
                        nc.vector.tensor_tensor(y_out[:, q, :], ps[:, 5, 0:D], b_down[:, ds(fetched[par], 1), :],
                                                ALU.add).then_inc(f.y, 1)

            pipeline(dve, NS, 3, step, fetch if L.n == 1 else None)

        def wait_scattered(eng, layer):
            f, NS = ffn[layer.n], layer.slots
            for k in range(RING):
                eng.wait_ge(scattered(f)[k], 16 * len(range(k, NS, RING)))

        block = stack.enter_context(nc.Block())

        @block.sync
        def _(sp):
            sp.dma_start(ctx_sb[:, 0:2, :], ctx_rows[0:2 * P, :].rearrange("(t p) d -> p t d", p=P)).then_inc(ld.ctx, 16)
            sp.dma_start(ctx_sb[0:CTX - 2 * P, 2, :], ctx_rows[2 * P:CTX, :]).then_inc(ld.ctx, 16)
            for dst, src in ((gate_in[:, 0:2], g_xattn.to_broadcast([P, 2])), (gate_in[:, 2:4], g_ffn.to_broadcast([P, 2])),
                             (gb[:, :], ln_gb)):
                sp.dma_start(dst, src).then_inc(ld.gates, 16)
            sp.dma_start(k_sb[:, :], const).then_inc(ld.const, 16)
            sp.dma_start(wkv0_sb[:, :], wkv0).then_inc(ld.w0, 16)
            sp.dma_start(c_t[:, :], ctx_cols).then_inc(ld.w1, 16)
            sp.dma_start(wqkvo1_sb[:, :, :], wqkvo1).then_inc(ld.w1, 16)
            sp.dma_start(wq0_sb[:, :, :], wq0.rearrange("(c p) d -> p c d", p=P)).then_inc(ld.w0, 16)
            sp.dma_start(wout0_sb[:, :, :], wout0.rearrange("(c p) d -> p c d", p=P)).then_inc(ld.w0, 16)
            sp.dma_start(res[:, :, :], x_tiles).then_inc(ld.x, 16)
            small = ((bout_b[:, :], out_bias.to_broadcast([P, D])),
                     (vlen_i[:, :], valid_len.to_broadcast([P, B])), (rw[:, 0, :], rw0), (rw[:, 1, :], rw1),
                     (rb[:, 0, :], rb0.to_broadcast([P, E])), (rb[:, 1, :], rb1.to_broadcast([P, E])),
                     (b_down[:, :, :], b2_1.to_broadcast([P, E, D])))
            assert len(small) == N_SMALL
            for dst, src in small:
                sp.dma_start(dst, src).then_inc(ld.small, 16)
            sp.dma_start(w_up[0], w1_0.rearrange("e d f -> d e f")).then_inc(ld.up0, 16)
            sp.dma_start(w_down[:, :, :, :], w2_0.rearrange("e (c p) d -> p e c d", p=P)).then_inc(ld.down0, 16)
            sp_attention(sp, LAYERS[0])
            wait_scattered(sp, LAYERS[0])
            for b, landed in enumerate((att.y0, att.y1, att.y2, att.y3)):
                t = slice(b * TPB, (b + 1) * TPB)
                sp.dma_start(base[:, t, :], y_tiles[:, t, :]).then_inc(landed, 16)
            sp.wait_ge(ffn[0].up, LAYERS[0].slots)
            sp.wait_ge(ffn[0].down, LAYERS[0].slots)
            sp.dma_start(w_up[1], w1_1.rearrange("e d f -> d e f")).then_inc(ld.up1, 16)
            sp.dma_start(b_up, b1_1.to_broadcast([P, E, FFN])).then_inc(ld.up1, 16)
            sp.dma_start(w_down[:, :, :, :], w2_1.rearrange("e (c p) d -> p e c d", p=P)).then_inc(ld.down1, 16)
            sp_attention(sp, LAYERS[1])
            wait_scattered(sp, LAYERS[1])
            sp.wait_ge(ffn[1].up, LAYERS[1].slots)
            for b, landed in enumerate((att.y0, att.y1, att.y2, att.y3)):
                t = slice(b * TPB, (b + 1) * TPB)
                sp.dma_start(base[:, t, :], y_tiles[:, t, :]).then_inc(landed, 16)
                sp.dma_start(y_second[:, t, :], y_tiles[:, NT + b * TPB:NT + (b + 1) * TPB, :]).then_inc(landed, 16)
            for b in range(B):
                t = slice(b * TPB, (b + 1) * TPB)
                sp.wait_ge(fin.done, (b + 1) * TPB)
                sp.dma_start(out_tiles[:, t, :], res[:, t, :]).then_inc(fin.stored, 16)
            sp.wait_ge(fin.stored, 16 * B)

        @block.gpsimd
        def _(pool):
            pool.wait_ge(ld.small, 16 * N_SMALL)
            pool.wait_ge(init.gates, 1)
            nc.gpsimd.tensor_scalar(bout_g[:, :], bout_b[:, :], gate_t[:, 0:1], None, ALU.mult
                                    ).then_inc(init.base_bias, 1)
            pool.wait_ge(ld.x, 16)
            pool.wait_ge(init.base_bias, 1)
            nc.gpsimd.tensor_tensor(base[:, :, :], res[:, :, :], spread(bout_g[:, :], [P, NT, D], 1),
                                    ALU.add).then_inc(init.base, 1)
            pool_blocks(pool)
            for layer in LAYERS:
                pool_attention(pool, layer)
                pool_experts(pool, layer)

        @block.scalar
        def _(act):
            p = prep
            act.wait_ge(ld.gates, 48)
            nc.scalar.activation(gate_t[:, :], gate_in[:, :], ACT.Tanh).then_inc(init.gates, 1)
            nc.scalar.preload_act_table_set("natural_log_exp_and_others")
            act.wait_ge(p.mv, 3)
            act.wait_ge(ld.const, 16)
            nc.scalar.activation(ctx_rs[:, :, 0:1], ctx_mv[:, :, 1:2], ACT.Ln, bias=kc("eps")).then_inc(p.ln, 1)
            act.wait_ge(p.ln, 1)
            nc.scalar.activation(ctx_rs[:, :, 1:2], ctx_rs[:, :, 0:1], ACT.Exp, scale=-0.5).then_inc(p.rs, 1)
            act.wait_ge(p.cn_turned, 1)
            nc.scalar.activation(cn_t[:, :], ps[:, 6, 0:CTX], ACT.Identity, bias=gb[:, 3:4],
                                 scale=gb[:, 2:3]).then_inc(p.cn_t, 1)
            act.wait_ge(init.gates, 1)
            copy_products(act, 0)
            copy_turned(act, nc.scalar.copy, 1, p.turned_act)
            for layer in LAYERS:
                act_attention(act, layer)
                act_route(act, layer)
                act_experts(act, layer)

        @block.tensor
        def _(pe):
            p = prep
            pe.wait_ge(ld.const, 16)
            pe.wait_ge(p.cn, 3)
            for k in range(3):
                rows = min(P, CTX - k * P)
                last = nc.tensor.transpose(ps[:, 6, k * P:k * P + rows], ctx_n[0:rows, k, :], ident[0:rows, 0:rows])
            last.then_inc(p.cn_turned, 1)
            pe.wait_ge(ld.w0, 48)
            pe.wait_ge(p.cn_t, 1)
            pe_products(pe)
            pe.wait_ge(p.turned_act, 2 * (B // 2))
            pe.wait_ge(p.turned_dve, 2 * (B // 2))
            pe.wait_ge(ld.small, 16 * N_SMALL)
            pe.wait_ge(init.constb, 1)
            pe.wait_ge(init.drop, 1)
            for layer in LAYERS:
                pe_attention(pe, layer)
                pe_route(pe, layer)
                pe_experts(pe, layer)

        @block.vector
        def _(dve):
            p = prep
            nc.vector.memset(ctx_mv[:, :, :], 1.0).then_inc(init.neg, 1)
            nc.vector.memset(exp_i[:, :], 0).then_inc(init.experts, 1)
            dve.wait_ge(init.neg, 1)
            dve.wait_ge(ld.ctx, 32)
            for k in range(3):
                rows = min(P, CTX - k * P)
                nc.vector.bn_stats(ctx_st[0:rows, k, :], ctx_sb[0:rows, k, :]).then_inc(p.stats, 1)
                dve.wait_ge(p.stats, k + 1)
                nc.vector.bn_aggr(ctx_mv[0:rows, k, :], ctx_st[0:rows, k, :]).then_inc(p.mv, 1)
            dve.wait_ge(p.rs, 1)
            for k in range(3):
                rows = min(P, CTX - k * P)
                nc.vector.tensor_scalar(ctx_n[0:rows, k, :], ctx_sb[0:rows, k, :], ctx_mv[0:rows, k, 0:1],
                                        ctx_rs[0:rows, k, 1:2], ALU.subtract, ALU.mult).then_inc(p.cn, 1)
            dve.wait_ge(init.gates, 1)
            copy_products(dve, 1)
            copy_turned(dve, nc.vector.tensor_copy, 0, p.turned_dve)
            dve.wait_ge(ld.small, 16 * N_SMALL)
            nc.vector.tensor_copy(vlen[:, :], vlen_i[:, :]).then_inc(init.vlen, 1)
            dve.wait_ge(ld.const, 16)
            nc.vector.tensor_copy(kb_sb[:, :], k_sb[:, :]).then_inc(init.constb, 1)
            dve.wait_ge(init.vlen, 1)
            nc.vector.tensor_tensor(keep[:, :, :], spread(kc("key_number"), [P, B, NKEY], 1),
                                    spread(vlen[:, :], [P, B, NKEY], 2), ALU.is_le).then_inc(init.keep, 1)
            dve.wait_ge(init.keep, 1)
            nc.vector.tensor_scalar(drop[:, :, :], keep[:, :, :], -1.0, -NEG / LAYERS[1].scale,
                                    ALU.add, ALU.mult).then_inc(init.drop, 1)
            wait_copied(dve, 8)
            nc.vector.tensor_tensor(kv1_t[:, 0, :], kv1_t[:, 0, :], keep[:, :, :].rearrange("p b k -> p (b k)"),
                                    ALU.mult).then_inc(blk.kept, 1)
            dve.wait_ge(ld.x, 16)
            for layer in LAYERS:
                dve_attention(dve, layer)
                dve_route(dve, layer)
                dve_experts(dve, layer)
            for t in range(NT):
                a = att
                dve.wait_ge((a.y0, a.y1, a.y2, a.y3)[t // TPB], 48)
                nc.vector.scalar_tensor_tensor(base[:, t, :], base[:, t, :], coef[:, 0, t:t + 1], res[:, t, :],
                                               ALU.mult, ALU.add).then_inc(fin.half, 1)
                dve.wait_ge(fin.half, t + 1)
                nc.vector.scalar_tensor_tensor(res[:, t, :], y_second[:, t, :], coef[:, 1, t:t + 1], base[:, t, :],
                                               ALU.mult, ALU.add).then_inc(fin.done, 1)


def constants():
    import numpy as np

    k = np.zeros((P, NCONST), np.float32)

    def put(name, values):
        a, n = CONST_COLS[name]
        values = np.asarray(values, np.float32)
        k[:values.shape[0], a:a + n] = values

    p, t, e = np.arange(P), np.arange(P) // E, np.arange(P) % E
    put("ident", np.eye(P))
    put("ones", np.ones((P, P)))
    put("before", p[:, None] < p[None, :])
    put("earlier_tile", (e[:, None] == e[None, :]) & (t[:, None] < t[None, :]))
    put("same_expert", e[:, None] == np.arange(E)[None, :])
    put("lower_expert", P * (np.arange(E)[:, None] < e[None, :]))
    put("upto_expert", np.arange(E)[:, None] <= np.arange(E)[None, :])
    put("row_number", np.tile(p, (P, 1)))
    put("slot_number", np.tile(np.arange(MAXSLOTS), (P, 1)))
    put("partition", p[:, None])
    put("tile_number", np.tile(np.arange(2 * NT), (P, 1)))
    put("expert_rank", np.tile(E - np.arange(E), (P, 1)))
    put("head_rows", p[:, None] // HD1 == np.arange(H1)[None, :])
    put("slot_edges", np.tile(P * np.arange(NT), (P, 1)))
    put("key_number", np.tile(1 + np.arange(NKEY), (P, 1)))
    put("pad_rows", 2 * B * S + P * np.arange(MAXSLOTS)[None, :] + p[:, None])
    put("eps", np.full((P, 1), EPS))
    put("eps2", np.full((P, 1), EPS * EPS))
    return k


def kernel(**inputs):
    import numpy as np
    import concourse.bacc as bacc
    from concourse.bass_utils import run_bass_kernel_spmd

    a = {n: np.asarray(v) for n, v in inputs.items()}
    ctx = a["ctx_1024"].reshape(CTX, D)
    by_head = a["L1_xattn_Wq"].transpose(0, 2, 1).reshape(D, D)
    wqkvo1 = np.stack([by_head, a["L1_xattn_Wk"].transpose(1, 0, 2).reshape(D, D),
                       a["L1_xattn_Wv"].transpose(1, 0, 2).reshape(D, D), a["L1_xattn_Wo"]], axis=1)
    arrays = {
        "x": a["x"].reshape(B * S, D),
        "ctx_rows": ctx,
        "ctx_cols": ctx.T,
        "valid_len": a["mask_B_ik0"][None, :],
        "g_xattn": a["g_xattn"][None, :],
        "g_ffn": a["g_ffn"][None, :],
        "ln_gb": np.stack([a["L0_xattn_g1"], a["L0_xattn_b1"], a["L0_xattn_g2"], a["L0_xattn_b2"]], axis=1),
        "out_bias": a["L0_xattn_bout"][None, :],
        "wq0": a["L0_xattn_Wq"].T,
        "wkv0": a["L0_xattn_Wkv"],
        "wout0": a["L0_xattn_Wout"],
        "rw0": a["L0_ffn_router_w"],
        "rb0": a["L0_ffn_router_b"][None, :],
        "w1_0": a["L0_ffn_w1"],
        "w2_0": a["L0_ffn_w2"],
        "wqkvo1": wqkvo1,
        "w1_1": a["L1_ffn_W1"],
        "b1_1": a["L1_ffn_b1"][None, :, :],
        "w2_1": a["L1_ffn_W2"],
        "b2_1": a["L1_ffn_b2"][None, :, :],
        "rw1": a["L1_ffn_Wr"],
        "rb1": a["L1_ffn_br"][None, :],
        "const": constants(),
    }
    arrays = {n: np.ascontiguousarray(v) for n, v in arrays.items()}
    nc = bacc.Bacc("TRN2", target_bir_lowering=False, num_devices=1)
    aps = {n: nc.dram_tensor(f"in_{n}", v.shape, mybir.dt.from_np(v.dtype), kind="ExternalInput").ap()
           for n, v in arrays.items()}
    aps["out"] = nc.dram_tensor("out_dram", (B * S, D), F32, kind="ExternalOutput").ap()
    gated_stack(nc, **aps)
    r = run_bass_kernel_spmd(nc, [{f"in_{n}": v for n, v in arrays.items()}], core_ids=[0])
    return r.results[0]["out_dram"].reshape(B, S, D)
```

```python
from collections import namedtuple
from contextlib import ExitStack

import concourse.bass as bass
from concourse import mybir

P = 128
B, S, D = 4, 512, 128
NKEY = 77
CTX = B * NKEY
NT = B * S // P
TPB = NT // B
E = 8
H0, HD0 = 8, 64
H1, HD1 = 16, 8
FFN = 512
EPS = 1e-5
NEG = -1.0e6
BIG = 1.0e30
PAD = 3
RING = 4

ALU = mybir.AluOpType
ACT = mybir.ActivationFunctionType
AX = mybir.AxisListType
F32 = mybir.dt.float32
BF16 = mybir.dt.bfloat16
I32 = mybir.dt.int32
U32 = mybir.dt.uint32
ds = bass.ds

MAXSLOTS = 2 * NT + E - 1
CONST_COLS = {}
_at = 0
for _name, _n in (("ident", P), ("eps", 1), ("eps2", 1), ("ones", P), ("before", P), ("earlier_tile", P), ("same_expert", E),
                  ("lower_expert", P), ("upto_expert", E), ("row_number", P), ("slot_number", MAXSLOTS),
                  ("row_plus_1", 1), ("tile_number", 2 * NT), ("expert_rank", E), ("head_rows", H1),
                  ("slot_edges", NT), ("key_number", NKEY), ("pad_rows_plus_1", MAXSLOTS)):
    CONST_COLS[_name] = (_at, _n)
    _at += _n
NCONST = _at
FIRST_CONST = P + 2


def live(step, lag, n):
    return not isinstance(step, int) or 0 <= step - lag < n


def past(i, n):
    return not isinstance(i, int) or i >= n


def pipeline(eng, n, depth, body, fetch=None):
    head = -(-(depth + RING) // RING) * RING
    end = n // RING * RING

    def turn(first):
        fetched = fetch(first) if fetch else None
        for k in range(RING):
            if not isinstance(first, int) or first + k < n + depth:
                body(first + k, k, fetched)

    for first in range(0, head, RING):
        turn(first)
    with eng.Fori(head // RING, end // RING) as number:
        turn(number * RING)
    for first in range(end, n + depth, RING):
        turn(first)


def key_chunks(heads):
    cols = heads * NKEY
    chunks = [(a, min(P, cols - a)) for a in range(0, cols, P)]
    return chunks, [list(range(a, min(a + 4, len(chunks)))) for a in range(0, len(chunks), 4)]


def full_and_rest(group, chunks):
    full = [c for c in group if chunks[c][1] == P]
    rest = [c for c in group if chunks[c][1] < P]
    return [r for r in (full, rest) if r]


Layer = namedtuple("Layer", "n heads scale pair choices cols chunks groups slots")


def layer_plan(n, heads, scale, pair, choices):
    return Layer(n, heads, scale, pair, choices, heads * NKEY, *key_chunks(heads), choices * NT + E - 1)


def gated_stack(nc, x, ctx_rows, ctx_cols, valid_len, g_xattn, g_ffn, ln_gb, out_bias, wq0, wkv0, wout0,
                rw0, rb0, w1_0, w2_0, wqkvo1, w1_1, b1_1, w2_1, b2_1, rw1, rb1, const, out):
    with ExitStack() as stack:
        def sb(name, shape, dt=F32):
            return stack.enter_context(nc.sbuf_tensor(name, shape, dt))

        def sem(name):
            return stack.enter_context(nc.semaphore(name))

        def sems(tag, names):
            return namedtuple("Sems", names)(*[sem(f"{n}_{tag}") for n in names.split()])

        ps = stack.enter_context(nc.psum_tensor("ps", [P, 8, 512], F32))
        k_sb = sb("k_sb", [P, NCONST])
        kb_sb = sb("kb_sb", [P, NCONST], BF16)
        res = sb("res", [P, NT, D])
        base = sb("base", [P, NT, D])
        gate_in = sb("gate_in", [P, 4])
        gate_t = sb("gate_t", [P, 4])
        gb = sb("gb", [P, 4])
        bout_b = sb("bout_b", [P, D])
        bout_g = sb("bout_g", [P, D])
        vlen_i = sb("vlen_i", [P, B], I32)
        vlen = sb("vlen", [P, B])
        keep = sb("keep", [P, B, NKEY])
        drop = sb("drop", [P, B, NKEY], BF16)
        ctx_sb = sb("ctx_sb", [P, 3, D])
        ctx_n = sb("ctx_n", [P, 3, D])
        ctx_st = sb("ctx_st", [P, 3, 6])
        ctx_mv = sb("ctx_mv", [P, 3, 2])
        ctx_rs = sb("ctx_rs", [P, 3, 2])
        cn_t = sb("cn_t", [P, CTX])
        c_t = sb("c_t", [P, CTX])
        wq0_sb = sb("wq0_sb", [P, 4, D])
        wkv0_sb = sb("wkv0_sb", [P, 2 * H0 * HD0])
        wout0_sb = sb("wout0_sb", [P, 4, D])
        wqkvo1_sb = sb("wqkvo1_sb", [P, 4, D])
        kv1_t = sb("kv1_t", [P, 2, CTX])
        score_mat = [sb("score_mat0", [P, B, H0 * NKEY]), sb("score_mat1", [P, B, H1 * NKEY])]
        value_mat = [sb("value_mat0", [P, B * 5, D]), sb("value_mat1", [P, B * 10, D])]
        temp = score_mat[1][:, :, :].rearrange("p b c -> p (b c)")
        kv_t = temp[:, 0:8 * CTX].rearrange("p (c n) -> p c n", c=8)
        vw_t = temp[:, 8 * CTX:8 * CTX + B * H0 * NKEY].rearrange("p (b c) -> p b c", b=B)
        shared = sb("shared", [P, E * 2 * FFN])
        w_up = [shared[:, :].rearrange("p (e f) -> p e f", e=E),
                shared[:, 0:E * FFN].rearrange("p (e f) -> p e f", e=E)]
        y_second = shared[:, 0:NT * D].rearrange("p (t d) -> p t d", t=NT)
        w_down = sb("w_down", [P, E, 4, D])
        b_up = sb("b_up", [P, E, 4])
        b_down = sb("b_down", [P, E, D])
        rw = sb("rw", [P, 2, E])
        rb = sb("rb", [P, 2, E])
        xn = sb("xn", [P, 2, D])
        xn_t = sb("xn_t", [P, 2, P])
        work = sb("work", [P, 3 * H1 * NKEY])
        sub = work[:, 0:H1 * NKEY]
        expd = [work[:, (1 + k) * H1 * NKEY:(2 + k) * H1 * NKEY] for k in range(2)]
        act_a = work[:, 0:2 * FFN].rearrange("p (k f) -> p k f", k=2)
        hid_t = work[:, 2 * FFN:(2 + RING) * FFN].rearrange("p (k c n) -> p k c n", k=RING, c=4)
        w_slot = score_mat[0][:, :, :].rearrange("p b c -> p (b c)")[:, 0:4 * FFN].rearrange("p (k f) -> p k f", k=2)
        probs_t = sb("probs_t", [P, 10, P])
        mx = sb("mx", [P, H1])
        rec = sb("rec", [P, 2, 2, H1])
        stats = sb("stats", [P, 4, 6])
        mv = sb("mv", [P, 8, 2])
        rs = sb("rs", [P, 8, 2])
        xo = sb("xo", [P, RING, D])
        xo_t = sb("xo_t", [P, 2, P])
        logits = sb("logits", [P, NT, E])
        pick = sb("pick", [P, 2, NT, E])
        rt = sb("rt", [P, 3, NT, E])
        rcol = sb("rcol", [P, 8, NT])
        pick_b = sb("pick_b", [P, NT, E], BF16)
        totals = sb("totals", [P, P], BF16)
        nblk = sb("nblk", [P, NT + 1])
        nblk_b = sb("nblk_b", [P, P], BF16)
        pos_f = sb("pos_f", [P, 3, 2 * NT])
        pos_i = sb("pos_i", [P, 3, 2 * NT], I32)
        slot_rhs = sb("slot_rhs", [P, 2 * NT, 3, MAXSLOTS], BF16)
        at_row = work[:, 0:NT * P].bitcast(BF16).rearrange("p (m r) -> p m r", r=P)
        ids_f = sb("ids_f", [P, 3, MAXSLOTS])
        ids_put = sb("ids_put", [P, MAXSLOTS], I32)
        ids_get = sb("ids_get", [P, MAXSLOTS], I32)
        cums = sb("cums", [1, E])
        exp_cmp = sb("exp_cmp", [1, MAXSLOTS, E])
        exp_f = sb("exp_f", [1, MAXSLOTS])
        exp_i = sb("exp_i", [1, PAD + MAXSLOTS + 2 * RING], I32)
        coef = sb("coef", [P, 2, NT])
        tied_rows = sb("tied_rows", [P, 1])
        tied_rows_b = sb("tied_rows_b", [P, 1], BF16)
        tied_i = sb("tied_i", [1, 1], I32)
        tied_coef = sb("tied_coef", [P, E])
        xg = sb("xg", [P, RING, D])
        xg_t = sb("xg_t", [P, 2, P])
        y_out = sb("y_out", [P, RING, D])

        xn_dram = nc.dram_tensor("xn_scratch", [B * S, D], F32, kind="Internal").ap()
        y_dram = nc.dram_tensor("y_scratch", [2 * B * S + P * MAXSLOTS, D], F32, kind="Internal").ap()

        def kc(name, rows=P):
            a, n = CONST_COLS[name]
            return k_sb[0:rows, a:a + n]

        def kcb(name, rows=P):
            a, n = CONST_COLS[name]
            return kb_sb[0:rows, a:a + n]

        ident = kc("ident")
        x_tiles = x.rearrange("(t p) d -> p t d", p=P)
        out_tiles = out.rearrange("(t p) d -> p t d", p=P)
        xn_tiles = xn_dram.rearrange("(t p) d -> p t d", p=P)
        y_tiles = y_dram.rearrange("(t p) d -> p t d", p=P)

        def spread(ap, shape, axis):
            return ap.unsqueeze(axis).to_broadcast(shape)

        ld = sems("landed", "const0 const x gates small ctx wkv0 w0 w1 up0 up1 down0 down1")
        N_SMALL = 8
        init = sems("ready", "gates base_bias base constb vlen keep drop neg experts")
        prep = sems("prep0", "stats mv ln rs cn cn_turned cn_t prod out_act out_dve turned turned_act turned_dve")
        blk = sems("prep1", "kept built_v built_k made copied")
        att = sems("att", "y0 y1 y2 y3 base st_a mv_a ln_a rs_a xn xn_turned xn_t scores max sub exp sum "
                    "rec probs turned probs_t pv res st_b mv_b ln_b rs_b xo xo_turned xo_t stored0 stored1 stored2 stored3 "
                    "logit logit_out")
        rout = [sems(f"route{n}", "dve picked totals counts blocks positions gap expd halves placed apart hit "
                     "tile_hit at_row at_row_act ids rows experts")
                for n in range(2)]
        ffn = [sems(f"ffn{n}", names + "gathered0 gathered1 gathered2 gathered3 turned xg_t weights up hid "
                    "down y scattered0 scattered1 scattered2 scattered3") for n, names in enumerate(("act ", "biased "))]
        fin = sems("final", "coef half second last done done_dve stored")
        tie = sems("tied", "rows total number landed dve")

        LAYERS = (layer_plan(0, H0, HD0 ** -0.5, 4, 1), layer_plan(1, H1, HD1 ** -0.5, 6, 2))

        xn_ps, xo_ps = ps[:, 6, 0:P], ps[:, 6, P:2 * P]
        pv_ps, logit_ps = ps[:, 7, 0:P], ps[:, 7, P:P + E]

        def score_banks(layer, i):
            hn = layer.pair
            rest = [(2 + i % 2, 2 * hn, layer.heads - 2 * hn)] if layer.heads > 2 * hn else []
            return rest + [(0, 0, hn), (1, hn, hn)]

        def n_banks(layer):
            return len(score_banks(layer, 0))

        def seen_banks(layer):
            return layer.n * NT * n_banks(LAYERS[0])

        N_PROJ = 10
        N_SCORED = N_PROJ + H0
        N_PROD = N_SCORED + H0

        def wait_copied(eng, j):
            if j < N_PROJ and j % 2:
                eng.wait_ge(prep.out_dve, j // 2 + 1)
            elif j < N_PROJ:
                eng.wait_ge(prep.out_act, j // 2 + 1)
            else:
                eng.wait_ge(prep.out_act, N_PROJ // 2 + j - N_PROJ + 1)

        def projection(j):
            return kv_t[:, j, :] if j < 8 else kv1_t[:, j - 8, :]

        def dve_copy_projections(dve):
            for j in range(1, N_PROJ, 2):
                dve.wait_ge(prep.prod, j + 1)
                nc.vector.tensor_copy(projection(j), ps[:, 2 + j % 4, 0:CTX]).then_inc(prep.out_dve, 1)

        def act_copy_products(act, products):
            for j in products:
                act.wait_ge(prep.prod, j + 1)
                src = ps[:, 2 + j % 4, 0:CTX]
                if j < N_PROJ:
                    nc.scalar.copy(projection(j), src).then_inc(prep.out_act, 1)
                else:
                    h = (j - N_PROJ) % H0
                    value = j >= N_SCORED
                    nc.scalar.activation(
                        (vw_t if value else score_mat[0])[:, :, h * NKEY:(h + 1) * NKEY],
                        src.rearrange("p (b k) -> p b k", b=B), ACT.Copy,
                        scale=gate_t[:, 0:1] if value else 1.0).then_inc(prep.out_act, 1)

        def pe_products(pe, first, end):
            for j in range(first, end):
                if j >= 4:
                    wait_copied(pe, j - 4)
                dst = ps[:, 2 + j % 4, 0:CTX]
                if j < 8:
                    nc.tensor.matmul(dst, wkv0_sb[:, j * P:(j + 1) * P], cn_t[:, :], start=True,
                                     stop=True).then_inc(prep.prod, 1)
                elif j < N_PROJ:
                    pe.wait_ge(ld.w1, 32)
                    nc.tensor.matmul(dst, wqkvo1_sb[:, 1 + j - 8, :], c_t[:, :], start=True,
                                     stop=True).then_inc(prep.prod, 1)
                else:
                    value = j >= N_SCORED
                    h = (j - N_PROJ) % H0
                    if j == N_PROJ:
                        pe.wait_ge(ld.w0, 32)
                    wait_copied(pe, 4 * value + h // 2)
                    w = wout0_sb if value else wq0_sb
                    r = slice(64 * (h % 2), 64 * (h % 2) + 64)
                    nc.tensor.matmul(dst, w[r, h // 2, :], kv_t[r, 4 * value + h // 2, :],
                                     start=True, stop=True).then_inc(prep.prod, 1)

        def pe_turn_values(pe):
            wait_copied(pe, N_PROD - 1)
            L = LAYERS[0]
            for b in range(B):
                for g, group in enumerate(L.groups):
                    if b >= 2:
                        pe.wait_ge((prep.turned_dve, prep.turned_act)[b % 2], (b - 2) // 2 * 2 + g + 1)
                    for k, c in enumerate(group):
                        a, size = L.chunks[c]
                        last = nc.tensor.transpose(ps[0:size, 2 + 2 * (b % 2) + g, k * P:(k + 1) * P],
                                                   vw_t[:, b, a:a + size], ident)
                    last.then_inc(prep.turned, 1)

        def copy_turned(eng, copy, first, done):
            L = LAYERS[0]
            for b in range(first, B, 2):
                for g, group in enumerate(L.groups):
                    eng.wait_ge(prep.turned, b * 2 + g + 1)
                    for run in full_and_rest(group, L.chunks):
                        size, k = L.chunks[run[0]][1], run[0] - group[0]
                        last = copy(value_mat[0][0:size, b * 5 + run[0]:b * 5 + run[-1] + 1, :],
                                    ps[0:size, 2 + 2 * (b % 2) + g, k * P:(k + len(run)) * P
                                       ].rearrange("p (c d) -> p c d", d=D))
                    last.then_inc(done, 1)

        def build_block(tensor_tensor, value, b, built):
            dst = (value_mat[1][:, b * 10:(b + 1) * 10, :].rearrange("p c d -> p (c d)")[:, 0:H1 * NKEY]
                   if value else score_mat[1][:, b, :])
            rows = kv1_t[:, value, b * NKEY:(b + 1) * NKEY]
            tensor_tensor(dst.rearrange("p (h k) -> p h k", k=NKEY), spread(rows, [P, H1, NKEY], 1),
                          spread(kc("head_rows"), [P, H1, NKEY], 2), ALU.mult).then_inc(built, 1)

        N_PARTS = 6 * B

        def score_part(n):
            b, k = divmod(n - 3 * B, 3)
            return score_mat[1][:, b, slice(k * 6 * NKEY, min((k + 1) * 6, H1) * NKEY)]

        def value_part(n):
            group = LAYERS[1].groups[n % 3]
            return n // 3 * 10, group[0], group

        def pe_part(pe, n):
            if n < 3 * B:
                pe.wait_ge(blk.built_v, n // 3 + 1)
            else:
                pe.wait_ge(blk.built_k, n // 3 - B + 1)
            if n >= 2:
                pe.wait_ge(blk.copied, n - 1)
            bank = 2 + n % 2
            if n >= 3 * B:
                src = score_part(n)
                nc.tensor.matmul(ps[:, bank, 0:src.shape[-1]], wqkvo1_sb[:, 0, :], src, start=True,
                                 stop=True).then_inc(blk.made, 1)
            else:
                at, first, group = value_part(n)
                for c in group:
                    size = LAYERS[1].chunks[c][1]
                    last = nc.tensor.matmul(ps[0:size, bank, (c - first) * P:(c - first + 1) * P],
                                            value_mat[1][:, at + c, 0:size], wqkvo1_sb[:, 3, :],
                                            start=True, stop=True)
                last.then_inc(blk.made, 1)

        def act_part(act, n):
            act.wait_ge(blk.made, n + 1)
            bank = 2 + n % 2
            if n >= 3 * B:
                dst = score_part(n)
                nc.scalar.copy(dst, ps[:, bank, 0:dst.shape[-1]]).then_inc(blk.copied, 1)
            else:
                at, first, group = value_part(n)
                for run in full_and_rest(group, LAYERS[1].chunks):
                    size, k = LAYERS[1].chunks[run[0]][1], run[0] - first
                    last = nc.scalar.activation(
                        value_mat[1][0:size, at + run[0]:at + run[-1] + 1, :],
                        ps[0:size, bank, k * P:(k + len(run)) * P].rearrange("p (c d) -> p c d", d=D),
                        ACT.Copy, scale=gate_t[0:size, 1:2])
                last.then_inc(blk.copied, 1)

        (ROWS, RSTD_A, NORM_A, SCORES, SOFTMAX, SUMS, VALUES, RESIDUAL, RSTD_B, NORM_B, ROUTER, LOGITS) = range(12)
        STEPS = range(NT + LOGITS)
        EARLY_STEPS = SCORES + 1
        PART_STEPS = range(EARLY_STEPS, EARLY_STEPS + 9)
        PARTS_EARLY = len(PART_STEPS)
        PARTS_PICKED, PARTS_PLACED, PARTS_ROUTED, PARTS_BETWEEN = (PARTS_EARLY + n for n in (1, 4, 7, 12))

        def parts_of(layer, t):
            if layer.n == 0:
                return [PART_STEPS.index(t)] if t in PART_STEPS else []
            return [PARTS_BETWEEN + t] if 0 <= t < N_PARTS - PARTS_BETWEEN else []

        def tiles(t, *stages):
            return [t - stage if 0 <= t - stage < NT else None for stage in stages]

        def dve_attention(dve, layer, steps):
            s, L = att, layer
            seen = L.n * NT
            src = res if L.n == 0 else base
            for t in steps:
                i_res, i_rows = tiles(t, RESIDUAL, ROWS)
                i, = tiles(t, NORM_B)
                if i is not None and i >= DVE_NORMS:
                    dve.wait_ge(s.xo, seen + i)
                    norm_b(dve, nc.vector.tensor_scalar, i, seen)
                i, = tiles(t, SOFTMAX)
                if i is not None:
                    banks = score_banks(L, i)
                    for n, (bank, h, hn) in enumerate(banks):
                        dve.wait_ge(s.scores, seen_banks(L) + i * n_banks(L) + n + 1)
                        last = nc.vector.tensor_reduce(mx[:, h:h + hn], ps[:, bank, 0:hn * NKEY].rearrange(
                            "p (h k) -> p h k", k=NKEY), AX.X, ALU.max)
                    last.then_inc(s.max, 1)
                    dve.wait_ge(s.max, seen + i + 1)
                    if i >= 1:
                        dve.wait_ge(s.exp, seen + i)
                    for bank, h, hn in sorted(banks):
                        nc.vector.tensor_tensor(
                            sub[:, h * NKEY:(h + hn) * NKEY].rearrange("p (h k) -> p h k", k=NKEY),
                            ps[:, bank, 0:hn * NKEY].rearrange("p (h k) -> p h k", k=NKEY),
                            spread(mx[:, h:h + hn], [P, hn, NKEY], 2), ALU.subtract).then_inc(s.sub, 1)
                i_res, i_log = tiles(t, RESIDUAL, LOGITS)
                if i_res is not None:
                    if L.n == 0 and i_res == 0:
                        dve.wait_ge(init.base, 1)
                    dve.wait_ge(s.pv, seen + i_res + 1)
                    if i_log is not None:
                        dve.wait_ge(s.logit, seen + i_log + 1)
                    nc.vector.tensor_tensor(res[:, i_res, :], pv_ps, base[:, i_res, :], ALU.add).then_inc(s.res, 1)
                if i_log is not None:
                    dve.wait_ge(s.logit, seen + i_log + 1)
                    nc.vector.tensor_tensor(logits[:, i_log, :], logit_ps, rb[:, L.n, :],
                                            ALU.add).then_inc(s.logit_out, 1)
                i, = tiles(t, SUMS)
                if i is not None:
                    dve.wait_ge(s.exp, seen + i + 1)
                    nc.vector.tensor_reduce(rec[:, i % 2, 0, 0:L.heads],
                                            expd[i % 2][:, 0:L.cols].rearrange("p (h k) -> p h k", k=NKEY),
                                            AX.X, ALU.add).then_inc(s.sum, 1)
                    dve.wait_ge(s.sum, seen + i + 1)
                    if i >= 2:
                        dve.wait_ge(s.probs, seen + i - 1)
                    nc.vector.reciprocal(rec[:, i % 2, 1, 0:L.heads], rec[:, i % 2, 0, 0:L.heads]).then_inc(s.rec, 1)
                    if i == NT - 1:
                        dve.wait_ge(s.rec, seen + i + 1)
                        dve.wait_ge(s.probs, seen + i)
                        probabilities(nc.vector.tensor_tensor, L, i)
                if i_rows is not None:
                    i = i_rows
                    if L.n == 1:
                        dve.wait_ge((s.y0, s.y1, s.y2, s.y3)[i // TPB], 16)
                        nc.vector.scalar_tensor_tensor(base[:, i, :], base[:, i, :], coef[:, 0, i:i + 1],
                                                       res[:, i, :], ALU.mult, ALU.add).then_inc(s.base, 1)
                        dve.wait_ge(s.base, i + 1)
                    nc.vector.bn_stats(stats[:, i % 2, :], src[:, i, :]).then_inc(s.st_a, 1)
                if i_res is not None:
                    dve.wait_ge(s.res, seen + i_res + 1)
                    nc.vector.bn_stats(stats[:, 2 + i_res % 2, :], res[:, i_res, :]).then_inc(s.st_b, 1)
                if i_rows is not None:
                    dve.wait_ge(s.st_a, seen + i_rows + 1)
                    if i_rows >= 4:
                        dve.wait_ge(s.xn, seen + i_rows - 3)
                    nc.vector.bn_aggr(mv[:, i_rows % 4, :], stats[:, i_rows % 2, :]).then_inc(s.mv_a, 1)
                if i_res is not None:
                    dve.wait_ge(s.st_b, seen + i_res + 1)
                    if i_res >= 4:
                        dve.wait_ge(s.xo, seen + i_res - 3)
                    nc.vector.bn_aggr(mv[:, 4 + i_res % 4, :], stats[:, 2 + i_res % 2, :]).then_inc(s.mv_b, 1)

        def act_attention(act, layer, steps):
            s, L = att, layer
            seen = L.n * NT
            seen_groups = L.n * NT * len(LAYERS[0].groups)
            v_scale, eps_a = (1.0 + EPS, kc("eps2")) if L.n == 0 else (1.0, kc("eps"))
            if L.n == 1:
                nc.scalar.preload_act_table_set("natural_log_exp_and_others")
            for t in steps:
                i, i_router = tiles(t, SCORES, ROUTER)
                if i_router is not None:
                    act.wait_ge(s.xo_turned, seen + i_router + 1)
                if i is not None:
                    act.wait_ge(s.xn_turned, seen + i + 1)
                    if i >= 2:
                        act.wait_ge(s.scores, seen_banks(L) + (i - 1) * n_banks(L))
                    if L.n == 0:
                        nc.scalar.activation(xn_t[:, i % 2, :], xn_ps, ACT.Identity, bias=gb[:, 1:2],
                                             scale=gb[:, 0:1]).then_inc(s.xn_t, 1)
                    else:
                        nc.scalar.copy(xn_t[:, i % 2, :], xn_ps).then_inc(s.xn_t, 1)
                i = i_router
                if i is not None:
                    if i >= 2:
                        act.wait_ge(s.logit, seen + i - 1)
                    nc.scalar.copy(xo_t[:, i % 2, :], xo_ps).then_inc(s.xo_t, 1)
                i, = tiles(t, VALUES)
                if i is not None:
                    if i >= 1:
                        act.wait_ge(s.pv, seen + i)
                    for g, group in enumerate(L.groups):
                        act.wait_ge(s.turned, seen_groups + i * len(L.groups) + g + 1)
                        for run in full_and_rest(group, L.chunks):
                            size, k = L.chunks[run[0]][1], run[0] - group[0]
                            last = nc.scalar.copy(
                                probs_t[0:size, run[0]:run[-1] + 1, :],
                                ps[0:size, 4 + g % 2, k * P:(k + len(run)) * P].rearrange("p (c n) -> p c n", n=P))
                        last.then_inc(s.probs_t, 1)
                i_a, i_b = tiles(t, RSTD_A, RSTD_B)
                if i_a is not None:
                    act.wait_ge(s.mv_a, seen + i_a + 1)
                    nc.scalar.activation(rs[:, i_a % 4, 0:1], mv[:, i_a % 4, 1:2], ACT.Ln, bias=eps_a,
                                         scale=v_scale).then_inc(s.ln_a, 1)
                if i_b is not None:
                    act.wait_ge(s.mv_b, seen + i_b + 1)
                    nc.scalar.activation(rs[:, 4 + i_b % 4, 0:1], mv[:, 4 + i_b % 4, 1:2], ACT.Ln,
                                         bias=kc("eps")).then_inc(s.ln_b, 1)
                if i_a is not None:
                    act.wait_ge(s.ln_a, seen + i_a + 1)
                    nc.scalar.activation(rs[:, i_a % 4, 1:2], rs[:, i_a % 4, 0:1], ACT.Exp,
                                         scale=-0.5).then_inc(s.rs_a, 1)
                if i_b is not None:
                    act.wait_ge(s.ln_b, seen + i_b + 1)
                    nc.scalar.activation(rs[:, 4 + i_b % 4, 1:2], rs[:, 4 + i_b % 4, 0:1], ACT.Exp,
                                         scale=-0.5).then_inc(s.rs_b, 1)
                for part in parts_of(L, t - 1):
                    act_part(act, part)
                i, = tiles(t, SOFTMAX)
                if i is not None:
                    act.wait_ge(s.sub, seen_banks(L) + (i + 1) * n_banks(L))
                    if i >= 2:
                        act.wait_ge(s.turned, seen_groups + (i - 1) * len(L.groups))
                    nc.scalar.activation(expd[i % 2][:, 0:L.cols], sub[:, 0:L.cols], ACT.Exp,
                                         scale=L.scale).then_inc(s.exp, 1)

        def stored(s):
            return s.stored0, s.stored1, s.stored2, s.stored3

        DVE_NORMS = NT - 4

        def norm_b(eng, tensor_scalar, i, seen):
            s = att
            eng.wait_ge(s.rs_b, seen + i + 1)
            if i >= RING:
                eng.wait_ge(s.xo_turned, seen + i - RING + 1)
                eng.wait_ge(stored(s)[i % RING], (seen + i) // RING * 16)
            tensor_scalar(xo[:, i % RING, :], res[:, i, :], mv[:, 4 + i % 4, 0:1],
                          rs[:, 4 + i % 4, 1:2], ALU.subtract, ALU.mult).then_inc(s.xo, 1)

        def probabilities(tensor_tensor, layer, i):
            e = expd[i % 2][:, 0:layer.cols].rearrange("p (h k) -> p h k", k=NKEY)
            tensor_tensor(e, e, spread(rec[:, i % 2, 1, 0:layer.heads], [P, layer.heads, NKEY], 2),
                          ALU.mult).then_inc(att.probs, 1)

        def pool_attention(pool, layer, steps):
            s, L = att, layer
            seen = L.n * NT
            src = res if L.n == 0 else base
            for t in steps:
                i, = tiles(t, NORM_A)
                if i is not None:
                    pool.wait_ge(s.rs_a, seen + i + 1)
                    if i >= 2:
                        pool.wait_ge(s.xn_turned, seen + i - 1)
                    nc.gpsimd.tensor_scalar(xn[:, i % 2, :], src[:, i, :], mv[:, i % 4, 0:1], rs[:, i % 4, 1:2],
                                            ALU.subtract, ALU.mult).then_inc(s.xn, 1)
                i, = tiles(t, NORM_B)
                if i is not None and i < DVE_NORMS:
                    norm_b(pool, nc.gpsimd.tensor_scalar, i, seen)
                i, = tiles(t, SUMS)
                if i is not None and i < NT - 1:
                    pool.wait_ge(s.rec, seen + i + 1)
                    probabilities(nc.gpsimd.tensor_tensor, L, i)
                b = t - EARLY_STEPS
                if L.n == 0 and 0 <= b < B:
                    if b == 0:
                        pool.wait_ge(blk.kept, 1)
                        pool.wait_ge(prep.turned, B * 2)
                    build_block(nc.gpsimd.tensor_tensor, 0, b, blk.built_k)

        def pe_attention(pe, layer, steps):
            s, L = att, layer
            seen = L.n * NT
            G, per = len(L.groups), len(L.chunks)
            seen_groups = L.n * NT * len(LAYERS[0].groups)
            turned_in = {}

            def turn_probs(i, first, end):
                for g in range(first, min(end, G)):
                    if g % 2 in turned_in:
                        pe.wait_ge(s.probs_t, seen_groups + turned_in[g % 2] + 1)
                    turned_in[g % 2] = i * G + g
                    for k, c in enumerate(L.groups[g]):
                        a, size = L.chunks[c]
                        last = nc.tensor.transpose(ps[0:size, 4 + g % 2, k * P:(k + 1) * P],
                                                   expd[i % 2][:, a:a + size], ident)
                    last.then_inc(s.turned, 1)

            for t in steps:
                i, i_router = tiles(t, SCORES, ROUTER)
                before, router_before = tiles(t - 1, SCORES, ROUTER)
                if before is not None:
                    pe.wait_ge(s.xn_t, seen + before + 1)
                if router_before is not None:
                    pe.wait_ge(s.xo_t, seen + router_before + 1)
                if i is not None:
                    pe.wait_ge(s.xn, seen + i + 1)
                    nc.tensor.transpose(xn_ps, xn[:, i % 2, :], ident).then_inc(s.xn_turned, 1)
                if i_router is not None:
                    pe.wait_ge(s.xo, seen + i_router + 1)
                    nc.tensor.transpose(xo_ps, xo[:, i_router % RING, :], ident).then_inc(s.xo_turned, 1)
                i, = tiles(t, VALUES)
                if i is not None:
                    pe.wait_ge(s.probs, seen + i + 1)
                    turn_probs(i, 0, 2)
                i, = tiles(t, SCORES)
                if i is not None:
                    pe.wait_ge(s.xn_t, seen + i + 1)
                    if L.n == 1 and i == 0:
                        pe.wait_ge(blk.copied, N_PARTS)
                    for bank, h, hn in score_banks(L, i):
                        n = seen_banks(L) + i * n_banks(L)
                        if bank < 2 and i >= 1:
                            pe.wait_ge(s.sub, n - n_banks(L) + bank + 1)
                        elif i >= 2:
                            pe.wait_ge(s.sub, n - n_banks(L))
                        dst = ps[:, bank, 0:hn * NKEY]
                        if L.n == 1:
                            nc.tensor.matmul(dst, kcb("ones", 1),
                                             spread(drop[0:1, i // TPB, :], [1, hn, NKEY], 1),
                                             start=True, stop=False)
                        nc.tensor.matmul(dst, xn_t[:, i % 2, :],
                                         score_mat[L.n][:, i // TPB, h * NKEY:(h + hn) * NKEY],
                                         start=(L.n == 0), stop=True).then_inc(s.scores, 1)
                i, = tiles(t, VALUES)
                if i is not None:
                    turn_probs(i, 2, G)
                i, i_router = tiles(t, VALUES, ROUTER)
                before, router_before = tiles(t - 1, VALUES, ROUTER)
                if before is not None:
                    pe.wait_ge(s.res, seen + before + 1)
                if router_before is not None:
                    pe.wait_ge(s.logit_out, seen + router_before + 1)
                if i_router is not None:
                    pe.wait_ge(s.xo_t, seen + i_router + 1)
                    nc.tensor.matmul(logit_ps, xo_t[:, i_router % 2, :], rw[:, L.n, :], start=True,
                                     stop=True).then_inc(s.logit, 1)
                if i is not None:
                    for g, group in enumerate(L.groups):
                        pe.wait_ge(s.probs_t, seen_groups + i * G + g + 1)
                        for c in group:
                            size = L.chunks[c][1]
                            last = nc.tensor.matmul(pv_ps, probs_t[0:size, c, :],
                                                    value_mat[L.n][0:size, i // TPB * per + c, :],
                                                    start=(c == 0), stop=(c == per - 1))
                    last.then_inc(s.pv, 1)
                if L.n == 1 and t == 0:
                    pe.wait_ge(s.y0, 16)
                for part in parts_of(L, t):
                    pe_part(pe, part)

        def sp_attention(sp, layer):
            s, seen = att, layer.n * NT
            for i in range(NT):
                sp.wait_ge(s.xo, seen + i + 1)
                sp.dma_start(xn_tiles[:, i, :], xo[:, i % RING, :]).then_inc(stored(s)[i % RING], 16)

        def rows_by_act(n):
            return n // 16 * 6

        def dve_route(dve, layer):
            r, L, K, NS = rout[layer.n], layer, layer.choices, layer.slots
            done = [0]

            def link(ins):
                done[0] += 1
                ins.then_inc(r.dve, 1)
                dve.wait_ge(r.dve, done[0])

            def col(c, shape=(P, NT, E)):
                return spread(rcol[:, c, :], list(shape), 2)

            dve.wait_ge(att.logit_out, (L.n + 1) * NT)
            rank = spread(kc("expert_rank"), [P, NT, E], 1)
            cand = logits
            for k in range(K):
                link(nc.vector.tensor_reduce(rcol[:, 2 * k, :], cand[:, :, :], AX.X, ALU.max))
                link(nc.vector.tensor_tensor(rt[:, 0], cand[:, :, :], col(2 * k), ALU.is_equal))
                link(nc.vector.tensor_tensor(rt[:, 0], rt[:, 0], rank, ALU.mult))
                link(nc.vector.tensor_reduce(rcol[:, 1, :], rt[:, 0], AX.X, ALU.max))
                link(nc.vector.tensor_tensor(pick[:, k], rt[:, 0], col(1), ALU.is_equal))
                if k + 1 < K:
                    link(nc.vector.scalar_tensor_tensor(rt[:, 1], pick[:, k], -BIG, logits[:, :, :],
                                                        ALU.mult, ALU.add))
                    cand = rt[:, 1]
            if K == 1:
                nc.vector.tensor_copy(pick_b[:, :, :], pick[:, 0]).then_inc(r.picked, 1)
            else:
                nc.vector.tensor_tensor(pick_b[:, :, :], pick[:, 0], pick[:, 1], ALU.add).then_inc(r.picked, 1)
            if K == 1:
                nc.vector.tensor_tensor(rt[:, 2], logits[:, :, :], col(0), ALU.subtract).then_inc(r.gap, 1)
            else:
                nc.vector.tensor_tensor(rcol[:, 4, :], rcol[:, 2, :], rcol[:, 0, :], ALU.subtract).then_inc(r.gap, 1)
            dve.wait_ge(r.totals, 1)
            nc.vector.tensor_copy(totals[:, :], ps[:, 6, 0:P]).then_inc(r.totals, 1)
            dve.wait_ge(r.counts, 1)
            link(nc.vector.tensor_scalar(nblk[0:E, 0:NT], kc("slot_edges", E), ps[0:E, 7, 0:1], None, ALU.is_lt))
            link(nc.vector.tensor_reduce(nblk[0:E, NT:NT + 1], nblk[0:E, 0:NT], AX.X, ALU.add))
            nc.vector.tensor_scalar(nblk_b[0:E, :], kc("ones", E), nblk[0:E, NT:NT + 1], None,
                                    ALU.mult).then_inc(r.blocks, 1)
            dve.wait_ge(r.positions, 1)
            link(nc.vector.tensor_tensor(rt[:, 0:K], spread(ps[:, 5, 0:P].rearrange("p (t e) -> p t e", e=E),
                                                            [P, K, NT, E], 1), pick[:, 0:K], ALU.mult))
            n = K * NT
            link(nc.vector.tensor_reduce(pos_f[:, 0, 0:n].rearrange("p (k t) -> p k t", k=K), rt[:, 0:K], AX.X, ALU.add))
            link(nc.vector.tensor_copy(pos_i[:, 0, 0:n], pos_f[:, 0, 0:n]))
            nc.vector.tensor_scalar(pos_i[:, 1, 0:n], pos_i[:, 0, 0:n], 7, None, ALU.logical_shift_right
                                    ).then_inc(r.halves, 1)
            nc.vector.tensor_scalar(pos_i[:, 2, 0:n], pos_i[:, 0, 0:n], P - 1, None, ALU.bitwise_and
                                    ).then_inc(r.halves, 1)
            dve.wait_ge(r.halves, 2)
            nc.vector.tensor_copy(pos_f[:, 1:3, 0:n], pos_i[:, 1:3, 0:n]).then_inc(r.placed, 1)
            dve.wait_ge(r.placed, 1)
            hit = slot_rhs[:, 0:n, 2, 0:NS]
            nc.vector.tensor_tensor(hit, spread(kc("slot_number")[:, 0:NS], [P, n, NS], 1),
                                    spread(pos_f[:, 1, 0:n], [P, n, NS], 2), ALU.is_equal).then_inc(r.hit, 1)
            dve.wait_ge(r.hit, 1)
            nc.vector.tensor_scalar(slot_rhs[:, 0:n, 0, 0:NS], hit, kc("row_plus_1"), None,
                                    ALU.mult).then_inc(r.hit, 1)
            for m in range(n - rows_by_act(n)):
                nc.vector.tensor_scalar(at_row[:, m, :], kcb("row_number"), pos_f[:, 2, m:m + 1], None,
                                        ALU.is_equal).then_inc(r.at_row, 1)
            dve.wait_ge(r.ids, 1)
            by_row, by_tile = ps[:, 4, 0:NS], ps[:, 4, NS:2 * NS]
            nc.vector.tensor_copy(ids_f[:, 2, 0:NS], by_tile).then_inc(r.apart, 1)
            nc.vector.scalar_tensor_tensor(ids_f[:, 1, 0:NS], by_row, 0.0, kc("pad_rows_plus_1")[:, 0:NS],
                                           ALU.is_equal, ALU.mult).then_inc(r.apart, 1)
            dve.wait_ge(r.apart, 1)
            nc.vector.scalar_tensor_tensor(ids_f[:, 0, 0:NS], ids_f[:, 2, 0:NS], float(P), by_row, ALU.mult, ALU.add
                                           ).then_inc(r.apart, 1)
            dve.wait_ge(r.apart, 3)
            link(nc.vector.scalar_tensor_tensor(ids_put[:, 0:NS], ids_f[:, 0, 0:NS], -1.0, ids_f[:, 1, 0:NS],
                                                ALU.add, ALU.add))
            nc.vector.tensor_scalar(ids_get[:, 0:NS], ids_put[:, 0:NS], B * S - 1, None,
                                    ALU.bitwise_and).then_inc(r.rows, 1)
            link(nc.vector.tensor_copy(cums[:, :], ps[0:1, 1, 0:E]))
            link(nc.vector.tensor_tensor(exp_cmp[:, 0:NS, :], spread(cums[:, :], [1, NS, E], 1),
                                         spread(kc("slot_number", 1)[:, 0:NS], [1, NS, E], 2), ALU.is_le))
            link(nc.vector.tensor_reduce(exp_f[:, 0:NS], exp_cmp[:, 0:NS, :], AX.X, ALU.add))
            nc.vector.tensor_scalar(exp_i[:, PAD:PAD + NS], exp_f[:, 0:NS], E - 1.0, None, ALU.min
                                    ).then_inc(r.experts, 1)
            gate = gate_t[:, 2 + L.n:3 + L.n]
            dve.wait_ge(r.expd, 1)
            if K == 1:
                link(nc.vector.tensor_reduce(rcol[:, 5, :], rt[:, 2], AX.X, ALU.add))
                link(nc.vector.reciprocal(rcol[:, 6, :], rcol[:, 5, :]))
            else:
                link(nc.vector.tensor_scalar(rcol[:, 5, :], rcol[:, 7, :], 1.0, None, ALU.add))
                link(nc.vector.reciprocal(rcol[:, 6, :], rcol[:, 5, :]))
            link(nc.vector.tensor_scalar(coef[:, 0, :], rcol[:, 6, :], gate, None, ALU.mult))
            if K == 2:
                nc.vector.tensor_tensor(coef[:, 1, :], coef[:, 0, :], rcol[:, 7, :], ALU.mult).then_inc(fin.coef, 1)

        def act_route(act, layer):
            r = rout[layer.n]
            act.wait_ge(r.gap, 1)
            if layer.choices == 1:
                nc.scalar.activation(rt[:, 2], rt[:, 2], ACT.Exp).then_inc(r.expd, 1)
            else:
                nc.scalar.activation(rcol[:, 7, :], rcol[:, 4, :], ACT.Exp).then_inc(r.expd, 1)
            if layer.n == 0:
                for part in range(PARTS_EARLY, PARTS_PICKED):
                    act_part(act, part)
            nc.scalar.preload_act_table_set(("silu_and_others", "gelu_and_others")[layer.n])
            n = layer.choices * NT
            mine = range(n - rows_by_act(n), n)
            act.wait_ge(r.placed, 1)
            for m in mine:
                last = nc.scalar.activation(at_row[:, m, :], kcb("row_number"), ACT.Abs, bias=pos_f[:, 2, m:m + 1],
                                            scale=-1.0)
            last.then_inc(r.at_row_act, 1)
            act.wait_ge(r.at_row_act, 1)
            nc.scalar.activation(at_row[:, mine[0]:n, :], at_row[:, mine[0]:n, :], ACT.Relu,
                                 bias=kc("ones")[:, 0:1], scale=-1.0).then_inc(r.at_row_act, 1)
            if layer.n == 0:
                for part in range(PARTS_PICKED, PARTS_ROUTED):
                    act_part(act, part)

        def pool_route(pool, layer):
            r, n, NS = rout[layer.n], layer.choices * NT, layer.slots
            pool.wait_ge(r.hit, 1)
            for first in (0, n // 2):
                half = slice(first, first + n // 2)
                nc.gpsimd.tensor_tensor(slot_rhs[:, half, 1, 0:NS], slot_rhs[:, half, 2, 0:NS],
                                        spread(kc("tile_number")[:, half], [P, n // 2, NS], 2),
                                        ALU.mult).then_inc(r.tile_hit, 1)

        def pe_route(pe, layer):
            r, n, NS = rout[layer.n], layer.choices * NT, layer.slots
            flat = pick_b[:, :, :].rearrange("p t e -> p (t e)")
            if layer.n == 0:
                for part in range(PARTS_EARLY, PARTS_PICKED):
                    pe_part(pe, part)
            pe.wait_ge(r.picked, 1)
            nc.tensor.matmul(ps[:, 5, 0:P], kcb("before"), flat, start=True, stop=False)
            nc.tensor.matmul(ps[:, 6, 0:P], flat, kcb("ones"), start=True, stop=True).then_inc(r.totals, 1)
            pe.wait_ge(r.totals, 2)
            nc.tensor.matmul(ps[0:E, 7, 0:P], kcb("same_expert"), totals[:, :], start=True,
                             stop=True).then_inc(r.counts, 1)
            nc.tensor.matmul(ps[:, 5, 0:P], totals[:, :], kcb("earlier_tile"), start=False, stop=False)
            pe.wait_ge(r.blocks, 1)
            nc.tensor.matmul(ps[:, 1, 0:E], nblk_b[0:E, :], kcb("upto_expert", E), start=True, stop=True)
            nc.tensor.matmul(ps[:, 5, 0:P], nblk_b[0:E, :], kcb("lower_expert", E), start=False,
                             stop=True).then_inc(r.positions, 1)
            if layer.n == 0:
                for part in range(PARTS_PICKED, PARTS_PLACED):
                    pe_part(pe, part)
            pe.wait_ge(r.hit, 2)
            for m in range(n):
                pe.wait_ge(r.tile_hit, m // (n // 2) + 1)
                if m < n - rows_by_act(n):
                    pe.wait_ge(r.at_row, m + 1)
                else:
                    pe.wait_ge(r.at_row_act, 2)
                last = nc.tensor.matmul(ps[:, 4, 0:2 * NS], at_row[:, m, :], slot_rhs[:, m, 0:2, 0:NS],
                                        start=(m == 0), stop=(m == n - 1))
            last.then_inc(r.ids, 1)
            if layer.n == 0:
                for part in range(PARTS_PLACED, PARTS_ROUTED):
                    pe_part(pe, part)

        def gathered(f):
            return f.gathered0, f.gathered1, f.gathered2, f.gathered3

        def scattered(f):
            return f.scattered0, f.scattered1, f.scattered2, f.scattered3

        def pool_experts(pool, layer):
            f, NS = ffn[layer.n], layer.slots
            pool.wait_ge(rout[layer.n].rows, 1)
            for buffer_stored in stored(att):
                pool.wait_ge(buffer_stored, 16 * (NT // RING) * (layer.n + 1))
            for t in range(NS + 7):
                if t < NS:
                    if t >= RING:
                        pool.wait_ge(f.turned, t - RING + 1)
                    pool.indirect_dma_start(
                        xg[:, t % RING, :], None, xn_dram,
                        bass.IndirectOffsetOnAxis(ap=ids_get[:, t:t + 1].bitcast(U32), axis=0)
                    ).then_inc(gathered(f)[t % RING], 16)
                if t >= 7:
                    j = t - 7
                    pool.wait_ge(f.y, j + 1)
                    pool.indirect_dma_start(
                        y_dram, bass.IndirectOffsetOnAxis(ap=ids_put[:, j:j + 1].bitcast(U32), axis=0),
                        y_out[:, j % RING, :], None
                    ).then_inc(scattered(f)[j % RING], 16)

        def expert_numbers(eng, first, n):
            return nc.values_load_multi_w_load_instructions(
                exp_i[0:1, ds(first, n)], engines=[eng.engine], min_val=0, max_val=E - 1,
                skip_runtime_bounds_check_because="the table is clamped to 0..E-1 where it is made")[1]

        def turn_bank(q):
            return ps[:, (6, 4)[q], 0:P]

        def up_bank(q):
            return ps[:, q, :]

        def gate_bank(q):
            return ps[:, (2, 7)[q], :]

        def down_bank(q):
            return ps[:, (5, 3)[q], 0:D]

        def pe_experts(pe, layer):
            f, L, NS = ffn[layer.n], layer, layer.slots
            pe.wait_ge(rout[L.n].experts, 1)
            pe.wait_ge((ld.down0, ld.down1)[L.n], 16)

            def step(t, par, fetched):
                if live(t, 0, NS):
                    i, q = t, par % 2
                    pe.wait_ge(gathered(f)[par], (i - par) * (16 // RING) + 16)
                    if past(i, 2):
                        pe.wait_ge(f.xg_t, i - 1)
                    nc.tensor.transpose(turn_bank(q), xg[:, par, :], ident).then_inc(f.turned, 1)
                if live(t, 1, NS):
                    i, q = t - 1, (par - 1) % 2
                    pe.wait_ge(f.xg_t, i + 1)
                    pe.wait_ge(f.weights, i + 1)
                    if past(i, 2):
                        pe.wait_ge(f.hid if L.n == 0 else f.biased, i - 1)
                    for c in range(w_up[L.n].shape[-1] // P):
                        bank = (up_bank, gate_bank)[c // 4](q)
                        last = nc.tensor.matmul(bank[:, c % 4 * P:(c % 4 + 1) * P], w_slot[:, q, c * P:(c + 1) * P],
                                                xg_t[:, q, :], start=True, stop=True)
                    last.then_inc(f.up, 1)
                if live(t, 3, NS):
                    i, q = t - 3, (par - 3) % 2
                    e = fetched[par]
                    pe.wait_ge(f.hid, i + 1)
                    if past(i, 2):
                        pe.wait_ge(f.y, i - 1)
                    for c in range(4):
                        last = nc.tensor.matmul(down_bank(q), hid_t[:, (par - 3) % RING, c, :],
                                                w_down[:, ds(e, 1), c, :], start=(c == 0), stop=(c == 3))
                    last.then_inc(f.down, 1)

            pipeline(pe, NS, 3, step, lambda t: expert_numbers(pe, t, RING))

        def act_experts(act, layer):
            f, L, NS = ffn[layer.n], layer, layer.slots

            def step(t, par, fetched):
                if live(t, 0, NS):
                    i, q = t, par % 2
                    act.wait_ge(f.turned, i + 1)
                    if past(i, 2):
                        act.wait_ge(f.up, i - 1)
                    nc.scalar.copy(xg_t[:, q, :], turn_bank(q)).then_inc(f.xg_t, 1)
                if L.n == 0 and live(t, 1, NS):
                    i, q = t - 1, (par - 1) % 2
                    act.wait_ge(f.up, i + 1)
                    if past(i, 2):
                        act.wait_ge(f.hid, i - 1)
                    nc.scalar.activation(act_a[:, q, :], up_bank(q), ACT.Silu).then_inc(f.act, 1)
                if L.n == 1 and live(t, 2, NS):
                    i, q = t - 2, (par - 2) % RING
                    act.wait_ge(f.biased, i + 1)
                    if past(i, RING):
                        act.wait_ge(f.down, i - RING + 1)
                    nc.scalar.activation(hid_t[:, q], by_chunk(act_a[:, q % 2, :]), ACT.Gelu).then_inc(f.hid, 1)

            pipeline(act, NS, 3, step)

        def by_chunk(row):
            return row.rearrange("p (c n) -> p c n", c=4)

        def dve_experts(dve, layer):
            f, L, NS = ffn[layer.n], layer, layer.slots
            dve.wait_ge(rout[L.n].experts, 1)
            dve.wait_ge((ld.up0, ld.up1)[L.n], 16)
            width = w_up[L.n].shape[-1]

            def step(t, par, fetched):
                if live(t, 0, NS):
                    i, q = t, par % 2
                    e = fetched[PAD + par]
                    if past(i, 2):
                        dve.wait_ge(f.up, i - 1)
                    nc.vector.tensor_copy(w_slot[:, q, 0:width], w_up[L.n][:, ds(e, 1), :]).then_inc(f.weights, 1)
                if live(t, 1, NS):
                    i, q = t - 1, (par - 1) % 2
                    dve.wait_ge(f.up, i + 1)
                    if L.n == 0:
                        dve.wait_ge(f.act, i + 1)
                        if past(i, RING):
                            dve.wait_ge(f.down, i - RING + 1)
                        nc.vector.tensor_tensor(hid_t[:, (par - 1) % RING], by_chunk(gate_bank(q)),
                                                by_chunk(act_a[:, q, :]), ALU.mult).then_inc(f.hid, 1)
                    else:
                        e = fetched[PAD - 1 + par]
                        if past(i, 2):
                            dve.wait_ge(f.hid, i - 1)
                        bias = b_up[:, ds(e, 1), :].rearrange("p o c -> p (o c)")
                        nc.vector.tensor_tensor(by_chunk(act_a[:, q, :]), by_chunk(up_bank(q)),
                                                spread(bias, [P, 4, P], 2), ALU.add).then_inc(f.biased, 1)
                if live(t, 3, NS):
                    i, q = t - 3, (par - 3) % RING
                    dve.wait_ge(f.down, i + 1)
                    if past(i, RING):
                        dve.wait_ge(scattered(f)[q], (i - q) * (16 // RING))
                    if L.n == 0:
                        nc.vector.tensor_copy(y_out[:, q, :], down_bank(q % 2)).then_inc(f.y, 1)
                    else:
                        nc.vector.tensor_tensor(y_out[:, q, :], down_bank(q % 2), b_down[:, ds(fetched[par], 1), :],
                                                ALU.add).then_inc(f.y, 1)

            pipeline(dve, NS, 3, step, lambda t: expert_numbers(dve, t, PAD + RING))

        def wait_scattered(eng, layer):
            f, NS = ffn[layer.n], layer.slots
            for k in range(RING):
                eng.wait_ge(scattered(f)[k], 16 * len(range(k, NS, RING)))

        Piece = namedtuple("Piece", "first end landed count")
        PIECES = (Piece(0, 4, att.y0, 48), Piece(4, 8, att.y1, 48), Piece(8, 11, att.y2, 48), Piece(11, 14, att.y3, 48),
                  Piece(14, NT, fin.last, 32))
        POOL_PIECES = len(PIECES) - 2

        def add_second(tensor_tensor, piece, done):
            t = slice(piece.first, piece.end)
            tensor_tensor(base[:, t, :], base[:, t, :], y_second[:, t, :], ALU.add).then_inc(done, 1)

        r, f, NS = rout[1], ffn[1], LAYERS[1].slots
        TIE_WEIGHTS, TIE_STEPS = 5, 2 + E

        def dve_find_ties(dve):
            nc.vector.tensor_tensor(rt[:, 0], logits[:, :, :], spread(rcol[:, 2, :], [P, NT, E], 2),
                                    ALU.is_ge).then_inc(tie.rows, 1)
            dve.wait_ge(tie.rows, 1)
            nc.vector.tensor_reduce(tied_rows[:, :], rt[:, 0].rearrange("p t e -> p (t e)"), AX.X,
                                    ALU.add).then_inc(tie.rows, 1)
            dve.wait_ge(tie.rows, 2)
            nc.vector.tensor_scalar(tied_rows_b[:, :], tied_rows[:, :], -2.0 * NT, None, ALU.add).then_inc(tie.rows, 1)
            dve.wait_ge(tie.total, 1)
            nc.vector.tensor_copy(tied_i[:, :], ps[0:1, 0, 0:1]).then_inc(tie.number, 1)

        def pe_sum_ties(pe):
            pe.wait_ge(tie.rows, 3)
            nc.tensor.matmul(ps[0:1, 0, 0:1], tied_rows_b[:, :], kcb("ones")[:, 0:1], start=True,
                             stop=True).then_inc(tie.total, 1)

        def any_ties(eng):
            eng.wait_ge(tie.number, 1)
            number, = nc.values_load_multi_w_load_instructions(
                tied_i[0:1, 0:1], engines=[eng.engine], min_val=0, max_val=B * S * (E - 2),
                skip_runtime_bounds_check_because="a token has two to E choices")[1]
            return number > 0

        def sp_tied(sp):
            sp.dma_start(w_up[1], w1_1.rearrange("e d f -> d e f")).then_inc(ld.up1, 16)
            with sp.Fori(0, NT) as t:
                sp.wait_ge(f.turned, t + NS)
                sp.dma_start(xg[:, 0:1, :], xn_tiles[:, ds(t, 1), :]).then_inc(tie.landed, 16)
                sp.wait_ge(tie.dve, t * TIE_STEPS + (TIE_WEIGHTS + TIE_STEPS))
                sp.dma_start(out_tiles[:, ds(t, 1), :], xo[:, 0:1, :]).then_inc(fin.stored, 16)
            sp.wait_ge(fin.stored, 16 * (len(PIECES) + NT))

        def pe_tied(pe):
            pe.wait_ge(ld.up1, 32)
            with pe.Fori(0, NT) as t:
                pe.wait_ge(tie.landed, t * 16 + 16)
                pe.wait_ge(f.xg_t, t + NS)
                nc.tensor.transpose(turn_bank(0), xg[:, 0, :], ident).then_inc(f.turned, 1)
                pe.wait_ge(f.xg_t, t + (NS + 1))
                for e in range(E):
                    pe.wait_ge(f.biased, t * E + (e + NS))
                    for c in range(4):
                        last = nc.tensor.matmul(up_bank(0)[:, c * P:(c + 1) * P], w_up[1][:, e, c * P:(c + 1) * P],
                                                xg_t[:, 0, :], start=True, stop=True)
                    last.then_inc(f.up, 1)
                    pe.wait_ge(f.hid, t * E + (e + 1 + NS))
                    pe.wait_ge(f.y, t * E + (e + NS))
                    for c in range(4):
                        last = nc.tensor.matmul(down_bank(0), hid_t[:, 0, c, :], w_down[:, e, c, :],
                                                start=(c == 0), stop=(c == 3))
                    last.then_inc(f.down, 1)

        def act_tied(act):
            nc.scalar.preload_act_table_set("natural_log_exp_and_others")
            act.wait_ge(r.gap, 2)
            nc.scalar.activation(rt[:, 1], rt[:, 1], ACT.Exp).then_inc(r.expd, 1)
            nc.scalar.preload_act_table_set("gelu_and_others")
            with act.Fori(0, NT) as t:
                act.wait_ge(f.turned, t + (NS + 1))
                act.wait_ge(f.up, t * E + NS)
                nc.scalar.copy(xg_t[:, 0, :], turn_bank(0)).then_inc(f.xg_t, 1)
                for e in range(E):
                    act.wait_ge(f.biased, t * E + (e + 1 + NS))
                    act.wait_ge(f.down, t * E + (e + NS))
                    nc.scalar.activation(hid_t[:, 0], by_chunk(act_a[:, 0, :]), ACT.Gelu).then_inc(f.hid, 1)

        def dve_tied(dve):
            nc.vector.tensor_tensor(rt[:, 1], logits[:, :, :], spread(rcol[:, 0, :], [P, NT, E], 2),
                                    ALU.subtract).then_inc(r.gap, 1)
            dve.wait_ge(r.expd, 2)
            nc.vector.tensor_tensor(rt[:, 1], rt[:, 1], rt[:, 0], ALU.mult).then_inc(tie.dve, 1)
            dve.wait_ge(tie.dve, 1)
            nc.vector.tensor_reduce(rcol[:, 5, :], rt[:, 1], AX.X, ALU.add).then_inc(tie.dve, 1)
            dve.wait_ge(tie.dve, 2)
            nc.vector.reciprocal(rcol[:, 6, :], rcol[:, 5, :]).then_inc(tie.dve, 1)
            dve.wait_ge(tie.dve, 3)
            nc.vector.tensor_scalar(rcol[:, 5, :], rcol[:, 6, :], gate_t[:, 3:4], None, ALU.mult).then_inc(tie.dve, 1)
            dve.wait_ge(tie.dve, 4)
            nc.vector.tensor_tensor(rt[:, 2], rt[:, 1], spread(rcol[:, 5, :], [P, NT, E], 2),
                                    ALU.mult).then_inc(tie.dve, 1)
            dve.wait_ge(tie.dve, 5)
            with dve.Fori(0, NT) as t:
                dve.wait_ge(tie.dve, t * TIE_STEPS + TIE_WEIGHTS)
                nc.vector.tensor_copy(tied_coef[:, :], rt[:, 2, ds(t, 1), :]).then_inc(tie.dve, 1)
                dve.wait_ge(fin.stored, t * 16 + 16 * len(PIECES))
                nc.vector.tensor_copy(xo[:, 0, :], res[:, ds(t, 1), :]).then_inc(tie.dve, 1)
                for e in range(E):
                    dve.wait_ge(f.up, t * E + (e + 1 + NS))
                    dve.wait_ge(f.hid, t * E + (e + NS))
                    nc.vector.tensor_tensor(by_chunk(act_a[:, 0, :]), by_chunk(up_bank(0)),
                                            spread(b_up[:, e, :], [P, 4, P], 2), ALU.add).then_inc(f.biased, 1)
                    dve.wait_ge(f.down, t * E + (e + 1 + NS))
                    dve.wait_ge(tie.dve, t * TIE_STEPS + (TIE_WEIGHTS + 2 + e))
                    nc.vector.tensor_tensor(y_out[:, 0, :], down_bank(0), b_down[:, e, :],
                                            ALU.add).then_inc(f.y, 1)
                    dve.wait_ge(f.y, t * E + (e + 1 + NS))
                    nc.vector.scalar_tensor_tensor(xo[:, 0, :], y_out[:, 0, :], tied_coef[:, e:e + 1], xo[:, 0, :],
                                                   ALU.mult, ALU.add).then_inc(tie.dve, 1)

        block = stack.enter_context(nc.Block())

        @block.sync
        def _(sp):
            sp.dma_start(ctx_sb[:, 0:2, :], ctx_rows[0:2 * P, :].rearrange("(t p) d -> p t d", p=P)).then_inc(ld.ctx, 16)
            sp.dma_start(ctx_sb[0:CTX - 2 * P, 2, :], ctx_rows[2 * P:CTX, :]).then_inc(ld.ctx, 16)
            for dst, src in ((gate_in[:, 0:2], g_xattn.to_broadcast([P, 2])), (gate_in[:, 2:4], g_ffn.to_broadcast([P, 2])),
                             (gb[:, :], ln_gb)):
                sp.dma_start(dst, src).then_inc(ld.gates, 16)
            sp.dma_start(k_sb[:, 0:FIRST_CONST], const[:, 0:FIRST_CONST]).then_inc(ld.const0, 16)
            sp.dma_start(wkv0_sb[:, :], wkv0).then_inc(ld.wkv0, 16)
            sp.dma_start(c_t[:, :], ctx_cols).then_inc(ld.w1, 16)
            sp.dma_start(wqkvo1_sb[:, :, :], wqkvo1).then_inc(ld.w1, 16)
            sp.dma_start(wq0_sb[:, :, :], wq0.rearrange("(c p) d -> p c d", p=P)).then_inc(ld.w0, 16)
            sp.dma_start(wout0_sb[:, :, :], wout0.rearrange("(c p) d -> p c d", p=P)).then_inc(ld.w0, 16)
            sp.dma_start(res[:, :, :], x_tiles).then_inc(ld.x, 16)
            sp.dma_start(k_sb[:, FIRST_CONST:], const[:, FIRST_CONST:]).then_inc(ld.const, 16)
            small = ((bout_b[:, :], out_bias.to_broadcast([P, D])),
                     (vlen_i[:, :], valid_len.to_broadcast([P, B])), (rw[:, 0, :], rw0), (rw[:, 1, :], rw1),
                     (rb[:, 0, :], rb0.to_broadcast([P, E])), (rb[:, 1, :], rb1.to_broadcast([P, E])),
                     (b_up[:, :, :], b1_1), (b_down[:, :, :], b2_1.to_broadcast([P, E, D])))
            assert len(small) == N_SMALL
            for dst, src in small:
                sp.dma_start(dst, src).then_inc(ld.small, 16)
            sp.dma_start(w_up[0], w1_0.rearrange("e d f -> d e f")).then_inc(ld.up0, 16)
            sp.dma_start(w_down[:, :, :, :], w2_0.rearrange("e (c p) d -> p e c d", p=P)).then_inc(ld.down0, 16)
            sp_attention(sp, LAYERS[0])
            wait_scattered(sp, LAYERS[0])
            for b, landed in enumerate((att.y0, att.y1, att.y2, att.y3)):
                t = slice(b * TPB, (b + 1) * TPB)
                sp.dma_start(base[:, t, :], y_tiles[:, t, :]).then_inc(landed, 16)
            sp.wait_ge(ffn[0].weights, LAYERS[0].slots)
            sp.wait_ge(ffn[0].down, LAYERS[0].slots)
            sp.dma_start(w_up[1], w1_1.rearrange("e d f -> d e f")).then_inc(ld.up1, 16)
            sp.dma_start(w_down[:, :, :, :], w2_1.rearrange("e (c p) d -> p e c d", p=P)).then_inc(ld.down1, 16)
            sp_attention(sp, LAYERS[1])
            wait_scattered(sp, LAYERS[1])
            sp.wait_ge(ffn[1].weights, LAYERS[1].slots)
            for piece in PIECES:
                t = slice(piece.first, piece.end)
                sp.dma_start(base[:, t, :], y_tiles[:, t, :]).then_inc(piece.landed, 16)
                sp.dma_start(y_second[:, t, :], y_tiles[:, NT + piece.first:NT + piece.end, :]).then_inc(piece.landed, 16)
            for n, piece in enumerate(PIECES):
                t = slice(piece.first, piece.end)
                if n < POOL_PIECES:
                    sp.wait_ge(fin.done, n + 1)
                else:
                    sp.wait_ge(fin.done_dve, n - POOL_PIECES + 1)
                sp.dma_start(out_tiles[:, t, :], base[:, t, :]).then_inc(fin.stored, 16)
            ties = any_ties(sp)
            sp.wait_ge(fin.stored, 16 * len(PIECES))
            with sp.If(ties):
                sp_tied(sp)

        @block.gpsimd
        def _(pool):
            pool_attention(pool, LAYERS[0], STEPS[:EARLY_STEPS])
            pool.wait_ge(ld.small, 16 * N_SMALL)
            pool.wait_ge(init.gates, 1)
            nc.gpsimd.tensor_scalar(bout_g[:, :], bout_b[:, :], gate_t[:, 0:1], None, ALU.mult
                                    ).then_inc(init.base_bias, 1)
            pool.wait_ge(ld.x, 16)
            pool.wait_ge(init.base_bias, 1)
            nc.gpsimd.tensor_tensor(base[:, :, :], res[:, :, :], spread(bout_g[:, :], [P, NT, D], 1),
                                    ALU.add).then_inc(init.base, 1)
            for layer in LAYERS:
                pool_attention(pool, layer, STEPS[EARLY_STEPS:] if layer.n == 0 else STEPS)
                pool_route(pool, layer)
                pool_experts(pool, layer)
            for piece in PIECES[:POOL_PIECES]:
                pool.wait_ge(fin.half, piece.end)
                pool.wait_ge(fin.second, piece.end)
                add_second(nc.gpsimd.tensor_tensor, piece, fin.done)

        @block.scalar
        def _(act):
            p = prep
            act.wait_ge(ld.gates, 48)
            nc.scalar.activation(gate_t[:, :], gate_in[:, :], ACT.Tanh).then_inc(init.gates, 1)
            nc.scalar.preload_act_table_set("natural_log_exp_and_others")
            act.wait_ge(p.mv, 3)
            act.wait_ge(ld.const0, 16)
            nc.scalar.activation(ctx_rs[:, :, 0:1], ctx_mv[:, :, 1:2], ACT.Ln, bias=kc("eps")).then_inc(p.ln, 1)
            act.wait_ge(p.ln, 1)
            nc.scalar.activation(ctx_rs[:, :, 1:2], ctx_rs[:, :, 0:1], ACT.Exp, scale=-0.5).then_inc(p.rs, 1)
            act.wait_ge(p.cn_turned, 1)
            nc.scalar.activation(cn_t[:, :], ps[:, 6, 0:CTX], ACT.Identity, bias=gb[:, 3:4],
                                 scale=gb[:, 2:3]).then_inc(p.cn_t, 1)
            act.wait_ge(init.gates, 1)
            act_copy_products(act, range(0, N_PROJ, 2))
            act_attention(act, LAYERS[0], STEPS[:SCORES])
            act_copy_products(act, range(N_PROJ, N_SCORED))
            act_attention(act, LAYERS[0], STEPS[SCORES:EARLY_STEPS])
            act_copy_products(act, range(N_SCORED, N_PROD))
            copy_turned(act, nc.scalar.copy, 1, p.turned_act)
            for layer in LAYERS:
                act_attention(act, layer, STEPS[EARLY_STEPS:] if layer.n == 0 else STEPS)
                act_route(act, layer)
                act_experts(act, layer)
                if layer.n == 0:
                    for part in range(PARTS_ROUTED, PARTS_BETWEEN):
                        act_part(act, part)
            act.wait_ge(fin.coef, 1)
            for piece in PIECES:
                act.wait_ge(piece.landed, piece.count)
                for t in range(piece.first, piece.end):
                    nc.scalar.activation(y_second[:, t, :], y_second[:, t, :], ACT.Copy,
                                         scale=coef[:, 1, t:t + 1]).then_inc(fin.second, 1)
            with act.If(any_ties(act)):
                act_tied(act)

        @block.tensor
        def _(pe):
            p = prep
            pe.wait_ge(ld.const0, 16)
            pe.wait_ge(p.cn, 3)
            for k in range(3):
                rows = min(P, CTX - k * P)
                last = nc.tensor.transpose(ps[:, 6, k * P:k * P + rows], ctx_n[0:rows, k, :], ident[0:rows, 0:rows])
            last.then_inc(p.cn_turned, 1)
            pe.wait_ge(ld.wkv0, 16)
            pe.wait_ge(p.cn_t, 1)
            pe_products(pe, 0, N_SCORED)
            pe_attention(pe, LAYERS[0], STEPS[:EARLY_STEPS])
            pe_products(pe, N_SCORED, N_PROD)
            pe_turn_values(pe)
            pe.wait_ge(p.turned_act, 2 * (B // 2))
            pe.wait_ge(p.turned_dve, 2 * (B // 2))
            pe.wait_ge(ld.small, 16 * N_SMALL)
            pe.wait_ge(init.constb, 1)
            pe.wait_ge(init.drop, 1)
            for layer in LAYERS:
                pe_attention(pe, layer, STEPS[EARLY_STEPS:] if layer.n == 0 else STEPS)
                pe_route(pe, layer)
                pe_experts(pe, layer)
                if layer.n == 0:
                    pe.wait_ge(ffn[0].y, LAYERS[0].slots)
                    for part in range(PARTS_ROUTED, PARTS_BETWEEN):
                        pe_part(pe, part)
            pe_sum_ties(pe)
            with pe.If(any_ties(pe)):
                pe_tied(pe)

        @block.vector
        def _(dve):
            p = prep
            nc.vector.memset(ctx_mv[:, :, :], 1.0).then_inc(init.neg, 1)
            nc.vector.memset(exp_i[:, :], 0).then_inc(init.experts, 1)
            dve.wait_ge(init.neg, 1)
            dve.wait_ge(ld.ctx, 32)
            for k in range(3):
                rows = min(P, CTX - k * P)
                nc.vector.bn_stats(ctx_st[0:rows, k, :], ctx_sb[0:rows, k, :]).then_inc(p.stats, 1)
                dve.wait_ge(p.stats, k + 1)
                nc.vector.bn_aggr(ctx_mv[0:rows, k, :], ctx_st[0:rows, k, :]).then_inc(p.mv, 1)
            dve.wait_ge(p.rs, 1)
            for k in range(3):
                rows = min(P, CTX - k * P)
                nc.vector.tensor_scalar(ctx_n[0:rows, k, :], ctx_sb[0:rows, k, :], ctx_mv[0:rows, k, 0:1],
                                        ctx_rs[0:rows, k, 1:2], ALU.subtract, ALU.mult).then_inc(p.cn, 1)
            dve.wait_ge(init.gates, 1)
            dve_copy_projections(dve)
            dve.wait_ge(ld.x, 16)
            dve_attention(dve, LAYERS[0], STEPS[:SCORES])
            dve.wait_ge(ld.const, 16)
            wait_copied(dve, 9)
            for b in range(B):
                build_block(nc.vector.tensor_tensor, 1, b, blk.built_v)
            dve.wait_ge(ld.small, 16 * N_SMALL)
            nc.vector.tensor_copy(vlen[:, :], vlen_i[:, :]).then_inc(init.vlen, 1)
            dve.wait_ge(ld.const, 16)
            nc.vector.tensor_copy(kb_sb[:, :], k_sb[:, :]).then_inc(init.constb, 1)
            dve.wait_ge(init.vlen, 1)
            nc.vector.tensor_tensor(keep[:, :, :], spread(kc("key_number"), [P, B, NKEY], 1),
                                    spread(vlen[:, :], [P, B, NKEY], 2), ALU.is_le).then_inc(init.keep, 1)
            dve.wait_ge(init.keep, 1)
            nc.vector.tensor_scalar(drop[:, :, :], keep[:, :, :], -1.0, -NEG / LAYERS[1].scale,
                                    ALU.add, ALU.mult).then_inc(init.drop, 1)
            wait_copied(dve, 8)
            nc.vector.tensor_tensor(kv1_t[:, 0, :], kv1_t[:, 0, :], keep[:, :, :].rearrange("p b k -> p (b k)"),
                                    ALU.mult).then_inc(blk.kept, 1)
            dve_attention(dve, LAYERS[0], STEPS[SCORES:EARLY_STEPS])
            copy_turned(dve, nc.vector.tensor_copy, 0, p.turned_dve)
            for layer in LAYERS:
                dve_attention(dve, layer, STEPS[EARLY_STEPS:] if layer.n == 0 else STEPS)
                dve_route(dve, layer)
                dve_experts(dve, layer)
            dve_find_ties(dve)
            for n, piece in enumerate(PIECES):
                dve.wait_ge(piece.landed, piece.count)
                for t in range(piece.first, piece.end):
                    nc.vector.scalar_tensor_tensor(base[:, t, :], base[:, t, :], coef[:, 0, t:t + 1], res[:, t, :],
                                                   ALU.mult, ALU.add).then_inc(fin.half, 1)
                if n >= POOL_PIECES:
                    dve.wait_ge(fin.half, piece.end)
                    dve.wait_ge(fin.second, piece.end)
                    add_second(nc.vector.tensor_tensor, piece, fin.done_dve)
            with dve.If(any_ties(dve)):
                dve_tied(dve)


def constants():
    import numpy as np

    k = np.zeros((P, NCONST), np.float32)

    def put(name, values):
        a, n = CONST_COLS[name]
        values = np.asarray(values, np.float32)
        k[:values.shape[0], a:a + n] = values

    p, t, e = np.arange(P), np.arange(P) // E, np.arange(P) % E
    put("ident", np.eye(P))
    put("ones", np.ones((P, P)))
    put("before", p[:, None] < p[None, :])
    put("earlier_tile", (e[:, None] == e[None, :]) & (t[:, None] < t[None, :]))
    put("same_expert", e[:, None] == np.arange(E)[None, :])
    put("lower_expert", P * (np.arange(E)[:, None] < e[None, :]))
    put("upto_expert", np.arange(E)[:, None] <= np.arange(E)[None, :])
    put("row_number", np.tile(p, (P, 1)))
    put("slot_number", np.tile(np.arange(MAXSLOTS), (P, 1)))
    put("row_plus_1", 1 + p[:, None])
    put("tile_number", np.tile(np.arange(2 * NT), (P, 1)))
    put("expert_rank", np.tile(E - np.arange(E), (P, 1)))
    put("head_rows", p[:, None] // HD1 == np.arange(H1)[None, :])
    put("slot_edges", np.tile(P * np.arange(NT), (P, 1)))
    put("key_number", np.tile(1 + np.arange(NKEY), (P, 1)))
    put("pad_rows_plus_1", 1 + 2 * B * S + P * np.arange(MAXSLOTS)[None, :] + p[:, None])
    put("eps", np.full((P, 1), EPS))
    put("eps2", np.full((P, 1), EPS * EPS))
    return k


def kernel(**inputs):
    import numpy as np
    import concourse.bacc as bacc
    from concourse.bass_utils import run_bass_kernel_spmd

    a = {n: np.asarray(v) for n, v in inputs.items()}
    ctx = a["ctx_1024"].reshape(CTX, D)
    by_head = a["L1_xattn_Wq"].transpose(0, 2, 1).reshape(D, D)
    wqkvo1 = np.stack([by_head, a["L1_xattn_Wk"].transpose(1, 0, 2).reshape(D, D),
                       a["L1_xattn_Wv"].transpose(1, 0, 2).reshape(D, D), a["L1_xattn_Wo"]], axis=1)
    arrays = {
        "x": a["x"].reshape(B * S, D),
        "ctx_rows": ctx,
        "ctx_cols": ctx.T,
        "valid_len": a["mask_B_ik0"][None, :],
        "g_xattn": a["g_xattn"][None, :],
        "g_ffn": a["g_ffn"][None, :],
        "ln_gb": np.stack([a["L0_xattn_g1"], a["L0_xattn_b1"], a["L0_xattn_g2"], a["L0_xattn_b2"]], axis=1),
        "out_bias": a["L0_xattn_bout"][None, :],
        "wq0": a["L0_xattn_Wq"].T,
        "wkv0": a["L0_xattn_Wkv"],
        "wout0": a["L0_xattn_Wout"],
        "rw0": a["L0_ffn_router_w"],
        "rb0": a["L0_ffn_router_b"][None, :],
        "w1_0": a["L0_ffn_w1"],
        "w2_0": a["L0_ffn_w2"],
        "wqkvo1": wqkvo1,
        "w1_1": a["L1_ffn_W1"],
        "b1_1": a["L1_ffn_b1"].reshape(E, FFN // P, P).transpose(2, 0, 1),
        "w2_1": a["L1_ffn_W2"],
        "b2_1": a["L1_ffn_b2"][None, :, :],
        "rw1": a["L1_ffn_Wr"],
        "rb1": a["L1_ffn_br"][None, :],
        "const": constants(),
    }
    arrays = {n: np.ascontiguousarray(v) for n, v in arrays.items()}
    nc = bacc.Bacc("TRN2", target_bir_lowering=False, num_devices=1)
    aps = {n: nc.dram_tensor(f"in_{n}", v.shape, mybir.dt.from_np(v.dtype), kind="ExternalInput").ap()
           for n, v in arrays.items()}
    aps["out"] = nc.dram_tensor("out_dram", (B * S, D), F32, kind="ExternalOutput").ap()
    gated_stack(nc, **aps)
    r = run_bass_kernel_spmd(nc, [{f"in_{n}": v for n, v in arrays.items()}], core_ids=[0])
    return r.results[0]["out_dram"].reshape(B, S, D)
```
